# Optimizing a Trainium2 kernel written in Bass

```python
import numpy as np
import jax
import jax.numpy as jnp

def _softmax(x, axis=-1):
    return jax.nn.softmax(x, axis=axis)

def _gelu(x):
    return jax.nn.gelu(x, approximate=True)

def _silu(x):
    return jax.nn.silu(x)

def _sigmoid(x):
    return jax.nn.sigmoid(x)

def _layernorm(x, axis=-1, eps=1e-05):
    m = jnp.mean(x, axis=axis, keepdims=True)
    v = jnp.var(x, axis=axis, keepdims=True)
    return (x - m) / jnp.sqrt(v + eps)

def _scatter_add(tgt, idx, src, axis=0):
    return tgt.at[idx].add(src)

def _segment_sum(src, seg, n):
    return jax.ops.segment_sum(src, seg, n)
kernel_name = 'mk_gnn_ffn_d2_gnn_r32_44c3b0'

def setup_inputs(seed: int=0):
    np.random.seed(seed)
    _w = jnp.asarray

    def _rec_inputs():
        import jax
        import jax.numpy as jnp
        _gk = jax.random.key(seed)
        x = -0.0003713 + 1 * jax.random.normal(jax.random.fold_in(_gk, 1), (3125, 256), jnp.float32)
        _s = jax.random.randint(jax.random.fold_in(_gk, 2), (25000,), 0, 3125, jnp.int32)
        _d = jax.random.randint(jax.random.fold_in(_gk, 3), (25000,), 0, 3125, jnp.int32)
        _loop = jnp.arange(3125, dtype=jnp.int32)
        src = jnp.concatenate([_s, _d, _loop])
        dst = jnp.concatenate([_d, _s, _loop])
        _o = jnp.argsort(dst, stable=True)
        src = src[_o]
        dst = dst[_o]
        edge_attr_64 = 0.000279952 + 1.00013 * jax.random.normal(jax.random.fold_in(_gk, 12), (53125, 64), jnp.float32)
        return (x, src, dst, edge_attr_64)
    x, src, dst, edge_attr_64 = _rec_inputs()

    def _L0_gnn_setup():
        import jax, jax.numpy as jnp
        import numpy as np
        N_NODES = 50000
        N_EDGES = 10000
        HIDDEN = 256
        EDGE_DIM = 64
        NUM_HEADS = 8
        HEAD_DIM = HIDDEN // NUM_HEADS
        key = jax.random.key(seed)
        ks = jax.random.split(key, 9)
        s = HIDDEN ** (-0.5)
        return {'x': jax.random.normal(ks[0], (N_NODES, HIDDEN), dtype=jnp.float32), 'edge_index': jax.random.randint(ks[1], (2, N_EDGES), 0, N_NODES, dtype=jnp.int64), 'edge_attr': jax.random.normal(ks[2], (N_EDGES, EDGE_DIM), dtype=jnp.float32), 'Wq': jax.random.normal(ks[3], (HIDDEN, HIDDEN), dtype=jnp.float32) * s, 'Wk': jax.random.normal(ks[4], (HIDDEN, HIDDEN), dtype=jnp.float32) * s, 'Wv': jax.random.normal(ks[5], (HIDDEN, HIDDEN), dtype=jnp.float32) * s, 'We': jax.random.normal(ks[6], (EDGE_DIM, NUM_HEADS), dtype=jnp.float32) * EDGE_DIM ** (-0.5), 'Wo': jax.random.normal(ks[7], (HIDDEN, HIDDEN), dtype=jnp.float32) * s, 'bo': jnp.zeros((HIDDEN,), dtype=jnp.float32)}
    _L0_gnn_all = _L0_gnn_setup()
    _L0_gnn_in = {k: v for k, v in _L0_gnn_all.items() if k in ('Wq', 'Wk', 'Wv', 'We', 'Wo', 'bo')}
    del _L0_gnn_all

    def _L0_ffn_setup():
        import jax, jax.numpy as jnp
        import numpy as np
        C = 256
        HID = 1024
        E = 8
        TEMP = 1.0
        key = jax.random.key(seed)
        ks = jax.random.split(key, 7)
        x = jax.random.normal(ks[0], (8, 512, C), dtype=jnp.float32)
        W1 = jax.random.normal(ks[1], (C, HID), dtype=jnp.float32) * 0.02
        b1 = jnp.zeros((HID,), dtype=jnp.float32)
        Wg = jax.random.normal(ks[2], (HID, E), dtype=jnp.float32) * 0.02
        bg = jnp.zeros((E,), dtype=jnp.float32)
        Wd = jax.random.normal(ks[3], (E, HID, C), dtype=jnp.float32) * 0.02
        bd = jnp.zeros((E, C), dtype=jnp.float32)
        return {'x': x, 'W1': W1, 'b1': b1, 'Wg': Wg, 'bg': bg, 'Wd': Wd, 'bd': bd}
    _L0_ffn_all = _L0_ffn_setup()
    _L0_ffn_in = {k: v for k, v in _L0_ffn_all.items() if k in ('W1', 'b1', 'Wg', 'bg', 'Wd', 'bd')}
    del _L0_ffn_all

    def _L1_gnn_setup():
        import jax, jax.numpy as jnp
        import numpy as np
        N_NODES = 25000
        N_EDGES = 12500
        D = 256
        key = jax.random.key(seed)
        k1, k2, k3, k4, k5 = jax.random.split(key, 5)
        feat = jax.random.normal(k1, (N_NODES, D), dtype=jnp.float32)
        src = jax.random.randint(k2, (N_EDGES,), 0, N_NODES, dtype=jnp.int32)
        dst = jax.random.randint(k3, (N_EDGES,), 0, N_NODES, dtype=jnp.int32)
        a = float(np.sqrt(6.0 / (D + D)))
        W1 = jax.random.uniform(k4, (D, D), minval=-a, maxval=a, dtype=jnp.float32)
        W2 = jax.random.uniform(k5, (D, D), minval=-a, maxval=a, dtype=jnp.float32)
        b = jnp.zeros((D,), dtype=jnp.float32)
        return {'feat': feat, 'W1': W1, 'W2': W2, 'b': b, 'src': src, 'dst': dst}
    _L1_gnn_all = _L1_gnn_setup()
    _L1_gnn_in = {k: v for k, v in _L1_gnn_all.items() if k in ('W1', 'W2', 'b')}
    del _L1_gnn_all

    def _L1_ffn_setup():
        import jax, jax.numpy as jnp
        import numpy as np
        TOP_K = 2
        LN_EPS = 1e-05
        key = jax.random.key(seed)
        ks = jax.random.split(key, 8)
        B, S, D, E, H = (16, 1024, 256, 8, 1024)
        x = jax.random.normal(ks[0], (B, S, D), dtype=jnp.float32)
        Wr = jax.random.normal(ks[1], (D, E), dtype=jnp.float32) * 0.1
        br = jnp.zeros((E,), dtype=jnp.float32)
        ln_g = jnp.ones((E, D), dtype=jnp.float32)
        ln_b = jnp.zeros((E, D), dtype=jnp.float32)
        W1 = jax.random.normal(ks[2], (E, D, H), dtype=jnp.float32) * (1.0 / np.sqrt(D))
        b1 = jnp.zeros((E, H), dtype=jnp.float32)
        W2 = jax.random.normal(ks[3], (E, H, D), dtype=jnp.float32) * (1.0 / np.sqrt(H))
        b2 = jnp.zeros((E, D), dtype=jnp.float32)
        return {'x': x, 'Wr': Wr, 'br': br, 'ln_g': ln_g, 'ln_b': ln_b, 'W1': W1, 'b1': b1, 'W2': W2, 'b2': b2}
    _L1_ffn_all = _L1_ffn_setup()
    _L1_ffn_in = {k: v for k, v in _L1_ffn_all.items() if k in ('Wr', 'br', 'ln_g', 'ln_b', 'W1', 'b1', 'W2', 'b2')}
    del _L1_ffn_all
    return {'x': x, 'src': src, 'dst': dst, 'edge_attr_64': edge_attr_64, 'L0_gnn_Wq': _L0_gnn_in['Wq'], 'L0_gnn_Wk': _L0_gnn_in['Wk'], 'L0_gnn_Wv': _L0_gnn_in['Wv'], 'L0_gnn_We': _L0_gnn_in['We'], 'L0_gnn_Wo': _L0_gnn_in['Wo'], 'L0_gnn_bo': _L0_gnn_in['bo'], 'L0_ffn_W1': _L0_ffn_in['W1'], 'L0_ffn_b1': _L0_ffn_in['b1'], 'L0_ffn_Wg': _L0_ffn_in['Wg'], 'L0_ffn_bg': _L0_ffn_in['bg'], 'L0_ffn_Wd': _L0_ffn_in['Wd'], 'L0_ffn_bd': _L0_ffn_in['bd'], 'L1_gnn_W1': _L1_gnn_in['W1'], 'L1_gnn_W2': _L1_gnn_in['W2'], 'L1_gnn_b': _L1_gnn_in['b'], 'L1_ffn_Wr': _L1_ffn_in['Wr'], 'L1_ffn_br': _L1_ffn_in['br'], 'L1_ffn_ln_g': _L1_ffn_in['ln_g'], 'L1_ffn_ln_b': _L1_ffn_in['ln_b'], 'L1_ffn_W1': _L1_ffn_in['W1'], 'L1_ffn_b1': _L1_ffn_in['b1'], 'L1_ffn_W2': _L1_ffn_in['W2'], 'L1_ffn_b2': _L1_ffn_in['b2']}

def reference(x, src, dst, edge_attr_64, L0_gnn_Wq, L0_gnn_Wk, L0_gnn_Wv, L0_gnn_We, L0_gnn_Wo, L0_gnn_bo, L0_ffn_W1, L0_ffn_b1, L0_ffn_Wg, L0_ffn_bg, L0_ffn_Wd, L0_ffn_bd, L1_gnn_W1, L1_gnn_W2, L1_gnn_b, L1_ffn_Wr, L1_ffn_br, L1_ffn_ln_g, L1_ffn_ln_b, L1_ffn_W1, L1_ffn_b1, L1_ffn_W2, L1_ffn_b2):
    import jax
    import jax.numpy as jnp

    def _L0_gnn_ref(x, edge_index, edge_attr, Wq, Wk, Wv, We, Wo, bo):
        import jax, jax.numpy as jnp
        import numpy as np
        N_NODES = 50000
        N_EDGES = 10000
        HIDDEN = 256
        EDGE_DIM = 64
        NUM_HEADS = 8
        HEAD_DIM = HIDDEN // NUM_HEADS
        N = x.shape[0]
        Q = (x @ Wq).reshape(N, NUM_HEADS, HEAD_DIM)
        K = (x @ Wk).reshape(N, NUM_HEADS, HEAD_DIM)
        V = (x @ Wv).reshape(N, NUM_HEADS, HEAD_DIM)
        src, tgt = (edge_index[0], edge_index[1])
        Q_src = Q[src]
        K_tgt = K[tgt]
        V_tgt = V[tgt]
        scale = jnp.float32(HEAD_DIM ** (-0.5))
        score = (Q_src * K_tgt).sum(axis=-1) * scale + edge_attr @ We
        m = jax.ops.segment_max(score, tgt, num_segments=N)
        ex = jnp.exp(score - m[tgt])
        den = jax.ops.segment_sum(ex, tgt, num_segments=N)
        attn = ex / den[tgt]
        agg = jax.ops.segment_sum(attn[:, :, None] * V_tgt, tgt, num_segments=N)
        out = agg.reshape(N, HIDDEN) @ Wo + bo
        return out

    def _L0_ffn_ref(x, W1, b1, Wg, bg, Wd, bd):
        import jax, jax.numpy as jnp
        import numpy as np
        C = 256
        HID = 1024
        E = 8
        TEMP = 1.0
        orig_shape = x.shape
        xf = x.reshape(-1, orig_shape[-1])
        H = jax.nn.gelu(xf @ W1 + b1, approximate=False)
        probs = jax.nn.softmax((H @ Wg + bg) / TEMP, axis=-1)
        assign = jnp.argmax(probs, axis=-1)
        out = jnp.zeros_like(xf)
        for e in range(Wd.shape[0]):
            y = H @ Wd[e] + bd[e]
            sel = (assign == e)[:, None]
            out = out + jnp.where(sel, probs[:, e:e + 1] * y, 0.0)
        return out.reshape(orig_shape)

    def _L1_gnn_ref(feat, W1, W2, b, src, dst):
        import jax, jax.numpy as jnp
        import numpy as np
        N_NODES = 25000
        N_EDGES = 12500
        D = 256
        n = feat.shape[0]
        ones = jnp.ones(src.shape[0], dtype=feat.dtype)
        out_deg = jnp.maximum(jax.ops.segment_sum(ones, src, num_segments=n), 1.0)
        in_cnt = jax.ops.segment_sum(ones, dst, num_segments=n)
        t1 = feat @ W1
        msg = t1[src] + feat[src] * feat[dst] @ W2
        scale = jnp.sqrt(out_deg[src]) * jnp.sqrt(out_deg[dst])
        msg = msg / scale[:, None]
        agg = jax.ops.segment_sum(msg, dst, num_segments=n)
        embed = jnp.where(in_cnt[:, None] > 0, t1 + agg, jnp.zeros_like(t1))
        embed = embed + b
        embed = jax.nn.leaky_relu(embed, negative_slope=0.01)
        norm = jnp.linalg.norm(embed, axis=1, keepdims=True)
        embed = embed / jnp.maximum(norm, 1e-12)
        return embed

    def _L1_ffn_ref(x, Wr, br, ln_g, ln_b, W1, b1, W2, b2):
        import jax, jax.numpy as jnp
        import numpy as np
        TOP_K = 2
        LN_EPS = 1e-05
        B, S, D = x.shape
        N = B * S
        xt = x.reshape(N, D)
        logits = xt @ Wr + br
        probs = jax.nn.softmax(logits, axis=-1)
        top_p, top_idx = jax.lax.top_k(probs, TOP_K)
        weights = top_p / top_p.sum(axis=-1, keepdims=True)
        mu = xt.mean(axis=-1, keepdims=True)
        var = ((xt - mu) ** 2).mean(axis=-1, keepdims=True)
        xn = (xt - mu) * jax.lax.rsqrt(var + LN_EPS)
        xe = xn[None, :, :] * ln_g[:, None, :] + ln_b[:, None, :]
        h = jax.nn.gelu(jnp.einsum('end,edh->enh', xe, W1) + b1[:, None, :], approximate=False)
        y = jnp.einsum('enh,ehd->end', h, W2) + b2[:, None, :]
        y_tok = jnp.transpose(y, (1, 0, 2))
        sel = jnp.take_along_axis(y_tok, top_idx[:, :, None], axis=1)
        out = (weights[:, :, None] * sel).sum(axis=1)
        return out.reshape(B, S, D)
    edge_index = jnp.stack([src, dst])
    x = x + _L0_gnn_ref(_layernorm(x, axis=-1), edge_index, edge_attr_64, L0_gnn_Wq, L0_gnn_Wk, L0_gnn_Wv, L0_gnn_We, L0_gnn_Wo, L0_gnn_bo)
    x = x + _L0_ffn_ref(_layernorm(x, axis=-1)[None], L0_ffn_W1, L0_ffn_b1, L0_ffn_Wg, L0_ffn_bg, L0_ffn_Wd, L0_ffn_bd)[0]
    x = x + _L1_gnn_ref(_layernorm(x, axis=-1), L1_gnn_W1, L1_gnn_W2, L1_gnn_b, src, dst)
    x = x + _L1_ffn_ref(_layernorm(x, axis=-1)[None], L1_ffn_Wr, L1_ffn_br, L1_ffn_ln_g, L1_ffn_ln_b, L1_ffn_W1, L1_ffn_b1, L1_ffn_W2, L1_ffn_b2)[0]
    return x

_drawn_inputs = setup_inputs


def setup_inputs(seed=0):
    import zlib

    import numpy as np

    out = dict(_drawn_inputs(seed))
    spreads = {'L0_gnn_bo': (0.0, 0.1),
     'L0_ffn_b1': (0.0, 0.369),
     'L0_ffn_bg': (0.0, 0.288),
     'L0_ffn_bd': (0.0, 0.361),
     'L1_gnn_b': (0.0, 0.534),
     'L1_ffn_br': (0.0, 0.1),
     'L1_ffn_ln_g': (1.0, 0.2),
     'L1_ffn_ln_b': (0.0, 0.1),
     'L1_ffn_b1': (0.0, 0.1),
     'L1_ffn_b2': (0.0, 0.1)}
    factors = {'edge_attr_64': 8.0, 'L0_gnn_Wq': 8.0, 'L0_gnn_Wk': 8.0, 'L0_gnn_We': 8.0}
    for name, (base, spread) in spreads.items():
        noise = np.random.default_rng([zlib.crc32(name.encode()), seed]).standard_normal(out[name].shape)
        drawn = base * np.exp(spread * noise) if base else spread * noise
        out[name] = jnp.asarray(drawn.astype(out[name].dtype))
    for name, factor in factors.items():
        out[name] = (out[name] * factor).astype(out[name].dtype)
    return out
```

```python
from contextlib import ExitStack

import concourse.bass as bass
from concourse import mybir

F32 = mybir.dt.float32
BF16 = mybir.dt.bfloat16
I32 = mybir.dt.int32
ALU = mybir.AluOpType
ACT = mybir.ActivationFunctionType
AX = mybir.AxisListType

N_NODES, D = 3125, 256
N_EDGES, ED = 53125, 64
H, DH = 8, 32
X, C = 8, 1024
P = 125
T = N_NODES // P
G = 5
NG = T // G
J = N_EDGES // P
EITER = J // (G * G)
KD, KC = D // 128, C // 128
S = 128
NB0 = (N_NODES + X * (S - 1)) // S
NB1 = (2 * N_NODES + X * (S - 1)) // S
BIG = 1.5e38
MAGIC = 1.5 * 2.0 ** 23
LN_EPS = 1e-5
HALVES = ((0, 112), (112, P))


def previous_use(u, n, per):
    return u - n if u >= n else max(v for v in range(per) if v % n == u % n) - per


class Order:

    def __init__(self, sem):
        self.sem, self.n, self.base = sem, 0, 0

    def link(self, eng, ins):
        ins.then_inc(self.sem, 1)
        self.n += 1
        eng.wait_ge(self.sem, self.base + self.n)

    def turn(self, i, per):
        self.base, self.start, self.per = i * per, self.n, per

    def leave(self, turns):
        assert self.n - self.start == self.per, (self.n - self.start, self.per)
        self.base, self.n = 0, self.start + turns * self.per


def build(nc, x, src, dst, edge_attr_64, L0_gnn_Wq, L0_gnn_Wk, L0_gnn_Wv, L0_gnn_We, L0_gnn_Wo, L0_gnn_bo,
          L0_ffn_W1, L0_ffn_b1, L0_ffn_Wg, L0_ffn_bg, L0_ffn_Wd, L0_ffn_bd, L1_gnn_W1, L1_gnn_W2, L1_gnn_b,
          L1_ffn_Wr, L1_ffn_br, L1_ffn_ln_g, L1_ffn_ln_b, L1_ffn_W1, L1_ffn_b1, L1_ffn_W2, L1_ffn_b2, out):
    top = ExitStack()

    def sb(ctx, name, shape, dt=F32):
        return ctx.enter_context(nc.sbuf_tensor(name, shape, dt))

    def ps(ctx, name, shape, dt=F32):
        return ctx.enter_context(nc.psum_tensor(name, shape, dt))

    def sem(name):
        return top.enter_context(nc.semaphore(name))

    def dram(name, shape, dt=F32):
        return nc.dram_tensor(name, shape, dt, kind="Internal").ap()

    def rows_of_tiles(a):
        return a.rearrange("(t p) d -> p t d", p=P)

    with top:
        q_rows = dram("q_rows", [N_NODES, D])
        k_rows = dram("k_rows", [N_NODES, D])
        expsum_rows = dram("expsum_rows", [N_EDGES, H])
        f_rows = dram("f_rows", [N_NODES, D])
        run_rows = dram("run_rows", [N_EDGES, D])
        xg0 = dram("xg0", [(NB0 + 1) * S, D])
        yg0 = dram("yg0", [NB0 * S, D])
        xg1 = dram("xg1", [(NB1 + 1) * S, D])
        yg1 = dram("yg1", [NB1 * S, D])

        x_sb = sb(top, "x_sb", [P, T, D])
        n_sb = sb(top, "n_sb", [P, T, D])
        ident = sb(top, "ident", [128, 128])
        iota_row = sb(top, "iota_row", [P, P])
        before = sb(top, "before", [P, P])
        ones = sb(top, "ones", [128, 128])
        rank8 = sb(top, "rank8", [P, T, X])
        src_i = sb(top, "src_i", [P, J], I32)
        dst_i = sb(top, "dst_i", [P, J], I32)
        dst_f = sb(top, "dst_f", [P, J])
        same = sb(top, "same", [P, J])
        carry_on = sb(top, "carry_on", [P, T, P])
        counts = sb(top, "counts", [P, 2, T])
        has_in = sb(top, "has_in", [P, T])
        rsq_deg = sb(top, "rsq_deg", [P, T])
        end_i = sb(top, "end_i", [P, T], I32)
        logits = sb(top, "logits", [P, T, X])
        gate = sb(top, "gate", [P, 2, T])
        slot_i = sb(top, "slot_i", [P, 2, T], I32)
        block_e = sb(top, "block_e", [1, NB1 + 2], I32)
        stats = sb(top, "stats", [P, G, 6])
        mean_var = sb(top, "mean_var", [P, G, 2])
        variance = sb(top, "variance", [P, G])
        rstd = sb(top, "rstd", [P, G])
        root_t = sb(top, "root_t", [P, T])
        tile_n = sb(top, "tile_n", [P, G, D])
        exp_par = sb(top, "exp_par", [128, X, KC + 2 * KD])
        b1_0 = sb(top, "b1_0", [128, KC])

        dve_order = Order(sem("dve_order"))
        act_order = Order(sem("act_order"))
        pool_order = Order(sem("pool_order"))
        carrier = sem("carrier")

        def inverse_root(v, y, a, t):
            link = lambda ins: dve_order.link(v, ins)
            link(nc.vector.tensor_scalar(y.bitcast(I32), a.bitcast(I32), 1, None, ALU.logical_shift_right))
            link(nc.vector.tensor_scalar(y.bitcast(I32), y.bitcast(I32), -1.0, float(0x5F3759DF), ALU.mult, ALU.add))
            for _ in range(3):
                link(nc.vector.tensor_tensor(t, y, y, ALU.mult))
                link(nc.vector.scalar_tensor_tensor(t, t, -0.5, a, ALU.mult, ALU.mult))
                link(nc.vector.scalar_tensor_tensor(y, t, 1.5, y, ALU.add, ALU.mult))

        def normalise(v, src_tile, dst_tile):
            v.sem_inc(carrier, 1)
            for u in range(G):
                last = nc.vector.bn_stats(stats[:, u, :], src_tile(u))
            dve_order.link(v, last)
            v.sem_inc(carrier, 1)
            for u in range(G):
                last = nc.vector.bn_aggr(mean_var[:, u, :], stats[:, u, :])
            dve_order.link(v, last)
            dve_order.link(v, nc.vector.tensor_scalar(variance[:], mean_var[:, :, 1], LN_EPS, None, ALU.add))
            inverse_root(v, rstd[:], variance[:], root_t[:, 0:G])
            for u in range(G):
                last = nc.vector.tensor_scalar(dst_tile(u), src_tile(u), mean_var[:, u, 0:1], rstd[:, u:u + 1],
                                               ALU.subtract, ALU.mult)
            return last

        def turn_tiles(pe, psum, tiles):
            for n in range(G * KD):
                u, k = n // KD, n % KD
                last = nc.tensor.transpose(psum[:, n // 4, (n % 4) * P:(n % 4 + 1) * P],
                                           tiles[:, u, k * 128:(k + 1) * 128], ident[0:P, 0:P])
            return last

        def fetch_turned(tT, psum):
            for b in range(3):
                n = min(4, G * KD - 4 * b)
                last = nc.scalar.activation(tT[:, 4 * b:4 * b + n, :].rearrange("p n c -> p (n c)"),
                                            psum[:, b, 0:n * P], ACT.Copy)
            return last

        s_x, s_edges, s_w0, s_par, s_zero, s_fill = (sem(n) for n in ("x_loaded", "edges_loaded", "qkv_w_loaded", "par_loaded",
                                                     "zeros_made", "slots_filled"))
        s_const, s_par_turned, s_par_kept = sem("consts_made"), sem("par_turned"), sem("par_kept")
        s_n0, s_tr0, s_t0, s_qk0, s_v0 = (sem(n) for n in ("n0_ready", "tr0_done", "t0_ready", "qk0_done", "v0_done"))
        s_qk0e, s_v0e, s_qst = sem("qk0_fetched"), sem("v0_fetched"), sem("qk_stored")
        with ExitStack() as st:
            w_qkv = sb(st, "w_qkv", [128, KD, 3 * D])
            qk = sb(st, "qk", [P, T, 2 * D])
            tT = sb(st, "tT0", [128, G * KD, P])
            zeros = sb(st, "zeros", [128, 2048])
            par = sb(st, "par", [X * KC, 4, 128])
            psT = ps(st, "psT0", [128, 3, 512])
            psQ = ps(st, "psQ0", [128, 2, 512])
            psV = ps(st, "psV0", [128, 2, 512])
            psP = ps(st, "psP0", [128, 512])
            par_rows = (X * KC, X * KD, X * KD, KC)
            par_at = (0, X * KC, X * (KC + KD), X * (KC + 2 * KD))
            block = st.enter_context(nc.Block())

            @block.sync
            def _(sp):
                sp.dma_start(x_sb[:], rows_of_tiles(x)).then_inc(s_x, 16)
                for n, w in enumerate((L0_gnn_Wq, L0_gnn_Wk, L0_gnn_Wv)):
                    sp.dma_start(w_qkv[:, :, n * D:(n + 1) * D], w.rearrange("(k p) d -> p k d", p=128)).then_inc(s_w0, 16)
                sp.dma_start(src_i[:], src.rearrange("(p j) -> p j", p=P)).then_inc(s_edges, 16)
                sp.dma_start(dst_i[:], dst.rearrange("(p j) -> p j", p=P)).then_inc(s_edges, 16)
                with sp.Fori(0, NG) as i:
                    sp.wait_ge(s_qk0e, (i + 1) * G + G)
                    for n, rows in enumerate((q_rows, k_rows)):
                        sp.dma_start(rows_of_tiles(rows)[:, bass.ds(i * G, G), :],
                                     qk[:, bass.ds(i * G, G), n * D:(n + 1) * D]).then_inc(s_qst, 16)
                sp.wait_ge(s_qst, 32 * NG)
                sp.wait_ge(s_edges, 32)

            @block.gpsimd
            def _(pool):
                nc.gpsimd.memset(zeros[:], 0.0).then_inc(s_zero, 1)
                nc.gpsimd.memset(ones[:], 1.0).then_inc(s_const, 1)
                pool_order.link(pool, nc.gpsimd.memset(ident[:], 0.0))
                nc.gpsimd.affine_select(out=ident[:], in_=ident[:], compare_op=ALU.not_equal, fill=1.0, base=0,
                                        pattern=[[-1, 128]], channel_multiplier=1).then_inc(s_const, 1)
                pool_order.link(pool, nc.gpsimd.memset(before[:], 1.0))
                nc.gpsimd.affine_select(out=before[:], in_=before[:], compare_op=ALU.is_gt, fill=0.0, base=0,
                                        pattern=[[1, P]], channel_multiplier=-1).then_inc(s_const, 1)
                nc.gpsimd.iota(iota_row[:], pattern=[[1, P]], base=0, channel_multiplier=0,
                               allow_small_or_imprecise_dtypes=True).then_inc(s_const, 1)
                nc.gpsimd.iota(rank8[:], pattern=[[0, T], [-1, X]], base=X, channel_multiplier=0,
                               allow_small_or_imprecise_dtypes=True).then_inc(s_const, 1)
                nc.gpsimd.iota(carry_on[:], pattern=[[P, T], [1, P]], base=0, channel_multiplier=0,
                               allow_small_or_imprecise_dtypes=True).then_inc(s_const, 1)

            @block.scalar
            def _(act):
                for n, (a, r) in enumerate(((L1_ffn_b1, "e (c f) -> (e c) f"), (L1_ffn_ln_g, "e (c f) -> (e c) f"),
                                            (L1_ffn_ln_b, "e (c f) -> (e c) f"), (L0_ffn_b1, "(c f) -> c f"))):
                    act.dma_start(par[0:par_rows[n], n, :], a.rearrange(r, f=128)).then_inc(s_par, 16)
                act.wait_ge(s_zero, 1)
                for xg, nb in ((xg0, NB0 + 1), (xg1, NB1 + 1)):
                    flat = xg.rearrange("(p r) d -> p (r d)", p=128)
                    for at in range(0, nb * D, 2048):
                        n = min(2048, nb * D - at)
                        act.dma_start(flat[:, at:at + n], zeros[:, 0:n]).then_inc(s_fill, 16)
                act.sem_inc(s_qk0e, G)
                with act.Fori(0, NG) as i:
                    act.wait_ge(s_tr0, i + 1)
                    fetch_turned(tT, psT).then_inc(s_t0, 1)
                    for u in range(G):
                        act.wait_ge(s_qk0, i * G + u + 1)
                        act.sem_inc(carrier, 1)
                        nc.scalar.activation(qk[:, bass.ds(i * G + u, 1), 0:D].rearrange("p a d -> p (a d)"),
                                             psQ[0:P, u % 2, 0:D], ACT.Copy, scale=DH ** -0.5)
                        nc.scalar.activation(qk[:, bass.ds(i * G + u, 1), D:2 * D].rearrange("p a d -> p (a d)"),
                                             psQ[0:P, u % 2, D:2 * D], ACT.Copy).then_inc(s_qk0e, 1)
                act.wait_ge(s_fill, 16 * ((NB0 * D + D + 2047) // 2048 + (NB1 * D + D + 2047) // 2048))

            @block.tensor
            def _(pe):
                pe.wait_ge(s_const, 6)
                pe.wait_ge(s_par, 64)
                for n in range(4):
                    last = nc.tensor.transpose(psP[:, par_at[n]:par_at[n] + par_rows[n]], par[0:par_rows[n], n, :],
                                               ident[0:par_rows[n], 0:par_rows[n]])
                last.then_inc(s_par_turned, 1)
                pe.wait_ge(s_w0, 48)
                with pe.Fori(0, NG) as i:
                    pe.wait_ge(s_n0, i + 1)
                    turn_tiles(pe, psT, tile_n).then_inc(s_tr0, 1)
                    pe.wait_ge(s_t0, i + 1)
                    for u in range(G):
                        pe.wait_ge(s_qk0e, i * G + previous_use(u, 2, G) + 1 + G)
                        for k in range(KD):
                            last = nc.tensor.matmul(psQ[0:P, u % 2, :], tT[:, u * KD + k, :], w_qkv[:, k, 0:2 * D],
                                                    start=(k == 0), stop=(k == KD - 1))
                        last.then_inc(s_qk0, 1)
                        pe.wait_ge(s_v0e, i * G + previous_use(u, 2, G) + 1 + G)
                        for k in range(KD):
                            last = nc.tensor.matmul(psV[0:P, u % 2, 0:D], tT[:, u * KD + k, :], w_qkv[:, k, 2 * D:3 * D],
                                                    start=(k == 0), stop=(k == KD - 1))
                        last.then_inc(s_v0, 1)

            @block.vector
            def _(v):
                v.wait_ge(s_par_turned, 1)
                for n, (a, b) in enumerate(((0, KC), (KC, KC + KD), (KC + KD, KC + 2 * KD))):
                    nc.vector.tensor_copy(exp_par[:, :, a:b], psP[:, par_at[n]:par_at[n] + par_rows[n]]
                                          .rearrange("p (e c) -> p e c", e=X))
                nc.vector.tensor_copy(b1_0[:], psP[:, par_at[3]:par_at[3] + KC]).then_inc(s_par_kept, 1)
                v.wait_ge(s_x, 16)
                v.sem_inc(s_v0e, G)
                with v.Fori(0, NG) as i:
                    dve_order.turn(i, 14)
                    normalise(v, lambda u: x_sb[:, bass.ds(i * G + u, 1), :].rearrange("p a d -> p (a d)"),
                              lambda u: tile_n[:, u, :]).then_inc(s_n0, 1)
                    for u in range(G):
                        v.wait_ge(s_v0, i * G + u + 1)
                        v.sem_inc(carrier, 1)
                        nc.vector.tensor_copy(n_sb[:, bass.ds(i * G + u, 1), :].rearrange("p a d -> p (a d)"),
                                              psV[0:P, u % 2, 0:D]).then_inc(s_v0e, 1)
                dve_order.leave(NG)

        score = sb(top, "score", [P, H, J])
        s_webd, s_ea = sem("we_loaded"), [sem(f"ea{g}_loaded") for g in range(G)]
        s_staged, s_open = sem("indices_staged"), sem("gathers_open")
        s_got = [sem(f"rows{g}_gathered") for g in range(G)]
        s_free, s_ead, s_eae, s_es = (sem(n) for n in ("rows_free", "ea_turned", "ea_fetched", "edge_score_done"))
        s_oh, s_ohu, s_cnt, s_webz, s_cntz = (sem(n) for n in ("onehots_made", "onehots_used", "counts_done", "we_zeroed",
                                                       "zero_lhs"))
        with ExitStack() as st:
            we2 = sb(st, "we2", [2 * ED, 2 * H])
            src_s = sb(st, "src_s", [P, G, G], I32)
            dst_s = sb(st, "dst_s", [P, G, G], I32)
            qr = sb(st, "qr", [P, G, G, D])
            kr = sb(st, "kr", [P, G, G, D])
            ea = sb(st, "ea", [P, G, G * ED])
            eaT = sb(st, "eaT", [128, G, 3 * P])
            dots = sb(st, "dots", [P, G * H])
            lo = sb(st, "lo", [P, 2, J])
            hi = sb(st, "hi", [P, 2, J])
            src_f = sb(st, "src_f", [P, J])
            oh_lo = sb(st, "oh_lo", [P, G, 2, G, P], BF16)
            oh_hi = sb(st, "oh_hi", [P, G, 2, G, T], BF16)
            zb = sb(st, "zb", [P, P], BF16)
            psE = ps(st, "psE1", [128, 3, 512])
            psS = ps(st, "psS1", [128, 3, 512])
            psC = ps(st, "psC1", [128, 512])
            block = st.enter_context(nc.Block())
            eav = edge_attr_64.rearrange("(p j) f -> p (j f)", p=P)

            @block.sync
            def _(sp):
                with sp.Fori(0, EITER) as i:
                    for g in range(G):
                        sp.wait_ge(s_ead, i * G + g + 1)
                        for a, b in HALVES:
                            sp.dma_start(ea[a:b, g, :], eav[a:b, bass.ds((i * G * G + g * G) * ED, G * ED)])\
                              .then_inc(s_ea[g], 16)

            @block.gpsimd
            def _(pool):
                with pool.Fori(0, EITER) as i:
                    for g in range(G):
                        pool.wait_ge(s_staged, (i * G + g) * 2 + 2)
                        pool.sem_inc(s_open, 1)
                        for u in range(G):
                            for rows, to, at in ((q_rows, qr, src_s), (k_rows, kr, dst_s)):
                                nc.gpsimd.indirect_dma_start(
                                    out=to[:, g, u, :], out_offset=None, in_=rows,
                                    in_offset=bass.IndirectOffsetOnAxis(ap=at[:, g, u:u + 1], axis=0)).then_inc(s_got[g], 16)

            @block.scalar
            def _(act):
                act.wait_ge(s_webz, 1)
                act.dma_start(we2[0:ED, 0:H], L0_gnn_We).then_inc(s_webd, 16)
                act.dma_start(we2[ED:2 * ED, H:2 * H], L0_gnn_We).then_inc(s_webd, 16)
                act.sem_inc(s_eae, G)
                with act.Fori(0, EITER) as i:
                    for g in range(G):
                        act.wait_ge(s_free, i * G + g + 1)
                        act.sem_inc(carrier, 1)
                        at = bass.ds(i * G * G + g * G, G)
                        nc.scalar.activation(src_s[:, g, :], src_i[:, at], ACT.Copy).then_inc(s_staged, 1)
                        nc.scalar.activation(dst_s[:, g, :], dst_i[:, at], ACT.Copy).then_inc(s_staged, 1)
                        act.wait_ge(s_ead, i * G + g + 1 + G)
                        nc.scalar.activation(eaT[:, g, 0:2 * P], psE[:, g % 3, 0:2 * P], ACT.Copy)
                        nc.scalar.activation(eaT[0:ED, g, 2 * P:3 * P], psE[0:ED, g % 3, 2 * P:3 * P], ACT.Copy)\
                          .then_inc(s_eae, 1)

            @block.tensor
            def _(pe):
                pe.wait_ge(s_cntz, 1)
                pe.wait_ge(s_webd, 32)
                nc.tensor.matmul(psC[0:P, 0:2 * T], zb[:], zb[:, 0:2 * T], start=True, stop=False, skip_group_check=True)
                pe.sem_inc(s_ead, G)
                pe.sem_inc(s_ohu, G)
                with pe.Fori(0, EITER) as i:
                    for g in range(G):
                        pe.wait_ge(s_ea[g], 32 * (i + 1))
                        pe.wait_ge(s_eae, i * G + previous_use(g, 3, G) + 1 + G)
                        for n in range(3):
                            w = min(128, G * ED - n * 128)
                            last = nc.tensor.transpose(psE[0:w, g % 3, n * P:(n + 1) * P], ea[:, g, n * 128:n * 128 + w],
                                                       ident[0:P, 0:P])
                        last.then_inc(s_ead, 1)
                        pe.wait_ge(s_eae, i * G + g + 1 + G)
                        pe.wait_ge(s_free, i * G + previous_use(g, 3, G) + 1 + G)
                        for n in range(3):
                            w = min(128, G * ED - n * 128)
                            last = nc.tensor.matmul(psS[0:P, g % 3, n * 2 * H:n * 2 * H + w // ED * H],
                                                    eaT[0:w, g, n * P:(n + 1) * P], we2[0:w, 0:w // ED * H],
                                                    start=True, stop=True)
                        last.then_inc(s_es, 1)
                        pe.wait_ge(s_oh, i * G + g + 1)
                        for n in range(2):
                            for u in range(G):
                                last = nc.tensor.matmul(psC[0:P, n * T:(n + 1) * T], oh_lo[:, g, n, u, :],
                                                        oh_hi[:, g, n, u, :], start=False, stop=False, skip_group_check=True)
                        last.then_inc(s_ohu, 1)
                nc.tensor.matmul(psC[0:P, 0:2 * T], zb[:], zb[:, 0:2 * T], start=False, stop=True,
                                 skip_group_check=True).then_inc(s_cnt, 1)

            @block.vector
            def _(v):
                nc.vector.memset(we2[:], 0.0).then_inc(s_webz, 1)
                nc.vector.memset(zb[:], 0.0).then_inc(s_cntz, 1)
                nc.vector.tensor_copy(src_f[:], src_i[:])
                dve_order.link(v, nc.vector.tensor_copy(dst_f[:], dst_i[:]))
                for n, f in enumerate((src_f, dst_f)):
                    dve_order.link(v, nc.vector.tensor_scalar(lo[:, n, :], f[:], -float(P // 2), 1.0 / P, ALU.add, ALU.mult))
                    dve_order.link(v, nc.vector.tensor_scalar(hi[:, n, :], lo[:, n, :], MAGIC, None, ALU.add))
                    dve_order.link(v, nc.vector.tensor_scalar(hi[:, n, :], hi[:, n, :], MAGIC, None, ALU.subtract))
                    dve_order.link(v, nc.vector.scalar_tensor_tensor(lo[:, n, :], hi[:, n, :], -float(P), f[:],
                                                                     ALU.mult, ALU.add))
                v.sem_inc(s_free, G)
                with v.Fori(0, EITER) as i:
                    dve_order.turn(i, 2 * G)
                    for g in range(G):
                        at = bass.ds(i * G * G + g * G, G)
                        v.wait_ge(s_ohu, i * G + g + 1)
                        for n in range(2):
                            nc.vector.tensor_tensor(oh_lo[:, g, n], iota_row[:].unsqueeze(1).to_broadcast([P, G, P]),
                                                    lo[:, n, at].unsqueeze(2).to_broadcast([P, G, P]), ALU.is_equal)
                            last = nc.vector.tensor_tensor(oh_hi[:, g, n], iota_row[:, 0:T].unsqueeze(1).to_broadcast([P, G, T]),
                                                           hi[:, n, at].unsqueeze(2).to_broadcast([P, G, T]), ALU.is_equal)
                        last.then_inc(s_oh, 1)
                        v.wait_ge(s_got[g], 2 * G * 16 * (i + 1))
                        dve_order.link(v, nc.vector.tensor_tensor(qr[:, g], qr[:, g], kr[:, g], ALU.mult))
                        dve_order.link(v, nc.vector.tensor_reduce(dots[:], qr[:, g].rearrange("p u (h d) -> p (u h) d", h=H),
                                                                  AX.X, ALU.add))
                        v.wait_ge(s_es, i * G + g + 1)
                        nc.vector.tensor_tensor(score[:, :, at].rearrange("p h u -> p u h"),
                                                dots[:].rearrange("p (u h) -> p u h", h=H),
                                                psS[0:P, g % 3, 0:G * H].rearrange("p (u h) -> p u h", h=H),
                                                ALU.add).then_inc(s_free, 1)
                dve_order.leave(EITER)
                v.wait_ge(s_cnt, 1)
                dve_order.link(v, nc.vector.tensor_copy(counts[:].rearrange("p n t -> p (n t)"), psC[0:P, 0:2 * T]))

        attn = sb(top, "attn", [P, T, H])
        s_next, s_rows, s_cont = sem("next_loaded"), sem("heads_tails"), sem("carry_on_made")
        s_rowsT, s_rowsK, s_lr, s_lrT = (sem(n) for n in ("rows_turned", "rows_kept", "reach_made", "reach_turned"))
        s_pre, s_end, s_m, s_ex, s_sums, s_sumst, s_den, s_over = (sem(n) for n in (
            "prefix_done", "ends_ready", "shifted", "exp_done", "sums_ready", "sums_stored", "sums_gathered", "over_done"))
        with ExitStack() as st:
            fmax = sb(st, "fmax", [P, H, J])
            rmax = sb(st, "rmax", [P, H, J])
            sums = sb(st, "sums", [P, J, H])
            next_i = sb(st, "next_i", [P, 1], I32)
            next_f = sb(st, "next_f", [P, 1])
            key = sb(st, "key", [P, 2])
            apart = sb(st, "apart", [P, J + 1])
            first = sb(st, "first", [P, 2, J])
            cols = sb(st, "cols", [P, 4, H])
            row = sb(st, "row", [H, 4, P])
            gap = sb(st, "gap", [H, 3, P])
            ext = sb(st, "ext", [H, 4, P])
            reach = sb(st, "reach", [P, 2, H])
            tot = sb(st, "tot", [P, T])
            pre = sb(st, "pre", [P, T])
            one_row = sb(st, "one_row", [P, T])
            den = sb(st, "den", [P, T, H])
            den2 = sb(st, "den2", [P, T, H])
            end_f = sb(st, "end_f", [P, T])
            psR = ps(st, "psR2", [128, 512])
            psL = ps(st, "psL2", [128, 512])
            psN = ps(st, "psN2", [128, 512])
            psO = ps(st, "psO2", [128, 512])
            block = st.enter_context(nc.Block())
            TAIL, HEAD, FIRST, LAST = range(4)

            @block.sync
            def _(sp):
                sp.wait_ge(s_next, 1)
                sp.dma_start(next_i[0:P - 1, :], dst.rearrange("(p j) -> p j", p=P)[1:P, 0:1],
                             allow_slow_non_contiguous=True).then_inc(s_next, 16)
                sp.wait_ge(s_sums, 1)
                for a, b in HALVES:
                    sp.dma_start(expsum_rows.rearrange("(p j) h -> p (j h)", p=P)[a:b, :],
                                 sums[a:b].rearrange("p j h -> p (j h)")).then_inc(s_sumst, 16)

            @block.gpsimd
            def _(pool):
                pool.wait_ge(s_sumst, 32)
                pool.wait_ge(s_end, 1)
                for t in range(T):
                    nc.gpsimd.indirect_dma_start(out=den[:, t, :], out_offset=None, in_=expsum_rows,
                                                 in_offset=bass.IndirectOffsetOnAxis(ap=end_i[:, t:t + 1], axis=0))\
                      .then_inc(s_den, 16)

            @block.scalar
            def _(act):
                act.wait_ge(s_m, 1)
                nc.scalar.activation(fmax[:], rmax[:], ACT.Exp).then_inc(s_ex, 1)

            @block.tensor
            def _(pe):
                nc.tensor.matmul(psN[0:P, 0:T], before[:], counts[:, 1, :], start=True, stop=True)
                nc.tensor.matmul(psN[0:P, T:2 * T], ones[0:P, 0:P], counts[:, 1, :], start=True, stop=True).then_inc(s_pre, 1)
                pe.wait_ge(s_rows, 1)
                for n in range(4):
                    last = nc.tensor.transpose(psR[0:H, n * P:(n + 1) * P], cols[:, n, :], ident[0:P, 0:P])
                last.then_inc(s_rowsT, 1)
                pe.wait_ge(s_lr, 1)
                for n in range(2):
                    last = nc.tensor.transpose(psL[0:P, n * H:(n + 1) * H], ext[:, 2 + n, :], ident[0:H, 0:H])
                last.then_inc(s_lrT, 1)
                pe.wait_ge(s_sums, 1)
                pe.wait_ge(s_cont, 1)
                for t in range(T):
                    last = nc.tensor.matmul(psO[0:P, t * H:(t + 1) * H], carry_on[:, t, :], sums[:, J - 1, :],
                                            start=True, stop=True)
                last.then_inc(s_over, 1)

            @block.vector
            def _(v):
                link = lambda ins: dve_order.link(v, ins)
                nc.vector.memset(next_i[:], -1).then_inc(s_next, 1)
                v.wait_ge(s_pre, 1)
                nc.vector.memset(one_row[:], 1.0)
                nc.vector.tensor_scalar(has_in[:], counts[:, 1, :], 0.0, None, ALU.is_gt)
                link(nc.vector.tensor_scalar(pre[:], counts[:, 0, :], 1.0, None, ALU.max))
                inverse_root(v, rsq_deg[:], pre[:], root_t[:])
                link(nc.vector.tensor_copy(tot[:], psN[0:P, T:2 * T]))
                link(nc.vector.tensor_tensor_scan(pre[:], one_row[:], tot[:], 0.0, ALU.mult, ALU.add))
                link(nc.vector.tensor_tensor(pre[:], pre[:], tot[:], ALU.subtract))
                link(nc.vector.tensor_tensor(pre[:], pre[:], psN[0:P, 0:T], ALU.add))
                link(nc.vector.tensor_tensor(pre[:], pre[:], counts[:, 1, :], ALU.add))
                link(nc.vector.tensor_scalar(end_f[:], pre[:], -1.0, 0.0, ALU.add, ALU.max))
                nc.vector.tensor_copy(end_i[:], end_f[:]).then_inc(s_end, 1)
                nc.vector.memset(same[:, 0:1], 0.0)
                link(nc.vector.tensor_tensor(same[:, 1:J], dst_f[:, 1:J], dst_f[:, 0:J - 1], ALU.is_equal))
                nc.vector.memset(apart[:, J:J + 1], -BIG)
                nc.vector.tensor_scalar(apart[:, 0:J], same[:], -1.0, BIG, ALU.add, ALU.mult)
                for n, c in ((0, 0), (1, J - 1)):
                    last = nc.vector.tensor_scalar(first[:, n, :], dst_f[:], dst_f[:, c:c + 1], None, ALU.is_equal)
                link(last)
                link(nc.vector.tensor_scalar(first[:], first[:], -1.0, BIG, ALU.add, ALU.mult))
                for h in range(H):
                    last = nc.vector.tensor_tensor_scan(fmax[:, h, :], apart[:, 0:J], score[:, h, :], -BIG, ALU.add, ALU.max)
                link(last)
                for h in range(H):
                    last = nc.vector.tensor_tensor_scan(rmax[:, h, ::-1], apart[:, 1:J + 1][:, ::-1], fmax[:, h, ::-1], -BIG,
                                                        ALU.add, ALU.max)
                link(last)
                nc.vector.tensor_copy(cols[:, TAIL, :], rmax[:, :, J - 1])
                nc.vector.tensor_copy(cols[:, HEAD, :], rmax[:, :, 0])
                nc.vector.tensor_copy(cols[:, FIRST, :], dst_f[:, 0:1].to_broadcast([P, H]))
                nc.vector.tensor_copy(cols[:, LAST, :], dst_f[:, J - 1:J].to_broadcast([P, H])).then_inc(s_rows, 1)
                v.wait_ge(s_rowsT, 1)
                nc.vector.memset(gap[:], 0.0)
                link(nc.vector.tensor_copy(row[:].rearrange("h n p -> h (n p)"), psR[0:H, 0:4 * P]))
                nc.vector.tensor_tensor(gap[:, 0, 1:P], row[:, LAST, 1:P], row[:, LAST, 0:P - 1], ALU.is_equal)
                nc.vector.tensor_tensor(gap[:, 1, 0:P - 1], row[:, FIRST, 0:P - 1], row[:, FIRST, 1:P], ALU.is_equal)
                link(nc.vector.tensor_tensor(gap[:, 2, 1:P], row[:, FIRST, 1:P], row[:, LAST, 0:P - 1], ALU.is_equal))
                link(nc.vector.tensor_scalar(gap[:], gap[:], -1.0, BIG, ALU.add, ALU.mult))
                nc.vector.memset(ext[:, 2:4, :], -BIG)
                nc.vector.tensor_tensor_scan(ext[:, 0, :], gap[:, 0, :], row[:, TAIL, :], -BIG, ALU.add, ALU.max)
                link(nc.vector.tensor_tensor_scan(ext[:, 1, ::-1], gap[:, 1, ::-1], row[:, HEAD, ::-1], -BIG, ALU.add, ALU.max))
                nc.vector.tensor_tensor(ext[:, 2, 1:P], ext[:, 0, 0:P - 1], gap[:, 2, 1:P], ALU.add)
                nc.vector.tensor_tensor(ext[:, 3, 0:P - 1], ext[:, 1, 1:P], gap[:, 2, 1:P], ALU.add).then_inc(s_lr, 1)
                v.wait_ge(s_lrT, 1)
                link(nc.vector.tensor_copy(reach[:].rearrange("p n h -> p (n h)"), psL[0:P, 0:2 * H]))
                for n in range(2):
                    for h in range(H):
                        last = nc.vector.scalar_tensor_tensor(rmax[:, h, :], first[:, n, :], reach[:, n, h:h + 1], rmax[:, h, :],
                                                              ALU.add, ALU.max)
                    link(last)
                nc.vector.tensor_tensor(rmax[:], score[:], rmax[:], ALU.subtract).then_inc(s_m, 1)
                v.wait_ge(s_next, 17)
                link(nc.vector.tensor_copy(next_f[:], next_i[:]))
                link(nc.vector.tensor_tensor(key[:, 0:1], dst_f[:, J - 1:J], next_f[:], ALU.is_equal))
                link(nc.vector.tensor_scalar(key[:, 1:2], dst_f[:, J - 1:J], 1.0, None, ALU.add))
                link(nc.vector.tensor_tensor(key[:, 1:2], key[:, 1:2], key[:, 0:1], ALU.mult))
                link(nc.vector.tensor_scalar(key[:, 1:2], key[:, 1:2], -1.0, None, ALU.add))
                nc.vector.tensor_scalar(carry_on[:], carry_on[:], key[:, 1:2], None, ALU.is_equal).then_inc(s_cont, 1)
                v.wait_ge(s_ex, 1)
                for h in range(H):
                    last = nc.vector.tensor_tensor_scan(sums[:, :, h], same[:], fmax[:, h, :], 0.0, ALU.mult, ALU.add)
                last.then_inc(s_sums, 1)
                v.wait_ge(s_den, 16 * T)
                v.wait_ge(s_over, 1)
                link(nc.vector.tensor_tensor(den[:], den[:], has_in[:].unsqueeze(2).to_broadcast([P, T, H]), ALU.mult))
                link(nc.vector.tensor_tensor(den[:], den[:], psO[0:P, 0:T * H].rearrange("p (t h) -> p t h", h=H), ALU.add))
                link(nc.vector.tensor_scalar(den2[:], den[:], 1e-30, None, ALU.max))
                link(nc.vector.reciprocal(den2[:], den2[:]))
                link(nc.vector.tensor_tensor(attn[:], den[:], den2[:], ALU.mult))

        s_w3, s_agg, s_tr3, s_t3, s_o3, s_n3, s_h3, s_ge3, s_lg3, s_lg3e = (sem(n) for n in (
            "w3_loaded", "agg_ready", "tr3_done", "t3_ready", "o3_done", "n3_ready", "h3_done", "gelu3_done", "logits3_done",
            "logits3_kept"))
        HALF = (313, 312)
        with ExitStack() as st:
            wo = sb(st, "wo", [128, KD, D])
            bo = sb(st, "bo", [1, D])
            w1 = sb(st, "w1_3", [128, KD, C])
            wg = sb(st, "wg", [128, KC, X])
            bg = sb(st, "bg", [P, X])
            tT = sb(st, "tT3", [128, G * KD, P])
            nT = sb(st, "nT3", [128, KD, G * P])
            hT = sb(st, "hT3", [128, KC, G * P])
            psT = ps(st, "psT3", [128, 3, 512])
            psO = ps(st, "psO3", [128, 3 * 512])
            psH = ps(st, "psH3", [128, 2, 512])
            psG = psO[0:P, G * D:G * D + G * X]
            block = st.enter_context(nc.Block())

            @block.sync
            def _(sp):
                sp.dma_start(wo[:], L0_gnn_Wo.rearrange("(k p) d -> p k d", p=128)).then_inc(s_w3, 16)
                sp.dma_start(bo[:], L0_gnn_bo.rearrange("(a d) -> a d", a=1)).then_inc(s_w3, 16)
                sp.dma_start(w1[:], L0_ffn_W1.rearrange("(k p) d -> p k d", p=128)).then_inc(s_w3, 16)
                sp.dma_start(wg[:], L0_ffn_Wg.rearrange("(k p) d -> p k d", p=128)).then_inc(s_w3, 16)
                sp.dma_start(bg[:], L0_ffn_bg.partition_broadcast(P)).then_inc(s_w3, 16)
                sp.wait_ge(s_w3, 80)

            @block.vector
            def _(v):
                v.wait_ge(s_w3, 80)
                with v.Fori(0, NG) as i:
                    dve_order.turn(i, 17)
                    tiles = bass.ds(i * G, G)
                    nc.vector.tensor_tensor(tile_n[:].rearrange("p u (h d) -> p (u h) d", h=H),
                                            n_sb[:, tiles, :].rearrange("p u (h d) -> p (u h) d", h=H),
                                            attn[:, tiles, :].rearrange("p u h -> p (u h)").unsqueeze(2)
                                            .to_broadcast([P, G * H, DH]), ALU.mult).then_inc(s_agg, 1)
                    v.wait_ge(s_o3, i + 1)
                    dve_order.link(v, nc.vector.tensor_tensor(x_sb[:, tiles, :], x_sb[:, tiles, :],
                                                              psO[0:P, 0:G * D].rearrange("p (u d) -> p u d", d=D), ALU.add))
                    dve_order.link(v, normalise(v, lambda u: x_sb[:, bass.ds(i * G + u, 1), :].rearrange("p a d -> p (a d)"),
                                                lambda u: tile_n[:, u, :]))
                    v.sem_inc(s_n3, 1)
                    dve_order.link(v, nc.vector.tensor_tensor(n_sb[:, tiles, :], tile_n[:], tile_n[:], ALU.max))
                    v.wait_ge(s_lg3, i + 1)
                    nc.vector.tensor_tensor(logits[:, tiles, :], psG.rearrange("p (u e) -> p u e", e=X),
                                            bg[:].unsqueeze(1).to_broadcast([P, G, X]), ALU.add).then_inc(s_lg3e, 1)
                dve_order.leave(NG)

            @block.scalar
            def _(act):
                with act.Fori(0, NG) as i:
                    act.wait_ge(s_tr3, i * 2 + 1)
                    fetch_turned(tT, psT).then_inc(s_t3, 1)
                    act.wait_ge(s_tr3, i * 2 + 2)
                    for u in range(G):
                        for k in range(KD):
                            n = u * KD + k
                            last = nc.scalar.activation(nT[:, k, u * P:(u + 1) * P],
                                                        psT[:, n // 4, (n % 4) * P:(n % 4 + 1) * P], ACT.Copy)
                    last.then_inc(s_t3, 1)
                    for n in range(2 * KC):
                        m, f = n // 2, n % 2
                        act.wait_ge(s_h3, i * 2 * KC + n + 1)
                        nc.scalar.activation(hT[:, m, f * HALF[0]:f * HALF[0] + HALF[f]], psH[:, n % 2, 0:HALF[f]], ACT.Gelu,
                                             bias=b1_0[:, m:m + 1]).then_inc(s_ge3, 1)

            @block.tensor
            def _(pe):
                pe.wait_ge(s_w3, 80)
                with pe.Fori(0, NG) as i:
                    pe.wait_ge(s_agg, i + 1)
                    turn_tiles(pe, psT, tile_n).then_inc(s_tr3, 1)
                    pe.wait_ge(s_t3, i * 2 + 1)
                    for u in range(G):
                        nc.tensor.matmul(psO[0:P, u * D:(u + 1) * D], ones[0:1, 0:P], bo[:], start=True, stop=False)
                        for k in range(KD):
                            last = nc.tensor.matmul(psO[0:P, u * D:(u + 1) * D], tT[:, u * KD + k, :], wo[:, k, :],
                                                    start=False, stop=(k == KD - 1))
                    last.then_inc(s_o3, 1)
                    pe.wait_ge(s_n3, i + 1)
                    turn_tiles(pe, psT, tile_n).then_inc(s_tr3, 1)
                    pe.wait_ge(s_t3, i * 2 + 2)
                    for n in range(2 * KC):
                        m, f = n // 2, n % 2
                        if n >= 2:
                            pe.wait_ge(s_ge3, i * 2 * KC + n - 1)
                        for k in range(KD):
                            last = nc.tensor.matmul(psH[:, n % 2, 0:HALF[f]], w1[:, k, m * 128:(m + 1) * 128],
                                                    nT[:, k, f * HALF[0]:f * HALF[0] + HALF[f]],
                                                    start=(k == 0), stop=(k == KD - 1))
                        last.then_inc(s_h3, 1)
                    pe.wait_ge(s_ge3, (i + 1) * 2 * KC)
                    for u in range(G):
                        for m in range(KC):
                            last = nc.tensor.matmul(psG[:, u * X:(u + 1) * X], hT[:, m, u * P:(u + 1) * P], wg[:, m, :],
                                                    start=(m == 0), stop=(m == KC - 1))
                    last.then_inc(s_lg3, 1)
                    pe.wait_ge(s_lg3e, i + 1)

        def route(name, picks, n_blocks, xg):
            s_pick, s_cum, s_slot, s_block, s_scat = (sem(name + n) for n in (
                "_picked", "_counted", "_slots", "_blocks", "_scattered"))
            with ExitStack() as st:
                e3 = sb(st, name + "e3", [P, T, X])
                prob = sb(st, name + "prob", [P, T, X])
                work = sb(st, name + "work", [P, T, X])
                pick = sb(st, name + "pick", [P, 2, T, X])
                both = sb(st, name + "both", [P, T, X])
                col = sb(st, name + "col", [P, 4, T])
                tot = sb(st, name + "tot", [P, T, X])
                run = sb(st, name + "run", [P, T, X])
                one_row = sb(st, name + "ones", [P, T])
                step = sb(st, name + "step", [P, X, T])
                full = sb(st, name + "full", [P, X, T])
                nblk = sb(st, name + "nblk", [P, 3, X])
                slot_f = sb(st, name + "slot_f", [P, 2, T])
                b_of = sb(st, name + "b_of", [1, n_blocks + 1, X])
                be_f = sb(st, name + "be_f", [1, n_blocks + 1])
                psN = ps(st, name + "psN", [128, 512])
                block = st.enter_context(nc.Block())
                s_iota = sem(name + "_iota")

                @block.gpsimd
                def _(pool):
                    nc.gpsimd.iota(step[:], pattern=[[0, X], [S, T]], base=0, channel_multiplier=0,
                                   allow_small_or_imprecise_dtypes=True).then_inc(s_iota, 1)
                    nc.gpsimd.iota(b_of[:], pattern=[[1, n_blocks + 1], [0, X]], base=0, channel_multiplier=0,
                                   allow_small_or_imprecise_dtypes=True).then_inc(s_iota, 1)
                    pool.wait_ge(s_slot, 1)
                    for k in range(picks):
                        for t in range(T):
                            nc.gpsimd.indirect_dma_start(out=xg, out_offset=bass.IndirectOffsetOnAxis(
                                ap=slot_i[:, k, t:t + 1], axis=0), in_=n_sb[:, t, :], in_offset=None).then_inc(s_scat, 16)
                    pool.wait_ge(s_scat, 16 * picks * T)

                @block.scalar
                def _(act):
                    act.wait_ge(s_pick, 1)
                    nc.scalar.activation(prob[:], work[:], ACT.Exp).then_inc(s_pick, 1)

                @block.tensor
                def _(pe):
                    pe.wait_ge(s_pick, 3)
                    nc.tensor.matmul(psN[0:P, 0:T * X], before[:], both[:].rearrange("p t e -> p (t e)"), start=True, stop=True)
                    nc.tensor.matmul(psN[0:P, T * X:2 * T * X], ones[0:P, 0:P], both[:].rearrange("p t e -> p (t e)"),
                                     start=True, stop=True).then_inc(s_cum, 1)

                @block.vector
                def _(v):
                    link = lambda ins: dve_order.link(v, ins)
                    over_e = lambda c: col[:, c, :].unsqueeze(2).to_broadcast([P, T, X])
                    link(nc.vector.memset(one_row[:], 1.0))
                    link(nc.vector.tensor_reduce(col[:, 0, :], logits[:], AX.X, ALU.max))
                    nc.vector.tensor_tensor(work[:], logits[:], over_e(0), ALU.subtract).then_inc(s_pick, 1)
                    v.wait_ge(s_pick, 2)
                    link(nc.vector.tensor_reduce(col[:, 0, :], prob[:], AX.X, ALU.add))
                    link(nc.vector.reciprocal(col[:, 0, :], col[:, 0, :]))
                    link(nc.vector.tensor_tensor(prob[:], prob[:], over_e(0), ALU.mult))
                    for k in range(picks):
                        link(nc.vector.tensor_reduce(gate[:, k, :], prob[:], AX.X, ALU.max))
                        link(nc.vector.tensor_tensor(work[:], prob[:], gate[:, k, :].unsqueeze(2).to_broadcast([P, T, X]),
                                                     ALU.is_equal))
                        link(nc.vector.tensor_tensor(work[:], work[:], rank8[:], ALU.mult))
                        link(nc.vector.tensor_reduce(col[:, 1, :], work[:], AX.X, ALU.max))
                        link(nc.vector.tensor_tensor(pick[:, k], rank8[:], over_e(1), ALU.is_equal))
                        if k + 1 < picks:
                            link(nc.vector.scalar_tensor_tensor(prob[:], pick[:, k], -2.0, prob[:], ALU.mult, ALU.add))
                    if picks == 2:
                        nc.vector.tensor_tensor(both[:], pick[:, 0], pick[:, 1], ALU.add).then_inc(s_pick, 1)
                        link(nc.vector.tensor_tensor(col[:, 2, :], gate[:, 0, :], gate[:, 1, :], ALU.add))
                        link(nc.vector.reciprocal(col[:, 2, :], col[:, 2, :]))
                        link(nc.vector.tensor_tensor(gate[:], gate[:], col[:, 2, :].unsqueeze(1).to_broadcast([P, 2, T]), ALU.mult))
                    else:
                        nc.vector.tensor_copy(both[:], pick[:, 0]).then_inc(s_pick, 1)
                    v.wait_ge(s_cum, 1)
                    v.wait_ge(s_iota, 2)
                    link(nc.vector.tensor_copy(tot[:].rearrange("p t e -> p (t e)"), psN[0:P, T * X:2 * T * X]))
                    for e in range(X):
                        last = nc.vector.tensor_tensor_scan(run[:, :, e], one_row[:], tot[:, :, e], 0.0, ALU.mult, ALU.add)
                    link(last)
                    link(nc.vector.tensor_tensor(full[:], run[:, T - 1, :].unsqueeze(2).to_broadcast([P, X, T]), step[:], ALU.is_gt))
                    link(nc.vector.tensor_reduce(nblk[:, 0, :], full[:], AX.X, ALU.add))
                    link(nc.vector.tensor_tensor_scan(nblk[:, 1, :], one_row[:, 0:X], nblk[:, 0, :], 0.0, ALU.mult, ALU.add))
                    link(nc.vector.tensor_tensor(nblk[:, 2, :], nblk[:, 1, :], nblk[:, 0, :], ALU.subtract))
                    link(nc.vector.tensor_tensor(run[:], run[:], tot[:], ALU.subtract))
                    link(nc.vector.tensor_tensor(run[:], run[:], psN[0:P, 0:T * X].rearrange("p (t e) -> p t e", e=X), ALU.add))
                    link(nc.vector.tensor_scalar(nblk[:, 0, :], nblk[:, 2, :], float(S), None, ALU.mult))
                    link(nc.vector.tensor_tensor(run[:], run[:], nblk[:, 0, :].unsqueeze(1).to_broadcast([P, T, X]), ALU.add))
                    for k in range(picks):
                        link(nc.vector.tensor_tensor(work[:], run[:], pick[:, k], ALU.mult))
                        link(nc.vector.tensor_reduce(slot_f[:, k, :], work[:], AX.X, ALU.add))
                        last = nc.vector.tensor_copy(slot_i[:, k, :], slot_f[:, k, :])
                    last.then_inc(s_slot, 1)
                    link(nc.vector.tensor_tensor(b_of[:], b_of[:], nblk[0:1, 1, :].unsqueeze(1)
                                                 .to_broadcast([1, n_blocks + 1, X]), ALU.is_ge))
                    link(nc.vector.tensor_reduce(be_f[:], b_of[:], AX.X, ALU.add))
                    link(nc.vector.tensor_scalar(be_f[:], be_f[:], float(X - 1), None, ALU.min))
                    link(nc.vector.tensor_copy(block_e[:, 0:n_blocks + 1], be_f[:]))

        def experts(name, n_blocks, xg, yg, W1, W2, b2, own_w1):
            s_w1, s_x0 = sem(name + "_common_w1"), [sem(f"{name}_rows{n}") for n in range(2)]
            s_w = [sem(f"{name}_weights{n}") for n in range(2)]
            s_tr, s_xT, s_h, s_ge, s_y, s_ye, s_yfree, s_yst = (sem(name + n) for n in (
                "_turned", "_xT_ready", "_hidden", "_gelu", "_y_done", "_y_ready", "_y_free", "_y_stored"))
            per_w = 16 * (3 if own_w1 else 2)
            turns = n_blocks // 2
            assert n_blocks == 2 * turns
            with ExitStack() as st:
                w1 = [sb(st, f"{name}w1_{n}", [128, KD, C]) for n in range(2 if own_w1 else 1)]
                w2 = [sb(st, f"{name}w2_{n}", [128, KC, D]) for n in range(2)]
                b2r = [sb(st, f"{name}b2_{n}", [1, D]) for n in range(2)]
                xr = [sb(st, f"{name}xr_{n}", [S, D]) for n in range(2)]
                xT = [sb(st, f"{name}xT_{n}", [128, KD, S]) for n in range(2)]
                hT = [sb(st, f"{name}hT_{n}", [128, KC, S]) for n in range(2)]
                yr = [sb(st, f"{name}yr_{n}", [S, D]) for n in range(2)]
                par = [sb(st, f"{name}par_{n}", [128, KC + 2 * KD]) for n in range(2)]
                psT = ps(st, name + "psT", [128, 2, 512])
                psH = [ps(st, f"{name}psH{n}", [128, C]) for n in range(2)]
                psY = ps(st, name + "psY", [128, 2, 512])
                exp_flat = exp_par[:].rearrange("p e c -> p (e c)")
                npar = KC + 2 * KD
                block = st.enter_context(nc.Block())

                @block.sync
                def _(sp):
                    if not own_w1:
                        sp.dma_start(w1[0][:], W1.rearrange("(k p) c -> p k c", p=128)).then_inc(s_w1, 16)
                    sp.dma_start(xr[0][:], xg[0:S, :]).then_inc(s_x0[0], 16)
                    with sp.Fori(0, turns) as i:
                        for s in range(2):
                            e = sp.value_load(block_e[0:1, bass.ds(i * 2 + s, 1)], min_val=0, max_val=X - 1)
                            sp.wait_ge(s_y, i * 2 + s + 1)
                            if own_w1:
                                sp.dma_start(w1[s][:], W1[bass.ds(e, 1)].rearrange("a (k p) c -> p (a k) c", p=128))\
                                  .then_inc(s_w[s], 16)
                            sp.dma_start(w2[s][:], W2[bass.ds(e, 1)].rearrange("a (k p) c -> p (a k) c", p=128)).then_inc(s_w[s], 16)
                            sp.dma_start(b2r[s][:], b2[bass.ds(e, 1), :]).then_inc(s_w[s], 16)
                            sp.wait_ge(s_tr, i * 2 + s + 1)
                            sp.dma_start(xr[1 - s][:], xg[bass.ds((i * 2 + s + 1) * S, S), :]).then_inc(s_x0[1 - s], 16)

                @block.gpsimd
                def _(pool):
                    pool.sem_inc(s_yfree, 2)
                    with pool.Fori(0, turns) as i:
                        for s in range(2):
                            pool.wait_ge(s_ye, i * 2 + s + 1 + 2)
                            pool.sem_inc(carrier, 1)
                            pool.dma_start(yg[bass.ds((i * 2 + s) * S, S), :], yr[s][:]).then_inc(s_yst, 16)
                            pool.wait_ge(s_yst, (i * 2 + s + 1) * 16)
                            pool.sem_inc(s_yfree, 1)

                @block.scalar
                def _(act):
                    act.sem_inc(s_ge, 2)
                    with act.Fori(0, turns) as i:
                        for s in range(2):
                            for m in range(KC):
                                if m % (KC // 2) == 0:
                                    act.wait_ge(s_h, (i * 2 + s) * 2 + 1 + m // (KC // 2))
                                last = nc.scalar.activation(hT[s][:, m, :], psH[s][:, m * 128:(m + 1) * 128], ACT.Gelu,
                                                            bias=par[s][:, m:m + 1] if own_w1 else b1_0[:, m:m + 1])
                            last.then_inc(s_ge, 1)

                def turn_block(n):
                    for k in range(KD):
                        last = nc.tensor.transpose(psT[:, n, k * 128:(k + 1) * 128], xr[n][:, k * 128:(k + 1) * 128], ident[:])
                    last.then_inc(s_tr, 1)

                @block.tensor
                def _(pe):
                    pe.sem_inc(s_y, 2)
                    pe.sem_inc(s_tr, 1)
                    pe.wait_ge(s_x0[0], 16)
                    turn_block(0)
                    if not own_w1:
                        pe.wait_ge(s_w1, 16)
                    with pe.Fori(0, turns) as i:
                        for s in range(2):
                            pe.wait_ge(s_xT, i * 2 + s + 1)
                            pe.wait_ge(s_w[s], (i + 1) * per_w)
                            pe.wait_ge(s_ge, i * 2 + s + 1)
                            for m in range(KC):
                                for k in range(KD):
                                    last = nc.tensor.matmul(psH[s][:, m * 128:(m + 1) * 128],
                                                            w1[s if own_w1 else 0][:, k, m * 128:(m + 1) * 128], xT[s][:, k, :],
                                                            start=(k == 0), stop=(k == KD - 1))
                                if m % (KC // 2) == KC // 2 - 1:
                                    last.then_inc(s_h, 1)
                            pe.wait_ge(s_x0[1 - s], (i + 1 + s) * 16)
                            turn_block(1 - s)
                            pe.wait_ge(s_ge, i * 2 + s + 3)
                            pe.wait_ge(s_ye, i * 2 + s + 1)
                            nc.tensor.matmul(psY[:, s, 0:D], ones[0:1, 0:S], b2r[s][:], start=True, stop=False)
                            for m in range(KC):
                                last = nc.tensor.matmul(psY[:, s, 0:D], hT[s][:, m, :], w2[s][:, m, :],
                                                        start=False, stop=(m == KC - 1))
                            last.then_inc(s_y, 1)

                @block.vector
                def _(v):
                    def fetch_rows(n, order, turned):
                        if own_w1:
                            e = v.value_load(block_e[0:1, order], min_val=0, max_val=X - 1)
                            dve_order.link(v, nc.vector.tensor_copy(par[n][:], exp_flat[:, bass.ds(e * npar, npar)]))
                        v.wait_ge(s_tr, turned)
                        if own_w1:
                            for k in range(KD):
                                last = nc.vector.tensor_scalar(xT[n][:, k, :], psT[:, n, k * 128:(k + 1) * 128],
                                                               par[n][:, KC + k:KC + k + 1],
                                                               par[n][:, KC + KD + k:KC + KD + k + 1], ALU.mult, ALU.add)
                        else:
                            last = nc.vector.tensor_copy(xT[n][:].rearrange("p k c -> p (k c)"), psT[:, n, 0:KD * 128])
                        last.then_inc(s_xT, 1)

                    v.sem_inc(s_ye, 2)
                    fetch_rows(0, slice(0, 1), 2)
                    with v.Fori(0, turns) as i:
                        if own_w1:
                            dve_order.turn(i, 2)
                        for s in range(2):
                            fetch_rows(1 - s, bass.ds(i * 2 + s + 1, 1), i * 2 + s + 3)
                            v.wait_ge(s_y, i * 2 + s + 3)
                            v.wait_ge(s_yfree, i * 2 + s + 1)
                            nc.vector.tensor_copy(yr[s][:], psY[:, s, 0:D]).then_inc(s_ye, 1)
                    if own_w1:
                        dve_order.leave(turns)

        route("r0", 1, NB0, xg0)
        experts("m0", NB0, xg0, yg0, L0_ffn_W1, L0_ffn_Wd, L0_ffn_bd, False)

        s_y0, s_f6, s_f6st = sem("y0_gathered"), sem("f6_ready"), sem("f6_stored")
        with ExitStack() as st:
            yt = sb(st, "yt6", [P, T, D])
            block = st.enter_context(nc.Block())

            @block.gpsimd
            def _(pool):
                for t in range(T):
                    nc.gpsimd.indirect_dma_start(out=yt[:, t, :], out_offset=None, in_=yg0,
                                                 in_offset=bass.IndirectOffsetOnAxis(ap=slot_i[:, 0, t:t + 1], axis=0))\
                      .then_inc(s_y0, 16)

            @block.vector
            def _(v):
                v.wait_ge(s_y0, 16 * T)
                with v.Fori(0, NG) as i:
                    dve_order.turn(i, 16)
                    one = lambda a, u: a[:, bass.ds(i * G + u, 1), :].rearrange("p a d -> p (a d)")
                    for u in range(G):
                        last = nc.vector.scalar_tensor_tensor(one(x_sb, u), one(yt, u), gate[:, 0, bass.ds(i * G + u, 1)],
                                                              one(x_sb, u), ALU.mult, ALU.add)
                    dve_order.link(v, last)
                    dve_order.link(v, normalise(v, lambda u: one(x_sb, u), lambda u: one(n_sb, u)))
                    nc.vector.tensor_tensor(yt[:, bass.ds(i * G, G), :], n_sb[:, bass.ds(i * G, G), :],
                                            rsq_deg[:, bass.ds(i * G, G)].unsqueeze(2).to_broadcast([P, G, D]), ALU.mult)\
                      .then_inc(s_f6, 1)
                dve_order.leave(NG)

            @block.sync
            def _(sp):
                with sp.Fori(0, NG) as i:
                    sp.wait_ge(s_f6, i + 1)
                    sp.dma_start(rows_of_tiles(f_rows)[:, bass.ds(i * G, G), :], yt[:, bass.ds(i * G, G), :]).then_inc(s_f6st, 16)
                sp.wait_ge(s_f6st, 16 * NG)

        s_st7, s_open7, s_free7, s_acc, s_accst, s_accfree, s_a0 = (sem(n) for n in (
            "indices7_staged", "gathers7_open", "rows7_free", "sums7_ready", "sums7_stored", "sums7_free", "sums7_zeroed"))
        s_got7 = [sem(f"rows7_{g}_gathered") for g in range(G)]
        acc_ctx = ExitStack()
        acc = sb(acc_ctx, "acc7", [P, G, G, D])
        with ExitStack() as st:
            src_s = sb(st, "src_s7", [P, G, G], I32)
            fr = sb(st, "fr", [P, G, G, D])
            block = st.enter_context(nc.Block())

            @block.scalar
            def _(act):
                with act.Fori(0, EITER) as i:
                    for g in range(G):
                        act.wait_ge(s_free7, i * G + g + 1)
                        act.sem_inc(carrier, 1)
                        nc.scalar.activation(src_s[:, g, :], src_i[:, bass.ds(i * G * G + g * G, G)], ACT.Copy).then_inc(s_st7, 1)

            @block.gpsimd
            def _(pool):
                with pool.Fori(0, EITER) as i:
                    for g in range(G):
                        pool.wait_ge(s_st7, i * G + g + 1)
                        pool.sem_inc(s_open7, 1)
                        for u in range(G):
                            nc.gpsimd.indirect_dma_start(out=fr[:, g, u, :], out_offset=None, in_=f_rows,
                                                         in_offset=bass.IndirectOffsetOnAxis(ap=src_s[:, g, u:u + 1], axis=0))\
                              .then_inc(s_got7[g], 16)

            @block.vector
            def _(v):
                dve_order.link(v, nc.vector.memset(acc[:, G - 1, G - 1, :], 0.0))
                v.sem_inc(s_free7, G)
                v.sem_inc(s_acc, 1)
                with v.Fori(0, EITER) as i:
                    dve_order.turn(i, G * (G - 1))
                    for g in range(G):
                        v.wait_ge(s_got7[g], (i + 1) * G * 16)
                        v.wait_ge(s_accfree, i * G + g + 1)
                        if g:
                            v.wait_ge(s_acc, i * G + g)
                        else:
                            v.wait_ge(s_acc, i * G + 1)
                        for u in range(G):
                            n = g * G + u - 1
                            ins = nc.vector.scalar_tensor_tensor(acc[:, g, u, :], acc[:, n // G % G, n % G, :],
                                                                 same[:, bass.ds(i * G * G + g * G + u, 1)], fr[:, g, u, :],
                                                                 ALU.mult, ALU.add)
                            if u < G - 1:
                                dve_order.link(v, ins)
                        ins.then_inc(s_acc, 1)
                        v.wait_ge(s_acc, i * G + g + 2)
                        v.sem_inc(s_free7, 1)
                dve_order.leave(EITER)

            @block.sync
            def _(sp):
                sp.sem_inc(s_accfree, G)
                to = run_rows.rearrange("(p j) d -> p j d", p=P)
                with sp.Fori(0, EITER) as i:
                    for g in range(G):
                        sp.wait_ge(s_acc, i * G + g + 2)
                        for a, b in HALVES:
                            sp.dma_start(to[a:b, bass.ds(i * G * G + g * G, G), :], acc[a:b, g]).then_inc(s_accst, 16)
                        sp.wait_ge(s_accst, (i * G + g + 1) * 32)
                        sp.sem_inc(s_accfree, 1)

        s_w8, s_b8, s_gr, s_bd, s_g8, s_tr8, s_t8, s_e8, s_n8, s_lg8, s_lg8e, s_cs = (sem(n) for n in (
            "w8_loaded", "bias8_loaded", "sums8_gathered", "joined8", "g8_ready", "tr8_done", "t8_ready", "e8_done", "n8_ready",
            "logits8_done", "logits8_kept", "carry_staged"))
        with ExitStack() as st:
            wg1 = sb(st, "wg1", [128, KD, D])
            wg2 = sb(st, "wg2", [128, KD, D])
            wr = sb(st, "wr", [128, KD, X])
            bn = sb(st, "bn", [P, D])
            br = sb(st, "br", [P, X])
            gr = sb(st, "gr", [P, T, D])
            tile_q = sb(st, "tile_q", [P, G, D])
            emb = sb(st, "emb", [P, G, D])
            sq = sb(st, "sq", [P, G])
            inv_norm = sb(st, "inv_norm", [P, G])
            carry_stage = sb(st, "carry_stage", [P, G, P])
            tS = sb(st, "tS8", [128, G * KD, P])
            tQ = sb(st, "tQ8", [128, G * KD, P])
            psT = ps(st, "psT8", [128, 3, 512])
            psO = ps(st, "psO8", [128, 3 * 512])
            psG = ps(st, "psG8", [128, 512])
            block = st.enter_context(nc.Block())

            @block.sync
            def _(sp):
                sp.dma_start(wg1[:], L1_gnn_W1.rearrange("(k p) d -> p k d", p=128)).then_inc(s_w8, 16)
                sp.dma_start(wg2[:], L1_gnn_W2.rearrange("(k p) d -> p k d", p=128)).then_inc(s_w8, 16)
                sp.dma_start(wr[:], L1_ffn_Wr.rearrange("(k p) d -> p k d", p=128)).then_inc(s_w8, 16)
                sp.dma_start(bn[:], L1_gnn_b.partition_broadcast(P)).then_inc(s_b8, 16)
                sp.dma_start(br[:], L1_ffn_br.partition_broadcast(P)).then_inc(s_b8, 16)
                sp.wait_ge(s_w8, 48)
                sp.wait_ge(s_b8, 32)

            @block.gpsimd
            def _(pool):
                for t in range(T):
                    nc.gpsimd.indirect_dma_start(out=gr[:, t, :], out_offset=None, in_=run_rows,
                                                 in_offset=bass.IndirectOffsetOnAxis(ap=end_i[:, t:t + 1], axis=0))\
                      .then_inc(s_gr, 16)

            @block.vector
            def _(v):
                v.wait_ge(s_gr, 16 * T)
                v.wait_ge(s_b8, 32)
                with v.Fori(0, NG) as i:
                    dve_order.turn(i, 50)
                    link = lambda ins: dve_order.link(v, ins)
                    tiles = bass.ds(i * G, G)
                    one = lambda a, u: a[:, bass.ds(i * G + u, 1), :].rearrange("p a d -> p (a d)")
                    nc.vector.tensor_tensor(carry_stage[:], carry_on[:, tiles, :], carry_on[:, tiles, :], ALU.max).then_inc(s_cs, 1)
                    v.wait_ge(s_bd, i + 1)
                    for u in range(G):
                        last = nc.vector.scalar_tensor_tensor(one(gr, u), one(gr, u), has_in[:, bass.ds(i * G + u, 1)],
                                                              psO[0:P, u * D:(u + 1) * D], ALU.mult, ALU.add)
                    link(last)
                    link(nc.vector.tensor_tensor(gr[:, tiles, :], gr[:, tiles, :],
                                                 rsq_deg[:, tiles].unsqueeze(2).to_broadcast([P, G, D]), ALU.mult))
                    nc.vector.tensor_tensor(tile_n[:], n_sb[:, tiles, :], gr[:, tiles, :], ALU.add)
                    nc.vector.tensor_tensor(tile_q[:], n_sb[:, tiles, :], gr[:, tiles, :], ALU.mult).then_inc(s_g8, 1)
                    v.wait_ge(s_e8, i + 1)
                    for u in range(G):
                        last = nc.vector.scalar_tensor_tensor(emb[:, u, :], psO[0:P, u * D:(u + 1) * D],
                                                              has_in[:, bass.ds(i * G + u, 1)], bn[:], ALU.mult, ALU.add)
                    link(last)
                    link(nc.vector.scalar_tensor_tensor(emb[:], emb[:], 0.01, emb[:], ALU.mult, ALU.max))
                    link(nc.vector.tensor_tensor(tile_q[:], emb[:], emb[:], ALU.mult))
                    link(nc.vector.tensor_reduce(sq[:], tile_q[:], AX.X, ALU.add))
                    link(nc.vector.tensor_scalar(sq[:], sq[:], 1e-24, None, ALU.max))
                    inverse_root(v, inv_norm[:], sq[:], root_t[:, 0:G])
                    link(nc.vector.tensor_tensor(emb[:], emb[:], inv_norm[:].unsqueeze(2).to_broadcast([P, G, D]), ALU.mult))
                    link(nc.vector.tensor_tensor(x_sb[:, tiles, :], x_sb[:, tiles, :], emb[:], ALU.add))
                    link(normalise(v, lambda u: one(x_sb, u), lambda u: tile_n[:, u, :]))
                    v.sem_inc(s_n8, 1)
                    link(normalise(v, lambda u: tile_n[:, u, :], lambda u: one(n_sb, u)))
                    v.wait_ge(s_lg8, i + 1)
                    nc.vector.tensor_tensor(logits[:, tiles, :], psG[0:P, 0:G * X].rearrange("p (u e) -> p u e", e=X),
                                            br[:].unsqueeze(1).to_broadcast([P, G, X]), ALU.add).then_inc(s_lg8e, 1)
                dve_order.leave(NG)

            @block.scalar
            def _(act):
                with act.Fori(0, NG) as i:
                    for n, to in enumerate((tS, tQ, tS)):
                        act.wait_ge(s_tr8, i * 3 + n + 1)
                        fetch_turned(to, psT).then_inc(s_t8, 1)

            @block.tensor
            def _(pe):
                pe.wait_ge(s_w8, 48)
                with pe.Fori(0, NG) as i:
                    pe.wait_ge(s_cs, i + 1)
                    for u in range(G):
                        last = nc.tensor.matmul(psO[0:P, u * D:(u + 1) * D],
                                                carry_stage[:, u, :], acc[:, G - 1, G - 1, :], start=True, stop=True)
                    last.then_inc(s_bd, 1)
                    pe.wait_ge(s_g8, i + 1)
                    turn_tiles(pe, psT, tile_n).then_inc(s_tr8, 1)
                    pe.wait_ge(s_t8, i * 3 + 1)
                    turn_tiles(pe, psT, tile_q).then_inc(s_tr8, 1)
                    pe.wait_ge(s_t8, i * 3 + 2)
                    for u in range(G):
                        for n, (tt, w) in enumerate(((tS, wg1), (tQ, wg2))):
                            for k in range(KD):
                                last = nc.tensor.matmul(psO[0:P, u * D:(u + 1) * D], tt[:, u * KD + k, :], w[:, k, :],
                                                        start=(n == 0 and k == 0), stop=(n == 1 and k == KD - 1))
                    last.then_inc(s_e8, 1)
                    pe.wait_ge(s_n8, i + 1)
                    turn_tiles(pe, psT, tile_n).then_inc(s_tr8, 1)
                    pe.wait_ge(s_t8, i * 3 + 3)
                    for u in range(G):
                        for k in range(KD):
                            last = nc.tensor.matmul(psG[0:P, u * X:(u + 1) * X], tS[:, u * KD + k, :], wr[:, k, :],
                                                    start=(k == 0), stop=(k == KD - 1))
                    last.then_inc(s_lg8, 1)
                    pe.wait_ge(s_lg8e, i + 1)

        acc_ctx.close()
        route("r1", 2, NB1, xg1)
        experts("m1", NB1, xg1, yg1, L1_ffn_W1, L1_ffn_W2, L1_ffn_b2, True)

        s_y1, s_o11, s_out = [sem(f"y1_{n}_gathered") for n in range(2)], sem("o11_ready"), sem("out_stored")
        with ExitStack() as st:
            yt = sb(st, "yt11", [P, 2, T, D])
            block = st.enter_context(nc.Block())

            @block.gpsimd
            def _(pool):
                for k in range(2):
                    for t in range(T):
                        nc.gpsimd.indirect_dma_start(out=yt[:, k, t, :], out_offset=None, in_=yg1,
                                                     in_offset=bass.IndirectOffsetOnAxis(ap=slot_i[:, k, t:t + 1], axis=0))\
                          .then_inc(s_y1[k], 16)

            @block.vector
            def _(v):
                for k in range(2):
                    v.wait_ge(s_y1[k], 16 * T)
                    with v.Fori(0, NG) as i:
                        one = lambda a, u: a[:, bass.ds(i * G + u, 1), :].rearrange("p a d -> p (a d)")
                        for u in range(G):
                            last = nc.vector.scalar_tensor_tensor(
                                one(x_sb, u), yt[:, k, bass.ds(i * G + u, 1), :].rearrange("p a d -> p (a d)"),
                                gate[:, k, bass.ds(i * G + u, 1)], one(x_sb, u), ALU.mult, ALU.add)
                        last.then_inc(s_o11, 1)
                    v.wait_ge(s_o11, NG * (k + 1))

            @block.sync
            def _(sp):
                with sp.Fori(0, NG) as i:
                    sp.wait_ge(s_o11, NG + i + 1)
                    sp.dma_start(rows_of_tiles(out)[:, bass.ds(i * G, G), :], x_sb[:, bass.ds(i * G, G), :]).then_inc(s_out, 16)
                sp.wait_ge(s_out, 16 * NG)


_INS = ['x', 'src', 'dst', 'edge_attr_64', 'L0_gnn_Wq', 'L0_gnn_Wk', 'L0_gnn_Wv', 'L0_gnn_We', 'L0_gnn_Wo', 'L0_gnn_bo',
        'L0_ffn_W1', 'L0_ffn_b1', 'L0_ffn_Wg', 'L0_ffn_bg', 'L0_ffn_Wd', 'L0_ffn_bd', 'L1_gnn_W1', 'L1_gnn_W2', 'L1_gnn_b',
        'L1_ffn_Wr', 'L1_ffn_br', 'L1_ffn_ln_g', 'L1_ffn_ln_b', 'L1_ffn_W1', 'L1_ffn_b1', 'L1_ffn_W2', 'L1_ffn_b2']


def kernel(**inputs):
    import numpy as _np
    import concourse.bacc as _bacc
    from concourse import mybir as _mybir
    from concourse.bass_utils import run_bass_kernel_spmd as _run

    nc = _bacc.Bacc("TRN2", target_bir_lowering=False, num_devices=1)
    arrays, args = {}, []
    for name in _INS:
        a = _np.ascontiguousarray(inputs[name])
        arrays[f"in_{name}_dram"] = a
        args.append(nc.dram_tensor(f"in_{name}_dram", a.shape, _mybir.dt.from_np(a.dtype), kind="ExternalInput").ap())
    args.append(nc.dram_tensor("out_0_dram", (N_NODES, D), F32, kind="ExternalOutput").ap())
    build(nc, *args)
    r = _run(nc, [arrays], core_ids=[0])
    return r.results[0]["out_0_dram"]
```

```python
from contextlib import ExitStack

import concourse.bass as bass
from concourse import mybir

F32 = mybir.dt.float32
BF16 = mybir.dt.bfloat16
I32 = mybir.dt.int32
ALU = mybir.AluOpType
ACT = mybir.ActivationFunctionType
AX = mybir.AxisListType

N_NODES, D = 3125, 256
N_EDGES, ED = 53125, 64
H, DH = 8, 32
X, C = 8, 1024
P = 125
T = N_NODES // P
G = 5
NG = T // G
J = N_EDGES // P
EITER = J // (G * G)
NK = J // G
AHEAD = 3
R = 42
CB = -(-(R - 1 + P) // R)
KB = -(-N_NODES // R) + CB - 1
KD, KC = D // 128, C // 128
S = 128
NB0 = (N_NODES + X * (S - 1)) // S
NB1 = (2 * N_NODES + X * (S - 1)) // S
BIG = 1.5e38
MAGIC = 1.5 * 2.0 ** 23
LN_EPS = 1e-5
HALVES = ((0, 112), (112, P))


def previous_use(u, n, per):
    return u - n if u >= n else max(v for v in range(per) if v % n == u % n) - per


class Order:

    def __init__(self, sem):
        self.sem, self.n, self.base = sem, 0, 0

    def link(self, eng, ins):
        ins.then_inc(self.sem, 1)
        self.n += 1
        eng.wait_ge(self.sem, self.base + self.n)

    def turn(self, i, per):
        self.base, self.start, self.per = i * per, self.n, per

    def leave(self, turns):
        assert self.n - self.start == self.per, (self.n - self.start, self.per)
        self.base, self.n = 0, self.start + turns * self.per


def build(nc, x, src, dst, edge_attr_64, L0_gnn_Wq, L0_gnn_Wk, L0_gnn_Wv, L0_gnn_We, L0_gnn_Wo, L0_gnn_bo,
          L0_ffn_W1, L0_ffn_b1, L0_ffn_Wg, L0_ffn_bg, L0_ffn_Wd, L0_ffn_bd, L1_gnn_W1, L1_gnn_W2, L1_gnn_b,
          L1_ffn_Wr, L1_ffn_br, L1_ffn_ln_g, L1_ffn_ln_b, L1_ffn_W1, L1_ffn_b1, L1_ffn_W2, L1_ffn_b2, out):
    top = ExitStack()

    def sb(ctx, name, shape, dt=F32):
        return ctx.enter_context(nc.sbuf_tensor(name, shape, dt))

    def ps(ctx, name, shape, dt=F32):
        return ctx.enter_context(nc.psum_tensor(name, shape, dt))

    def sem(name):
        return top.enter_context(nc.semaphore(name))

    def dram(name, shape, dt=F32):
        return nc.dram_tensor(name, shape, dt, kind="Internal").ap()

    def rows_of_tiles(a):
        return a.rearrange("(t p) d -> p t d", p=P)

    with top:
        q_rows = dram("q_rows", [N_NODES, D])
        k_rows = dram("k_rows", [KB * R, 3 * D], BF16)
        ranks = dram("ranks", [N_EDGES])
        locals_ = dram("locals_", [N_EDGES + G * P], BF16)
        bases = dram("bases", [1, J], I32)
        dot_rows = dram("dot_rows", [H, N_EDGES])
        expsum_rows = dram("expsum_rows", [N_EDGES, H])
        f_rows = dram("f_rows", [N_NODES, D])
        run_rows = dram("run_rows", [N_EDGES, D])
        xg0 = dram("xg0", [NB0 * S, D])
        yg0 = dram("yg0", [NB0 * S, D])
        xg1 = dram("xg1", [NB1 * S, D])
        yg1 = dram("yg1", [NB1 * S, D])

        n_sb = sb(top, "n_sb", [P, T, D])
        ident = sb(top, "ident", [128, 128])
        iota_row = sb(top, "iota_row", [P, P])
        before = sb(top, "before", [P, P])
        ones = sb(top, "ones", [128, 128])
        rank8 = sb(top, "rank8", [P, T, X])
        src_i = sb(top, "src_i", [P, J], I32)
        dst_i = sb(top, "dst_i", [P, J], I32)
        dst_f = sb(top, "dst_f", [P, J])
        same = sb(top, "same", [P, J])
        counts = sb(top, "counts", [P, 2, T])
        node_f = sb(top, "node_f", [P, T])
        rank_p = sb(top, "rank_p", [3 * R, CB])
        has_in = sb(top, "has_in", [P, T])
        rsq_deg = sb(top, "rsq_deg", [P, T])
        end_i = sb(top, "end_i", [P, T], I32)
        src_t = sb(top, "src_t", [P, NK + AHEAD, G], I32)
        base_i = sb(top, "base_i", [1, J], I32)
        logits = sb(top, "logits", [P, T, X])
        gate_b = sb(top, "gate_b", [P, X])
        gate = sb(top, "gate", [P, 2, T])
        slot_i = sb(top, "slot_i", [P, 2, T], I32)
        block_e = sb(top, "block_e", [1, NB1], I32)
        stats = sb(top, "stats", [P, G, 6])
        mean_var = sb(top, "mean_var", [P, G, 2])
        variance = sb(top, "variance", [P, G])
        rstd = sb(top, "rstd", [P, G])
        root_t = sb(top, "root_t", [P, T])
        tile_n = sb(top, "tile_n", [P, G, D])
        exp_par = sb(top, "exp_par", [128, X, KC + 2 * KD])
        b1_0 = sb(top, "b1_0", [128, KC])

        dve_order = Order(sem("dve_order"))
        act_order = Order(sem("act_order"))
        pool_order = Order(sem("pool_order"))
        carrier = sem("carrier")

        def inverse_root(v, y, a, t):
            link = lambda ins: dve_order.link(v, ins)
            link(nc.vector.tensor_scalar(y.bitcast(I32), a.bitcast(I32), 1, None, ALU.logical_shift_right))
            link(nc.vector.tensor_scalar(y.bitcast(I32), y.bitcast(I32), -1.0, float(0x5F3759DF), ALU.mult, ALU.add))
            for _ in range(3):
                link(nc.vector.tensor_tensor(t, y, y, ALU.mult))
                link(nc.vector.scalar_tensor_tensor(t, t, -0.5, a, ALU.mult, ALU.mult))
                link(nc.vector.scalar_tensor_tensor(y, t, 1.5, y, ALU.add, ALU.mult))

        def normalise(v, src_tile, dst_tile):
            v.sem_inc(carrier, 1)
            for u in range(G):
                last = nc.vector.bn_stats(stats[:, u, :], src_tile(u))
            dve_order.link(v, last)
            v.sem_inc(carrier, 1)
            for u in range(G):
                last = nc.vector.bn_aggr(mean_var[:, u, :], stats[:, u, :])
            dve_order.link(v, last)
            dve_order.link(v, nc.vector.tensor_scalar(variance[:], mean_var[:, :, 1], LN_EPS, None, ALU.add))
            inverse_root(v, rstd[:], variance[:], root_t[:, 0:G])
            for u in range(G):
                last = nc.vector.tensor_scalar(dst_tile(u), src_tile(u), mean_var[:, u, 0:1], rstd[:, u:u + 1],
                                               ALU.subtract, ALU.mult)
            return last

        def turn_tiles(pe, psum, tiles):
            for n in range(G * KD):
                u, k = n // KD, n % KD
                last = nc.tensor.transpose(psum[:, n // 4, (n % 4) * P:(n % 4 + 1) * P],
                                           tiles[:, u, k * 128:(k + 1) * 128], ident[0:P, 0:P])
            return last

        def fetch_turned(tT, psum):
            for b in range(3):
                n = min(4, G * KD - 4 * b)
                last = nc.scalar.activation(tT[:, 4 * b:4 * b + n, :].rearrange("p n c -> p (n c)"),
                                            psum[:, b, 0:n * P], ACT.Copy)
            return last

        sems0 = []

        def sem0(name):
            sems0.append(nc.alloc_semaphore(name=name))
            return sems0[-1]

        s_dst, s_src, s_srcp, s_x0, s_xr, s_w0, s_par, s_zero, s_fill = (sem0(n) for n in (
            "dst_loaded", "src_loaded", "src_by_partition", "x0_loaded", "x_rest_loaded", "qkv_w_loaded", "par_loaded", "zeros_made", "slots_filled"))
        s_const, s_par_turned, s_par_kept = sem0("consts_made"), sem0("par_turned"), sem0("par_kept")
        s_n0, s_tr0, s_t0, s_qk0, s_v0 = (sem0(n) for n in ("n0_ready", "tr0_done", "t0_ready", "qk0_done", "v0_done"))
        s_qk0e, s_v0e, s_qst = sem0("qk0_fetched"), sem0("v0_fetched"), sem0("q_stored")
        s_run, s_runpre, s_rank, s_rankst, s_rankd, s_local, s_localst, s_base = (sem0(n) for n in (
            "runs_counted", "run_prefix_done", "ranks_made", "ranks_stored", "ranks_by_tile", "locals_made", "locals_stored",
            "bases_loaded"))
        s_srcf, s_srcT, s_oh0, s_ohu0, s_cnt0, s_deg, s_degpre, s_pos, s_kst = (sem0(n) for n in (
            "src_float", "src_turned", "dst_onehots_made", "dst_onehots_used", "in_counts_done", "in_degrees", "degree_prefix_done",
            "k_places", "k_stored"))
        s_khi, s_krem, s_kmid, s_klo, s_tail = (sem0(n) for n in ("k_hi", "k_rest", "k_mid", "k_lo", "tail_zeroed"))
        with ExitStack() as st:
            x0 = sb(st, "x0", [P, T, D])
            w_qkv = sb(st, "w_qkv", [128, KD, 3 * D])
            q_sb = sb(st, "q_sb", [P, T, D])
            k_f = sb(st, "k_f", [P, G, D])
            k_r = sb(st, "k_r", [P, G, D])
            k3 = sb(st, "k3", [P, T, 3, D], BF16)
            tT = sb(st, "tT0", [128, G * KD, P])
            zeros = sb(st, "zeros", [128, 2048])
            par = sb(st, "par", [X * KC, 4, 128])
            prev_i = sb(st, "prev_i", [P, 1], I32)
            prev_f = sb(st, "prev_f", [P, 1])
            begins = sb(st, "begins", [P, J])
            rank_e = sb(st, "rank_e", [P, J])
            run_pre = sb(st, "run_pre", [P, 1])
            rank_g = sb(st, "rank_g", [NK, G * P])
            base_f = sb(st, "base_f", [NK, G])
            base_g = sb(st, "base_g", [NK, G], I32)
            base_p = sb(st, "base_p", [NK, G])
            local_g = sb(st, "local_g", [NK, G * P], BF16)
            src_g = sb(st, "src_g", [NK, G * P], I32)
            src_gf = sb(st, "src_gf", [NK, G * P])
            lo = sb(st, "lo0", [P, J])
            hi = sb(st, "hi0", [P, J])
            OH = 4
            oh_lo = sb(st, "oh_lo0", [P, OH, G, P], BF16)
            oh_hi = sb(st, "oh_hi0", [P, OH, G, T], BF16)
            zb = sb(st, "zb0", [P, P], BF16)
            deg = sb(st, "deg", [P, 2 * T])
            tot = sb(st, "tot0", [P, 2 * T])
            pre = sb(st, "pre0", [P, 2 * T])
            one_row = sb(st, "one_row0", [P, T])
            distinct = sb(st, "distinct", [P, 1])
            idle = sb(st, "idle", [P, T])
            pos_i = sb(st, "pos_i", [P, T], I32)
            psT = ps(st, "psT0", [128, 3, 512])
            psQ = ps(st, "psQ0", [128, 2, 512])
            psV = ps(st, "psV0", [128, 512])
            psP = ps(st, "psP0", [128, 512])
            psC = ps(st, "psC0", [128, 512])
            par_rows = (X * KC, X * KD, X * KD, KC)
            par_at = (0, X * KC, X * (KC + KD), X * (KC + 2 * KD))
            block = st.enter_context(nc.Block())
            by_tile = lambda a: a[:].rearrange("k (u q) -> k u q", q=P)
            HIST = (3, 3, 3, 4, 4)
            assert sum(HIST) == EITER and len(HIST) == G

            @block.sync
            def _(sp):
                dst_p = dst.rearrange("(p j) -> p j", p=P)
                sp.dma_start(dst_i[:], dst_p).then_inc(s_dst, 16)
                sp.wait_ge(s_const, 1)
                sp.dma_start(prev_i[1:P, :], dst_p[0:P - 1, J - 1:J], allow_slow_non_contiguous=True).then_inc(s_dst, 16)
                for i in range(NG):
                    for a, b in HALVES:
                        sp.dma_start(x0[a:b, i * G:(i + 1) * G, :], rows_of_tiles(x)[a:b, i * G:(i + 1) * G, :])\
                          .then_inc(s_xr if i else s_x0, 16)
                    if i == 0:
                        sp.dma_start(src_g[:], src.rearrange("(k e) -> k e", k=NK)).then_inc(s_src, 16)
                        for n, w in enumerate((L0_gnn_Wq, L0_gnn_Wk, L0_gnn_Wv)):
                            sp.dma_start(w_qkv[:, :, n * D:(n + 1) * D], w.rearrange("(k p) d -> p k d", p=128)).then_inc(s_w0, 16)
                sp.dma_start(src_i[:], src.rearrange("(p j) -> p j", p=P)).then_inc(s_srcp, 16)
                sp.wait_ge(s_rank, 1)
                sp.dma_start(ranks.rearrange("(p j) -> p j", p=P), rank_e[:]).then_inc(s_rankst, 16)
                sp.wait_ge(s_rankst, 16)
                sp.dma_start(rank_g[:], ranks.rearrange("(k e) -> k e", k=NK)).then_inc(s_rankd, 16)
                sp.wait_ge(s_local, 2)
                sp.dma_start(locals_[0:N_EDGES].rearrange("(k e) -> k e", k=NK), local_g[:]).then_inc(s_localst, 16)
                sp.dma_start(locals_[N_EDGES:N_EDGES + G * P].rearrange("(k e) -> k e", k=1), local_g[NK - 1:NK, :])\
                  .then_inc(s_localst, 16)
                sp.dma_start(bases.rearrange("a (k u) -> (a k) u", u=G), base_g[:]).then_inc(s_localst, 16)
                sp.wait_ge(s_localst, 48)
                sp.dma_start(base_i[:], bases).then_inc(s_base, 16)
                with sp.Fori(0, NG) as i:
                    sp.wait_ge(s_qk0e, (i + 1) * G + G)
                    for a, b in HALVES:
                        sp.dma_start(rows_of_tiles(q_rows)[a:b, bass.ds(i * G, G), :],
                                     q_sb[a:b, bass.ds(i * G, G), :]).then_inc(s_qst, 16)
                sp.wait_ge(s_qst, 32 * NG)
                sp.wait_ge(s_base, 16)
                sp.wait_ge(s_srcp, 16)

            @block.gpsimd
            def _(pool):
                nc.gpsimd.memset(prev_i[:], -1).then_inc(s_const, 1)
                nc.gpsimd.memset(ones[:], 1.0).then_inc(s_const, 1)
                pool_order.link(pool, nc.gpsimd.memset(ident[:], 0.0))
                nc.gpsimd.affine_select(out=ident[:], in_=ident[:], compare_op=ALU.not_equal, fill=1.0, base=0,
                                        pattern=[[-1, 128]], channel_multiplier=1).then_inc(s_const, 1)
                pool_order.link(pool, nc.gpsimd.memset(before[:], 1.0))
                nc.gpsimd.affine_select(out=before[:], in_=before[:], compare_op=ALU.is_gt, fill=0.0, base=0,
                                        pattern=[[1, P]], channel_multiplier=-1).then_inc(s_const, 1)
                nc.gpsimd.iota(iota_row[:], pattern=[[1, P]], base=0, channel_multiplier=0,
                               allow_small_or_imprecise_dtypes=True).then_inc(s_const, 1)
                nc.gpsimd.iota(node_f[:], pattern=[[P, T]], base=0, channel_multiplier=1,
                               allow_small_or_imprecise_dtypes=True).then_inc(s_const, 1)
                nc.gpsimd.iota(rank_p[:], pattern=[[R, CB]], base=0, channel_multiplier=1,
                               allow_small_or_imprecise_dtypes=True).then_inc(s_const, 1)
                nc.gpsimd.memset(zb[:], 0.0).then_inc(s_const, 1)
                nc.gpsimd.memset(zeros[:], 0.0).then_inc(s_zero, 1)
                nc.gpsimd.iota(rank8[:], pattern=[[0, T], [-1, X]], base=X, channel_multiplier=0,
                               allow_small_or_imprecise_dtypes=True).then_inc(s_const, 1)
                pool.wait_ge(s_pos, 1)
                pool.wait_ge(s_klo, NG + 1)
                for t in range(T):
                    nc.gpsimd.indirect_dma_start(out=k_rows, out_offset=bass.IndirectOffsetOnAxis(ap=pos_i[:, t:t + 1], axis=0),
                                                 in_=k3[:, t].rearrange("p c d -> p (c d)"), in_offset=None).then_inc(s_kst, 16)
                pool.wait_ge(s_kst, 16 * T)

            @block.scalar
            def _(act):
                for n, (a, r) in enumerate(((L1_ffn_b1, "e (c f) -> (e c) f"), (L1_ffn_ln_g, "e (c f) -> (e c) f"),
                                            (L1_ffn_ln_b, "e (c f) -> (e c) f"), (L0_ffn_b1, "(c f) -> c f"))):
                    act.dma_start(par[0:par_rows[n], n, :], a.rearrange(r, f=128)).then_inc(s_par, 16)
                act.wait_ge(s_zero, 1)
                for xg, nb in ((xg0, NB0), (xg1, NB1)):
                    flat = xg.rearrange("(p r) d -> p (r d)", p=128)
                    for at in range(0, nb * D, 2048):
                        n = min(2048, nb * D - at)
                        act.dma_start(flat[:, at:at + n], zeros[:, 0:n]).then_inc(s_fill, 16)
                for a in range(N_NODES, KB * R, 128):
                    n = min(128, KB * R - a)
                    act.dma_start(k_rows[a:a + n, :], zeros[0:n, 0:3 * D // 2].bitcast(BF16)).then_inc(s_tail, 16)
                act.sem_inc(s_qk0e, G)
                act.sem_inc(s_v0e, 1)
                with act.Fori(0, NG) as i:
                    act.wait_ge(s_tr0, i + 1)
                    fetch_turned(tT, psT).then_inc(s_t0, 1)
                    act.wait_ge(s_krem, i + 1)
                    for u in range(G):
                        act.wait_ge(s_qk0, i * G + u + 1)
                        act.sem_inc(carrier, 1)
                        nc.scalar.activation(q_sb[:, bass.ds(i * G + u, 1), :].rearrange("p a d -> p (a d)"),
                                             psQ[0:P, u % 2, 0:D], ACT.Copy, scale=DH ** -0.5)
                        nc.scalar.activation(k_f[:, u, :], psQ[0:P, u % 2, D:2 * D], ACT.Copy).then_inc(s_qk0e, 1)
                    act.wait_ge(s_qk0e, (i + 1) * G + G)
                    act.sem_inc(carrier, 1)
                    nc.scalar.activation(k3[:, bass.ds(i * G, G), 0, :], k_f[:], ACT.Copy).then_inc(s_khi, 1)
                    for u in range(G):
                        act.wait_ge(s_v0, i * G + u + 1)
                        act.sem_inc(carrier, 1)
                        nc.scalar.activation(n_sb[:, bass.ds(i * G + u, 1), :].rearrange("p a d -> p (a d)"),
                                             psV[0:P, 0:D], ACT.Copy).then_inc(s_v0e, 1)
                    act.wait_ge(s_krem, i + 2)
                    act.sem_inc(carrier, 1)
                    nc.scalar.activation(k3[:, bass.ds(i * G, G), 1, :], k_r[:], ACT.Copy).then_inc(s_kmid, 1)
                act.wait_ge(s_tail, 16 * -(-(KB * R - N_NODES) // 128))
                act.wait_ge(s_fill, 16 * (-(-NB0 * D // 2048) - (-NB1 * D // 2048)))

            @block.tensor
            def _(pe):
                pe.wait_ge(s_const, 9)
                pe.wait_ge(s_run, 1)
                nc.tensor.matmul(psV[0:P, 0:1], before[:], rank_e[:, J - 1:J], start=True, stop=True).then_inc(s_runpre, 1)
                pe.wait_ge(s_par, 64)
                for n in range(4):
                    last = nc.tensor.transpose(psP[:, par_at[n]:par_at[n] + par_rows[n]], par[0:par_rows[n], n, :],
                                               ident[0:par_rows[n], 0:par_rows[n]])
                last.then_inc(s_par_turned, 1)
                pe.wait_ge(s_srcf, 1)
                pe.wait_ge(s_par_kept, 1)
                for u in range(G):
                    last = nc.tensor.transpose(psP[0:P, u * NK:(u + 1) * NK], src_gf[:, u * P:(u + 1) * P], ident[0:NK, 0:NK])
                last.then_inc(s_srcT, 1)
                nc.tensor.matmul(psC[0:P, 0:T], zb[:], zb[:, 0:T], start=True, stop=False, skip_group_check=True)
                pe.sem_inc(s_ohu0, OH)
                pe.wait_ge(s_w0, 48)
                pe.wait_ge(s_rank, 1)
                with pe.Fori(0, NG) as i:
                    pe.wait_ge(s_n0, i + 1)
                    turn_tiles(pe, psT, tile_n).then_inc(s_tr0, 1)
                    pe.wait_ge(s_t0, i + 1)
                    for u in range(G):
                        pe.wait_ge(s_qk0e, i * G + previous_use(u, 2, G) + 1 + G)
                        for k in range(KD):
                            last = nc.tensor.matmul(psQ[0:P, u % 2, :], tT[:, u * KD + k, :], w_qkv[:, k, 0:2 * D],
                                                    start=(k == 0), stop=(k == KD - 1))
                        last.then_inc(s_qk0, 1)
                    m = 0
                    for u in range(G):
                        pe.wait_ge(s_v0e, i * G + u + 1)
                        for k in range(KD):
                            last = nc.tensor.matmul(psV[0:P, 0:D], tT[:, u * KD + k, :], w_qkv[:, k, 2 * D:3 * D],
                                                    start=(k == 0), stop=(k == KD - 1))
                        last.then_inc(s_v0, 1)
                        for _ in range(HIST[u]):
                            pe.wait_ge(s_oh0, i * EITER + m + 1)
                            for c in range(G):
                                last = nc.tensor.matmul(psC[0:P, 0:T], oh_lo[:, m % OH, c, :], oh_hi[:, m % OH, c, :],
                                                        start=False, stop=False, skip_group_check=True)
                            last.then_inc(s_ohu0, 1)
                            m += 1
                nc.tensor.matmul(psC[0:P, 0:T], zb[:], zb[:, 0:T], start=False, stop=True,
                                 skip_group_check=True).then_inc(s_cnt0, 1)
                pe.wait_ge(s_deg, 1)
                nc.tensor.matmul(psP[0:P, 0:2 * T], before[:], deg[:], start=True, stop=True)
                nc.tensor.matmul(psP[0:P, 2 * T:4 * T], ones[0:P, 0:P], deg[:], start=True, stop=True).then_inc(s_degpre, 1)

            @block.vector
            def _(v):
                link = lambda ins: dve_order.link(v, ins)

                def norm_group(tiles):
                    normalise(v, lambda u: x0[:, tiles(u), :].rearrange("p a d -> p (a d)"),
                              lambda u: tile_n[:, u, :]).then_inc(s_n0, 1)

                def onehots(i):
                    for m in range(EITER):
                        if m == OH:
                            v.wait_ge(s_khi, i + 1)
                            v.wait_ge(s_klo, i + 1)
                            v.sem_inc(carrier, 1)
                            nc.vector.tensor_tensor(k_r[:], k_f[:], k3[:, bass.ds(i * G, G), 0, :], ALU.subtract)\
                              .then_inc(s_krem, 1)
                        at = bass.ds((i * EITER + m) * G, G)
                        v.wait_ge(s_ohu0, i * EITER + previous_use(m, OH, EITER) + 1 + OH)
                        v.sem_inc(carrier, 1)
                        nc.vector.tensor_tensor(oh_lo[:, m % OH], iota_row[:].unsqueeze(1).to_broadcast([P, G, P]),
                                                lo[:, at].unsqueeze(2).to_broadcast([P, G, P]), ALU.is_equal)
                        nc.vector.tensor_tensor(oh_hi[:, m % OH], iota_row[:, 0:T].unsqueeze(1).to_broadcast([P, G, T]),
                                                hi[:, at].unsqueeze(2).to_broadcast([P, G, T]), ALU.is_equal).then_inc(s_oh0, 1)
                    v.wait_ge(s_kmid, i + 1)
                    v.wait_ge(s_krem, i + 2)
                    v.sem_inc(carrier, 1)
                    nc.vector.tensor_tensor(k3[:, bass.ds(i * G, G), 2, :], k_r[:], k3[:, bass.ds(i * G, G), 1, :], ALU.subtract)\
                      .then_inc(s_klo, 1)

                v.sem_inc(s_krem, 1)
                v.sem_inc(s_klo, 1)
                v.wait_ge(s_dst, 32)
                nc.vector.memset(same[:, 0:1], 0.0)
                nc.vector.memset(one_row[:], 1.0)
                nc.vector.tensor_copy(prev_f[:], prev_i[:])
                link(nc.vector.tensor_copy(dst_f[:], dst_i[:]))
                link(nc.vector.tensor_tensor(same[:, 1:J], dst_f[:, 1:J], dst_f[:, 0:J - 1], ALU.is_equal))
                nc.vector.tensor_tensor(begins[:, 0:1], dst_f[:, 0:1], prev_f[:], ALU.not_equal)
                link(nc.vector.tensor_scalar(begins[:, 1:J], same[:, 1:J], -1.0, 1.0, ALU.mult, ALU.add))
                nc.vector.tensor_tensor_scan(rank_e[:], begins[:], begins[:], 0.0, ALU.add, ALU.max).then_inc(s_run, 1)
                link(nc.vector.tensor_scalar(lo[:], dst_f[:], -float(P // 2), 1.0 / P, ALU.add, ALU.mult))
                link(nc.vector.tensor_scalar(hi[:], lo[:], MAGIC, None, ALU.add))
                link(nc.vector.tensor_scalar(hi[:], hi[:], MAGIC, None, ALU.subtract))
                link(nc.vector.scalar_tensor_tensor(lo[:], hi[:], -float(P), dst_f[:], ALU.mult, ALU.add))
                v.wait_ge(s_runpre, 1)
                link(nc.vector.tensor_copy(run_pre[:], psV[0:P, 0:1]))
                nc.vector.tensor_scalar(rank_e[:], rank_e[:], run_pre[:, 0:1], -1.0, ALU.add, ALU.add).then_inc(s_rank, 1)
                v.wait_ge(s_par_turned, 1)
                for n, (a, b) in enumerate(((0, KC), (KC, KC + KD), (KC + KD, KC + 2 * KD))):
                    nc.vector.tensor_copy(exp_par[:, :, a:b], psP[:, par_at[n]:par_at[n] + par_rows[n]]
                                          .rearrange("p (e c) -> p e c", e=X))
                nc.vector.tensor_copy(b1_0[:], psP[:, par_at[3]:par_at[3] + KC]).then_inc(s_par_kept, 1)
                v.wait_ge(s_x0, 32)
                norm_group(lambda u: slice(u, u + 1))
                v.wait_ge(s_src, 16)
                nc.vector.tensor_copy(src_gf[:], src_g[:]).then_inc(s_srcf, 1)
                v.wait_ge(s_rankd, 16)
                link(nc.vector.tensor_scalar(base_f[:], by_tile(rank_g)[:, :, 0], -(R - 1) / 2, 1.0 / R, ALU.add, ALU.mult))
                link(nc.vector.tensor_scalar(base_f[:], base_f[:], MAGIC, None, ALU.add))
                link(nc.vector.tensor_scalar(base_f[:], base_f[:], MAGIC, None, ALU.subtract))
                nc.vector.tensor_copy(base_g[:], base_f[:]).then_inc(s_local, 1)
                link(nc.vector.tensor_scalar(base_p[:], base_f[:], float(R), None, ALU.mult))
                nc.vector.tensor_tensor(by_tile(local_g), by_tile(rank_g), base_p[:].unsqueeze(2).to_broadcast([NK, G, P]),
                                        ALU.subtract).then_inc(s_local, 1)
                v.wait_ge(s_srcT, 1)
                nc.vector.memset(src_t[:, NK:], 0)
                nc.vector.tensor_copy(src_t[:, 0:NK], psP[0:P, 0:J].rearrange("p (u k) -> p k u", u=G))
                v.wait_ge(s_xr, 32 * (NG - 1))
                v.wait_ge(s_const, 9)
                with v.Fori(0, NG - 1) as i:
                    dve_order.turn(i, 14)
                    v.wait_ge(s_tr0, i + 1)
                    norm_group(lambda u: bass.ds((i + 1) * G + u, 1))
                    onehots(i)
                dve_order.leave(NG - 1)
                onehots(NG - 1)
                v.wait_ge(s_cnt0, 1)
                link(nc.vector.tensor_copy(deg[:, 0:T], psC[0:P, 0:T]))
                nc.vector.tensor_copy(counts[:, 1, :], deg[:, 0:T])
                link(nc.vector.tensor_scalar(has_in[:], deg[:, 0:T], 0.0, None, ALU.is_gt))
                nc.vector.tensor_copy(deg[:, T:2 * T], has_in[:]).then_inc(s_deg, 1)
                v.wait_ge(s_degpre, 1)
                link(nc.vector.tensor_copy(tot[:], psP[0:P, 2 * T:4 * T]))
                for n in range(2):
                    last = nc.vector.tensor_tensor_scan(pre[:, n * T:(n + 1) * T], one_row[:], tot[:, n * T:(n + 1) * T], 0.0,
                                                        ALU.mult, ALU.add)
                link(last)
                link(nc.vector.tensor_copy(distinct[:], pre[:, 2 * T - 1:2 * T]))
                link(nc.vector.tensor_tensor(pre[:], pre[:], tot[:], ALU.subtract))
                link(nc.vector.tensor_tensor(pre[:], pre[:], psP[0:P, 0:2 * T], ALU.add))
                link(nc.vector.tensor_tensor(idle[:], node_f[:], pre[:, T:2 * T], ALU.subtract))
                link(nc.vector.tensor_scalar(idle[:], idle[:], distinct[:, 0:1], None, ALU.add))
                link(nc.vector.tensor_tensor(pre[:, T:2 * T], pre[:, T:2 * T], idle[:], ALU.subtract))
                link(nc.vector.tensor_tensor(pre[:, T:2 * T], pre[:, T:2 * T], has_in[:], ALU.mult))
                link(nc.vector.tensor_tensor(idle[:], idle[:], pre[:, T:2 * T], ALU.add))
                nc.vector.tensor_copy(pos_i[:], idle[:]).then_inc(s_pos, 1)
                link(nc.vector.tensor_tensor(pre[:, 0:T], pre[:, 0:T], deg[:, 0:T], ALU.add))
                link(nc.vector.tensor_scalar(pre[:, 0:T], pre[:, 0:T], -1.0, 0.0, ALU.add, ALU.max))
                link(nc.vector.tensor_copy(end_i[:], pre[:, 0:T]))

        score = sb(top, "score", [P, H, J])
        s_webd, s_ea = sem("we_loaded"), [sem(f"ea{g}_loaded") for g in range(G)]
        s_staged, s_open = sem("indices_staged"), sem("gathers_open")
        s_got = [sem(f"rows{g}_gathered") for g in range(G)]
        s_loc = [sem(f"locals{g}_loaded") for g in range(G)]
        s_kp = sem("k_parts_loaded")
        s_free, s_ead, s_eae, s_es, s_esk = (sem(n) for n in ("rows_free", "ea_turned", "ea_fetched", "edge_score_done",
                                                       "edge_score_kept"))
        s_oh, s_ohu, s_cnt, s_webz, s_cntz = (sem(n) for n in ("onehots_made", "onehots_used", "counts_done", "we_zeroed",
                                                       "zero_lhs"))
        s_kt, s_kx, s_kfree, s_dT, s_dk, s_dst1 = (sem(n) for n in (
            "k_onehots", "k_expanded", "k_banks_free", "dots_turned", "dots_kept", "dots_stored"))
        with ExitStack() as st:
            we2 = sb(st, "we2", [2 * ED, 2 * H])
            src_s = sb(st, "src_s", [P, G, G], I32)
            qr = sb(st, "qr", [P, G, G, D])
            kp = sb(st, "kp", [3 * R, KB, D], BF16)
            loc = sb(st, "loc", [3 * R, G, G * P], BF16)
            k_at = sb(st, "k_at", [3 * R, CB])
            part_of = sb(st, "part_of", [3 * R, 2])
            oh_k = sb(st, "oh_k", [3 * R, 3, CB, G * P], BF16)
            ea = sb(st, "ea", [P, G, G * ED])
            eaT = sb(st, "eaT", [128, G, 3 * P])
            dots = sb(st, "dots", [P, H, J])
            lo = sb(st, "lo", [P, J])
            hi = sb(st, "hi", [P, J])
            src_f = sb(st, "src_f", [P, J])
            oh_lo = sb(st, "oh_lo", [P, G, G, P], BF16)
            oh_hi = sb(st, "oh_hi", [P, G, G, T], BF16)
            zb = sb(st, "zb", [P, P], BF16)
            psE = ps(st, "psE1", [128, 2, 512])
            psS = ps(st, "psS1", [128, 2, 512])
            psC = ps(st, "psC1", [128, 512])
            psK = ps(st, "psK1", [128, 3, 512])
            block = st.enter_context(nc.Block())
            eav = edge_attr_64.rearrange("(p j) f -> p (j f)", p=P)
            K_SLOT = (0, 1, 0, 1, 2)
            BANKS = ((0, 2), (2, 4), (4, G))
            CH = 112
            CHUNKS = [(a, min(a + CH, J)) for a in range(0, J, CH)]
            turned = qr[:].rearrange("p g u d -> p (g u d)")[:, 0:H * len(CHUNKS) * P]\
                          .rearrange("p (h c q) -> p h c q", h=H, c=len(CHUNKS))

            @block.sync
            def _(sp):
                sp.dma_start(loc[:, 0, :], locals_[0:G * P].partition_broadcast(3 * R)).then_inc(s_loc[0], 16)
                for c in range(3):
                    sp.dma_start(kp[c * R:(c + 1) * R], k_rows[:, c * D:(c + 1) * D].rearrange("(b r) d -> r b d", r=R))\
                      .then_inc(s_kp, 16)
                with sp.Fori(0, EITER) as i:
                    for g in range(G):
                        sp.wait_ge(s_ead, i * G + g + 1)
                        for a, b in HALVES:
                            sp.dma_start(ea[a:b, g, :], eav[a:b, bass.ds((i * G * G + g * G) * ED, G * ED)])\
                              .then_inc(s_ea[g], 16)
                        sp.wait_ge(s_kt, i * G + g + 2)
                        sp.dma_start(loc[:, (g + 1) % G, :], locals_[bass.ds((i * G + g + 1) * G * P, G * P)]
                                     .partition_broadcast(3 * R)).then_inc(s_loc[(g + 1) % G], 16)
                for part in range(2):
                    heads = slice(part * H // 2, (part + 1) * H // 2)
                    sp.wait_ge(s_dk, (part + 1) * H // 2)
                    for c, (a, b) in enumerate(CHUNKS):
                        sp.dma_start(dot_rows[heads, a * P:b * P].rearrange("h (t q) -> t h q", q=P),
                                     turned[0:b - a, heads, c, :]).then_inc(s_dst1, 16)
                sp.wait_ge(s_dst1, 2 * 16 * len(CHUNKS))

            @block.gpsimd
            def _(pool):
                with pool.Fori(0, EITER) as i:
                    for g in range(G):
                        pool.wait_ge(s_staged, i * G + g + 1)
                        pool.sem_inc(s_open, 1)
                        for u in range(G):
                            nc.gpsimd.indirect_dma_start(
                                out=qr[:, g, u, :], out_offset=None, in_=q_rows,
                                in_offset=bass.IndirectOffsetOnAxis(ap=src_s[:, g, u:u + 1], axis=0)).then_inc(s_got[g], 16)
                for s in sems0:
                    pool.sem_clear(s)

            @block.scalar
            def _(act):
                act.wait_ge(s_webz, 1)
                act.dma_start(we2[0:ED, 0:H], L0_gnn_We).then_inc(s_webd, 16)
                act.dma_start(we2[ED:2 * ED, H:2 * H], L0_gnn_We).then_inc(s_webd, 16)
                act.sem_inc(s_eae, G)
                act.sem_inc(s_esk, G)

                def stage(at, g):
                    nc.scalar.activation(src_s[:, g, :], src_t[:, at, :].rearrange("p a u -> p (a u)"), ACT.Copy)\
                      .then_inc(s_staged, 1)

                act.wait_ge(s_free, G)
                for k in range(AHEAD):
                    stage(slice(k, k + 1), k)
                with act.Fori(0, EITER) as i:
                    for g in range(G):
                        act.wait_ge(s_free, i * G + g + AHEAD + 1)
                        act.sem_inc(carrier, 1)
                        stage(bass.ds(i * G + g + AHEAD, 1), (g + AHEAD) % G)
                        act.wait_ge(s_ead, i * G + g + 1 + G)
                        nc.scalar.activation(eaT[:, g, 0:2 * P], psE[:, g % 2, 0:2 * P], ACT.Copy)
                        nc.scalar.activation(eaT[0:ED, g, 2 * P:3 * P], psE[0:ED, g % 2, 2 * P:3 * P], ACT.Copy)\
                          .then_inc(s_eae, 1)
                        act.wait_ge(s_es, i * G + g + 1)
                        act.sem_inc(carrier, 1)
                        nc.scalar.activation(score[:, :, bass.ds(i * G * G + g * G, G)].rearrange("p h u -> p u h"),
                                             psS[0:P, g % 2, 0:G * H].rearrange("p (u h) -> p u h", h=H), ACT.Copy)\
                          .then_inc(s_esk, 1)
                for h in range(H):
                    act.wait_ge(s_dT, h + 1)
                    for c, (a, b) in enumerate(CHUNKS):
                        if b - a < CH:
                            nc.scalar.activation(turned[0:CH, h, 0:c, :].rearrange("t c q -> t (c q)"),
                                                 psK[0:CH, h % 3, 0:c * P], ACT.Copy)
                            last = nc.scalar.activation(turned[0:b - a, h, c, :], psK[0:b - a, h % 3, c * P:(c + 1) * P], ACT.Copy)
                    last.then_inc(s_dk, 1)

            @block.tensor
            def _(pe):
                pe.wait_ge(s_cntz, 1)
                pe.wait_ge(s_webd, 32)
                nc.tensor.matmul(psC[0:P, 0:T], zb[:], zb[:, 0:T], start=True, stop=False, skip_group_check=True)
                pe.sem_inc(s_ead, G)
                pe.sem_inc(s_ohu, G)
                pe.wait_ge(s_kp, 48)
                with pe.Fori(0, EITER) as i:
                    for g in range(G):
                        _, first = nc.values_load_multi_w_load_instructions(
                            base_i[0:1, bass.ds(i * G * G + g * G, G)], engines=[mybir.EngineType.PE], min_val=0, max_val=KB - CB)
                        pe.wait_ge(s_ea[g], 32 * (i + 1))
                        pe.wait_ge(s_eae, i * G + previous_use(g, 2, G) + 1 + G)
                        for n in range(3):
                            w = min(128, G * ED - n * 128)
                            last = nc.tensor.transpose(psE[0:w, g % 2, n * P:(n + 1) * P], ea[:, g, n * 128:n * 128 + w],
                                                       ident[0:P, 0:P])
                        last.then_inc(s_ead, 1)
                        pe.wait_ge(s_kt, i * G + g + 1 + G)
                        for m, (a, b) in enumerate(BANKS):
                            pe.wait_ge(s_kfree, (i * G + g) * 3 + m + 1)
                            for u in range(a, b):
                                for c in range(CB):
                                    last = nc.tensor.matmul(psK[0:P, m, (u - a) * D:(u - a + 1) * D],
                                                            oh_k[:, K_SLOT[g], c, u * P:(u + 1) * P],
                                                            kp[:, bass.ds(first[u] + c, 1), :].rearrange("p a d -> p (a d)"),
                                                            start=(c == 0), stop=(c == CB - 1))
                            last.then_inc(s_kx, 1)
                        pe.wait_ge(s_eae, i * G + g + 1 + G)
                        pe.wait_ge(s_esk, i * G + previous_use(g, 2, G) + 1 + G)
                        for n in range(3):
                            w = min(128, G * ED - n * 128)
                            last = nc.tensor.matmul(psS[0:P, g % 2, n * 2 * H:n * 2 * H + w // ED * H],
                                                    eaT[0:w, g, n * P:(n + 1) * P], we2[0:w, 0:w // ED * H],
                                                    start=True, stop=True)
                        last.then_inc(s_es, 1)
                        pe.wait_ge(s_oh, i * G + g + 1)
                        for u in range(G):
                            last = nc.tensor.matmul(psC[0:P, 0:T], oh_lo[:, g, u, :], oh_hi[:, g, u, :], start=False, stop=False,
                                                    skip_group_check=True)
                        last.then_inc(s_ohu, 1)
                nc.tensor.matmul(psC[0:P, 0:T], zb[:], zb[:, 0:T], start=False, stop=True,
                                 skip_group_check=True).then_inc(s_cnt, 1)
                pe.wait_ge(s_free, G + NK)
                for h in range(H):
                    if h >= 3:
                        pe.wait_ge(s_dk, h - 2)
                    for c, (a, b) in enumerate(CHUNKS):
                        last = nc.tensor.transpose(psK[0:b - a, h % 3, c * P:(c + 1) * P], dots[:, h, a:b], ident[0:P, 0:P])
                    last.then_inc(s_dT, 1)

            @block.vector
            def _(v):
                def k_onehots(slot, k_slot, turn):
                    v.wait_ge(s_loc[slot], 16 * (turn + 1))
                    for c in range(CB):
                        last = nc.vector.tensor_scalar(oh_k[:, k_slot, c, :], loc[:, slot, :], k_at[:, c:c + 1], None, ALU.is_equal)
                    last.then_inc(s_kt, 1)

                nc.vector.memset(we2[:], 0.0).then_inc(s_webz, 1)
                nc.vector.memset(zb[:], 0.0).then_inc(s_cntz, 1)
                for n in range(2):
                    last = nc.vector.tensor_scalar(part_of[:, n:n + 1], rank_p[:, 0:1], float((n + 1) * R), -float(R), ALU.is_ge, ALU.mult)
                dve_order.link(v, last)
                for n in range(2):
                    dve_order.link(v, nc.vector.tensor_scalar(k_at[:], rank_p[:] if n == 0 else k_at[:], part_of[:, n:n + 1], None, ALU.add))
                dve_order.link(v, nc.vector.tensor_copy(src_f[:], src_i[:]))
                dve_order.link(v, nc.vector.tensor_scalar(lo[:], src_f[:], -float(P // 2), 1.0 / P, ALU.add, ALU.mult))
                dve_order.link(v, nc.vector.tensor_scalar(hi[:], lo[:], MAGIC, None, ALU.add))
                dve_order.link(v, nc.vector.tensor_scalar(hi[:], hi[:], MAGIC, None, ALU.subtract))
                dve_order.link(v, nc.vector.scalar_tensor_tensor(lo[:], hi[:], -float(P), src_f[:], ALU.mult, ALU.add))
                v.sem_inc(s_free, G)
                v.sem_inc(s_kt, G)
                v.sem_inc(s_kfree, 3)
                k_onehots(0, K_SLOT[0], 0)
                with v.Fori(0, EITER) as i:
                    for g in range(G):
                        at = bass.ds(i * G * G + g * G, G)
                        k_onehots((g + 1) % G, K_SLOT[(g + 1) % G], i + (g + 1) // G)
                        v.wait_ge(s_ohu, i * G + g + 1)
                        nc.vector.tensor_tensor(oh_lo[:, g], iota_row[:].unsqueeze(1).to_broadcast([P, G, P]),
                                                lo[:, at].unsqueeze(2).to_broadcast([P, G, P]), ALU.is_equal)
                        nc.vector.tensor_tensor(oh_hi[:, g], iota_row[:, 0:T].unsqueeze(1).to_broadcast([P, G, T]),
                                                hi[:, at].unsqueeze(2).to_broadcast([P, G, T]), ALU.is_equal).then_inc(s_oh, 1)
                        v.wait_ge(s_got[g], G * 16 * (i + 1))
                        for m, (a, b) in enumerate(BANKS):
                            v.wait_ge(s_kx, (i * G + g) * 3 + m + 1)
                            nc.vector.tensor_tensor(qr[:, g, a:b].rearrange("p u d -> p (u d)"),
                                                    qr[:, g, a:b].rearrange("p u d -> p (u d)"),
                                                    psK[0:P, m, 0:(b - a) * D], ALU.mult).then_inc(s_kfree, 1)
                        v.wait_ge(s_kfree, (i * G + g) * 3 + 6)
                        v.sem_inc(carrier, 1)
                        nc.vector.tensor_reduce(dots[:, :, at].rearrange("p h u -> p u h"),
                                                qr[:, g].rearrange("p u (h d) -> p u h d", h=H), AX.X, ALU.add).then_inc(s_free, 1)
                v.wait_ge(s_cnt, 1)
                dve_order.link(v, nc.vector.tensor_copy(counts[:, 0, :], psC[0:P, 0:T]))

        for s in sems0:
            nc.release_semaphore(s)

        x_sb = sb(top, "x_sb", [P, T, D])
        carry_on = sb(top, "carry_on", [P, T, P])
        attn = sb(top, "attn", [P, T, H])
        s_next, s_rows, s_cont = sem("next_loaded"), sem("heads_tails"), sem("carry_on_made")
        s_rowsT, s_rowsK, s_lr, s_lrT = (sem(n) for n in ("rows_turned", "rows_kept", "reach_made", "reach_turned"))
        s_dot, s_xback, s_targets, s_m, s_ex, s_sums, s_sumst, s_den, s_over = (sem(n) for n in (
            "dots_loaded", "x_back", "targets_ready", "shifted", "exp_done", "sums_ready", "sums_stored", "sums_gathered", "over_done"))
        with ExitStack() as st:
            fmax = sb(st, "fmax", [P, H, J])
            rmax = sb(st, "rmax", [P, H, J])
            sums = sb(st, "sums", [P, J, H])
            next_i = sb(st, "next_i", [P, 1], I32)
            next_f = sb(st, "next_f", [P, 1])
            key = sb(st, "key", [P, 2])
            apart = sb(st, "apart", [P, J + 1])
            first = sb(st, "first", [P, 2, J])
            cols = sb(st, "cols", [P, 4, H])
            row = sb(st, "row", [H, 4, P])
            gap = sb(st, "gap", [H, 3, P])
            ext = sb(st, "ext", [H, 4, P])
            reach = sb(st, "reach", [P, 2, H])
            pre = sb(st, "pre", [P, T])
            dot = sb(st, "dot", [P, H, J])
            den = sb(st, "den", [P, T, H])
            den2 = sb(st, "den2", [P, T, H])
            psR = ps(st, "psR2", [128, 512])
            psL = ps(st, "psL2", [128, 512])
            psO = ps(st, "psO2", [128, 512])
            block = st.enter_context(nc.Block())
            TAIL, HEAD, FIRST, LAST = range(4)

            @block.sync
            def _(sp):
                for a, b in HALVES:
                    sp.dma_start(dot[a:b], dot_rows.rearrange("h (p j) -> p h j", p=P)[a:b]).then_inc(s_dot, 16)
                sp.wait_ge(s_next, 1)
                sp.dma_start(next_i[0:P - 1, :], dst.rearrange("(p j) -> p j", p=P)[1:P, 0:1],
                             allow_slow_non_contiguous=True).then_inc(s_next, 16)
                for a, b in HALVES:
                    sp.dma_start(x_sb[a:b], rows_of_tiles(x)[a:b]).then_inc(s_xback, 16)
                sp.wait_ge(s_sums, 1)
                for a, b in HALVES:
                    sp.dma_start(expsum_rows.rearrange("(p j) h -> p (j h)", p=P)[a:b, :],
                                 sums[a:b].rearrange("p j h -> p (j h)")).then_inc(s_sumst, 16)
                sp.wait_ge(s_xback, 32)

            @block.gpsimd
            def _(pool):
                nc.gpsimd.iota(carry_on[:], pattern=[[P, T], [1, P]], base=0, channel_multiplier=0,
                               allow_small_or_imprecise_dtypes=True).then_inc(s_targets, 1)
                pool.wait_ge(s_sumst, 32)
                for t in range(T):
                    nc.gpsimd.indirect_dma_start(out=den[:, t, :], out_offset=None, in_=expsum_rows,
                                                 in_offset=bass.IndirectOffsetOnAxis(ap=end_i[:, t:t + 1], axis=0))\
                      .then_inc(s_den, 16)

            @block.scalar
            def _(act):
                act.wait_ge(s_m, 1)
                nc.scalar.activation(fmax[:], rmax[:], ACT.Exp).then_inc(s_ex, 1)

            @block.tensor
            def _(pe):
                pe.wait_ge(s_rows, 1)
                for n in range(4):
                    last = nc.tensor.transpose(psR[0:H, n * P:(n + 1) * P], cols[:, n, :], ident[0:P, 0:P])
                last.then_inc(s_rowsT, 1)
                pe.wait_ge(s_lr, 1)
                for n in range(2):
                    last = nc.tensor.transpose(psL[0:P, n * H:(n + 1) * H], ext[:, 2 + n, :], ident[0:H, 0:H])
                last.then_inc(s_lrT, 1)
                pe.wait_ge(s_sums, 1)
                pe.wait_ge(s_cont, 1)
                for t in range(T):
                    last = nc.tensor.matmul(psO[0:P, t * H:(t + 1) * H], carry_on[:, t, :], sums[:, J - 1, :],
                                            start=True, stop=True)
                last.then_inc(s_over, 1)

            @block.vector
            def _(v):
                link = lambda ins: dve_order.link(v, ins)
                nc.vector.memset(next_i[:], -1).then_inc(s_next, 1)
                link(nc.vector.tensor_scalar(pre[:], counts[:, 0, :], 1.0, None, ALU.max))
                inverse_root(v, rsq_deg[:], pre[:], root_t[:])
                nc.vector.memset(apart[:, J:J + 1], -BIG)
                nc.vector.tensor_scalar(apart[:, 0:J], same[:], -1.0, BIG, ALU.add, ALU.mult)
                for n, c in ((0, 0), (1, J - 1)):
                    last = nc.vector.tensor_scalar(first[:, n, :], dst_f[:], dst_f[:, c:c + 1], None, ALU.is_equal)
                link(last)
                link(nc.vector.tensor_scalar(first[:], first[:], -1.0, BIG, ALU.add, ALU.mult))
                v.wait_ge(s_dot, 32)
                link(nc.vector.tensor_tensor(score[:], score[:], dot[:], ALU.add))
                for h in range(H):
                    last = nc.vector.tensor_tensor_scan(fmax[:, h, :], apart[:, 0:J], score[:, h, :], -BIG, ALU.add, ALU.max)
                link(last)
                for h in range(H):
                    last = nc.vector.tensor_tensor_scan(rmax[:, h, ::-1], apart[:, 1:J + 1][:, ::-1], fmax[:, h, ::-1], -BIG,
                                                        ALU.add, ALU.max)
                link(last)
                nc.vector.tensor_copy(cols[:, TAIL, :], rmax[:, :, J - 1])
                nc.vector.tensor_copy(cols[:, HEAD, :], rmax[:, :, 0])
                nc.vector.tensor_copy(cols[:, FIRST, :], dst_f[:, 0:1].to_broadcast([P, H]))
                nc.vector.tensor_copy(cols[:, LAST, :], dst_f[:, J - 1:J].to_broadcast([P, H])).then_inc(s_rows, 1)
                v.wait_ge(s_rowsT, 1)
                nc.vector.memset(gap[:], 0.0)
                link(nc.vector.tensor_copy(row[:].rearrange("h n p -> h (n p)"), psR[0:H, 0:4 * P]))
                nc.vector.tensor_tensor(gap[:, 0, 1:P], row[:, LAST, 1:P], row[:, LAST, 0:P - 1], ALU.is_equal)
                nc.vector.tensor_tensor(gap[:, 1, 0:P - 1], row[:, FIRST, 0:P - 1], row[:, FIRST, 1:P], ALU.is_equal)
                link(nc.vector.tensor_tensor(gap[:, 2, 1:P], row[:, FIRST, 1:P], row[:, LAST, 0:P - 1], ALU.is_equal))
                link(nc.vector.tensor_scalar(gap[:], gap[:], -1.0, BIG, ALU.add, ALU.mult))
                nc.vector.memset(ext[:, 2:4, :], -BIG)
                nc.vector.tensor_tensor_scan(ext[:, 0, :], gap[:, 0, :], row[:, TAIL, :], -BIG, ALU.add, ALU.max)
                link(nc.vector.tensor_tensor_scan(ext[:, 1, ::-1], gap[:, 1, ::-1], row[:, HEAD, ::-1], -BIG, ALU.add, ALU.max))
                nc.vector.tensor_tensor(ext[:, 2, 1:P], ext[:, 0, 0:P - 1], gap[:, 2, 1:P], ALU.add)
                nc.vector.tensor_tensor(ext[:, 3, 0:P - 1], ext[:, 1, 1:P], gap[:, 2, 1:P], ALU.add).then_inc(s_lr, 1)
                v.wait_ge(s_lrT, 1)
                link(nc.vector.tensor_copy(reach[:].rearrange("p n h -> p (n h)"), psL[0:P, 0:2 * H]))
                for n in range(2):
                    for h in range(H):
                        last = nc.vector.scalar_tensor_tensor(rmax[:, h, :], first[:, n, :], reach[:, n, h:h + 1], rmax[:, h, :],
                                                              ALU.add, ALU.max)
                    link(last)
                nc.vector.tensor_tensor(rmax[:], score[:], rmax[:], ALU.subtract).then_inc(s_m, 1)
                v.wait_ge(s_next, 17)
                link(nc.vector.tensor_copy(next_f[:], next_i[:]))
                link(nc.vector.tensor_tensor(key[:, 0:1], dst_f[:, J - 1:J], next_f[:], ALU.is_equal))
                link(nc.vector.tensor_scalar(key[:, 1:2], dst_f[:, J - 1:J], 1.0, None, ALU.add))
                link(nc.vector.tensor_tensor(key[:, 1:2], key[:, 1:2], key[:, 0:1], ALU.mult))
                link(nc.vector.tensor_scalar(key[:, 1:2], key[:, 1:2], -1.0, None, ALU.add))
                v.wait_ge(s_targets, 1)
                nc.vector.tensor_scalar(carry_on[:], carry_on[:], key[:, 1:2], None, ALU.is_equal).then_inc(s_cont, 1)
                v.wait_ge(s_ex, 1)
                for h in range(H):
                    last = nc.vector.tensor_tensor_scan(sums[:, :, h], same[:], fmax[:, h, :], 0.0, ALU.mult, ALU.add)
                last.then_inc(s_sums, 1)
                v.wait_ge(s_den, 16 * T)
                v.wait_ge(s_over, 1)
                link(nc.vector.tensor_tensor(den[:], den[:], has_in[:].unsqueeze(2).to_broadcast([P, T, H]), ALU.mult))
                link(nc.vector.tensor_tensor(den[:], den[:], psO[0:P, 0:T * H].rearrange("p (t h) -> p t h", h=H), ALU.add))
                link(nc.vector.tensor_scalar(den2[:], den[:], 1e-30, None, ALU.max))
                link(nc.vector.reciprocal(den2[:], den2[:]))
                link(nc.vector.tensor_tensor(attn[:], den[:], den2[:], ALU.mult))

        s_w3, s_agg, s_trA, s_tA, s_trB, s_tB, s_o3, s_n3, s_kept3, s_h3, s_ge3, s_lg3, s_lg3e = (sem(n) for n in (
            "w3_loaded", "agg_ready", "agg_turned", "aggT_ready", "n3_turned", "n3T_ready", "o3_done", "n3_ready", "n3_kept",
            "h3_done", "gelu3_done", "logits3_done", "logits3_kept"))
        HALF = (313, 312)
        with ExitStack() as st:
            wo = sb(st, "wo", [128, KD, D])
            bo = sb(st, "bo", [1, D])
            w1 = sb(st, "w1_3", [128, KD, C])
            wg = sb(st, "wg", [128, KC, X])
            tile_a = sb(st, "tile_a", [P, G, D])
            tT = sb(st, "tT3", [128, G * KD, P])
            nT = sb(st, "nT3", [128, KD, G * P])
            hT = sb(st, "hT3", [128, KC, G * P])
            psT = ps(st, "psT3", [128, 3, 512])
            psO = ps(st, "psO3", [128, 3 * 512])
            psH = ps(st, "psH3", [128, 2, 512])
            psG = psT[0:P, 2, 256:256 + G * X]
            block = st.enter_context(nc.Block())

            @block.sync
            def _(sp):
                sp.dma_start(wo[:], L0_gnn_Wo.rearrange("(k p) d -> p k d", p=128)).then_inc(s_w3, 16)
                sp.dma_start(bo[:], L0_gnn_bo.rearrange("(a d) -> a d", a=1)).then_inc(s_w3, 16)
                sp.dma_start(w1[:], L0_ffn_W1.rearrange("(k p) d -> p k d", p=128)).then_inc(s_w3, 16)
                sp.dma_start(wg[:], L0_ffn_Wg.rearrange("(k p) d -> p k d", p=128)).then_inc(s_w3, 16)
                sp.dma_start(gate_b[:], L0_ffn_bg.partition_broadcast(P)).then_inc(s_w3, 16)
                sp.wait_ge(s_w3, 80)

            @block.vector
            def _(v):
                def weigh(i):
                    tiles = bass.ds(i * G, G)
                    nc.vector.tensor_tensor(tile_a[:].rearrange("p u (h d) -> p (u h) d", h=H),
                                            n_sb[:, tiles, :].rearrange("p u (h d) -> p (u h) d", h=H),
                                            attn[:, tiles, :].rearrange("p u h -> p (u h)").unsqueeze(2)
                                            .to_broadcast([P, G * H, DH]), ALU.mult).then_inc(s_agg, 1)

                def update(i):
                    tiles = bass.ds(i * G, G)
                    v.wait_ge(s_o3, i + 1)
                    dve_order.link(v, nc.vector.tensor_tensor(x_sb[:, tiles, :], x_sb[:, tiles, :],
                                                              psO[0:P, :].rearrange("p (u d) -> p u d", d=D)[:, 0:G, :], ALU.add))
                    v.wait_ge(s_trB, i + 1)
                    dve_order.link(v, normalise(v, lambda u: x_sb[:, bass.ds(i * G + u, 1), :].rearrange("p a d -> p (a d)"),
                                                lambda u: tile_n[:, u, :]))
                    v.sem_inc(s_n3, 1)
                    nc.vector.tensor_tensor(n_sb[:, tiles, :], tile_n[:], tile_n[:], ALU.max).then_inc(s_kept3, 1)

                v.sem_inc(s_n3, 1)
                weigh(0)
                update_links = 16
                update(0)
                weigh(1)
                with v.Fori(1, NG - 1) as i:
                    dve_order.turn(i - 1, update_links)
                    update(i)
                    weigh(i + 1)
                dve_order.leave(NG - 2)
                update(NG - 1)
                v.wait_ge(s_kept3, NG)

            @block.scalar
            def _(act):
                def fetch_aggregate(i):
                    act.wait_ge(s_trA, i + 1)
                    fetch_turned(tT, psT).then_inc(s_tA, 1)

                def gelus(i):
                    act.wait_ge(s_trB, i + 2)
                    for u in range(G):
                        for k in range(KD):
                            n = u * KD + k
                            last = nc.scalar.activation(nT[:, k, u * P:(u + 1) * P],
                                                        psT[:, n // 4, (n % 4) * P:(n % 4 + 1) * P], ACT.Copy)
                    last.then_inc(s_tB, 1)
                    for n in range(2 * KC):
                        m, f = n // 2, n % 2
                        act.wait_ge(s_h3, i * 2 * KC + n + 1)
                        nc.scalar.activation(hT[:, m, f * HALF[0]:f * HALF[0] + HALF[f]], psH[:, n % 2, 0:HALF[f]], ACT.Gelu,
                                             bias=b1_0[:, m:m + 1]).then_inc(s_ge3, 1)

                def keep_logits(i):
                    act.wait_ge(s_lg3, i + 1)
                    act.sem_inc(carrier, 1)
                    nc.scalar.activation(logits[:, bass.ds(i * G, G), :].rearrange("p u e -> p (u e)"), psG, ACT.Copy)\
                      .then_inc(s_lg3e, 1)

                act.sem_inc(s_lg3e, 1)
                fetch_aggregate(0)
                with act.Fori(0, NG - 1) as i:
                    fetch_aggregate(i + 1)
                    gelus(i)
                    keep_logits(i)
                gelus(NG - 1)
                keep_logits(NG - 1)

            @block.tensor
            def _(pe):
                def project(i):
                    pe.wait_ge(s_agg, i + 1)
                    turn_tiles(pe, psT, tile_a).then_inc(s_trA, 1)
                    pe.wait_ge(s_tA, i + 1)
                    pe.wait_ge(s_n3, i + 1)
                    for u in range(G):
                        nc.tensor.matmul(psO[0:P, u * D:(u + 1) * D], ones[0:1, 0:P], bo[:], start=True, stop=False)
                        for k in range(KD):
                            last = nc.tensor.matmul(psO[0:P, u * D:(u + 1) * D], tT[:, u * KD + k, :], wo[:, k, :],
                                                    start=False, stop=(k == KD - 1))
                    last.then_inc(s_o3, 1)

                def gate_logits(i):
                    pe.wait_ge(s_n3, i + 2)
                    turn_tiles(pe, psT, tile_n).then_inc(s_trB, 1)
                    pe.wait_ge(s_tB, i + 1)
                    for n in range(2 * KC):
                        m, f = n // 2, n % 2
                        if n >= 2:
                            pe.wait_ge(s_ge3, i * 2 * KC + n - 1)
                        for k in range(KD):
                            last = nc.tensor.matmul(psH[:, n % 2, 0:HALF[f]], w1[:, k, m * 128:(m + 1) * 128],
                                                    nT[:, k, f * HALF[0]:f * HALF[0] + HALF[f]],
                                                    start=(k == 0), stop=(k == KD - 1))
                        last.then_inc(s_h3, 1)
                    pe.wait_ge(s_ge3, (i + 1) * 2 * KC)
                    for u in range(G):
                        for m in range(KC):
                            last = nc.tensor.matmul(psG[:, u * X:(u + 1) * X], hT[:, m, u * P:(u + 1) * P], wg[:, m, :],
                                                    start=(m == 0), stop=(m == KC - 1))
                    last.then_inc(s_lg3, 1)

                pe.sem_inc(s_trB, 1)
                pe.wait_ge(s_w3, 80)
                project(0)
                with pe.Fori(0, NG - 1) as i:
                    pe.wait_ge(s_lg3e, i + 1)
                    project(i + 1)
                    gate_logits(i)
                pe.wait_ge(s_lg3e, NG)
                gate_logits(NG - 1)

        def route(name, picks, n_blocks, xg):
            s_pick, s_cum, s_slot, s_block, s_scat = (sem(name + n) for n in (
                "_picked", "_counted", "_slots", "_blocks", "_scattered"))
            with ExitStack() as st:
                e3 = sb(st, name + "e3", [P, T, X])
                prob = sb(st, name + "prob", [P, T, X])
                work = sb(st, name + "work", [P, T, X])
                pick = sb(st, name + "pick", [P, 2, T, X])
                both = sb(st, name + "both", [P, T, X])
                col = sb(st, name + "col", [P, 4, T])
                tot = sb(st, name + "tot", [P, T, X])
                run = sb(st, name + "run", [P, T, X])
                one_row = sb(st, name + "ones", [P, T])
                step = sb(st, name + "step", [P, X, T])
                full = sb(st, name + "full", [P, X, T])
                nblk = sb(st, name + "nblk", [P, 3, X])
                slot_f = sb(st, name + "slot_f", [P, 2, T])
                b_of = sb(st, name + "b_of", [1, n_blocks, X])
                be_f = sb(st, name + "be_f", [1, n_blocks])
                psN = ps(st, name + "psN", [128, 512])
                block = st.enter_context(nc.Block())
                s_iota = sem(name + "_iota")

                @block.gpsimd
                def _(pool):
                    nc.gpsimd.iota(step[:], pattern=[[0, X], [S, T]], base=0, channel_multiplier=0,
                                   allow_small_or_imprecise_dtypes=True).then_inc(s_iota, 1)
                    nc.gpsimd.iota(b_of[:], pattern=[[1, n_blocks], [0, X]], base=0, channel_multiplier=0,
                                   allow_small_or_imprecise_dtypes=True).then_inc(s_iota, 1)
                    pool.wait_ge(s_slot, 1)
                    for k in range(picks):
                        for t in range(T):
                            nc.gpsimd.indirect_dma_start(out=xg, out_offset=bass.IndirectOffsetOnAxis(
                                ap=slot_i[:, k, t:t + 1], axis=0), in_=n_sb[:, t, :], in_offset=None).then_inc(s_scat, 16)
                    pool.wait_ge(s_scat, 16 * picks * T)

                @block.scalar
                def _(act):
                    act.wait_ge(s_pick, 1)
                    nc.scalar.activation(prob[:], work[:], ACT.Exp).then_inc(s_pick, 1)

                @block.tensor
                def _(pe):
                    pe.wait_ge(s_pick, 3)
                    nc.tensor.matmul(psN[0:P, 0:T * X], before[:], both[:].rearrange("p t e -> p (t e)"), start=True, stop=True)
                    nc.tensor.matmul(psN[0:P, T * X:2 * T * X], ones[0:P, 0:P], both[:].rearrange("p t e -> p (t e)"),
                                     start=True, stop=True).then_inc(s_cum, 1)

                @block.vector
                def _(v):
                    link = lambda ins: dve_order.link(v, ins)
                    over_e = lambda c: col[:, c, :].unsqueeze(2).to_broadcast([P, T, X])
                    link(nc.vector.memset(one_row[:], 1.0))
                    link(nc.vector.tensor_tensor(logits[:], logits[:], gate_b[:].unsqueeze(1).to_broadcast([P, T, X]), ALU.add))
                    link(nc.vector.tensor_reduce(col[:, 0, :], logits[:], AX.X, ALU.max))
                    nc.vector.tensor_tensor(work[:], logits[:], over_e(0), ALU.subtract).then_inc(s_pick, 1)
                    v.wait_ge(s_pick, 2)
                    link(nc.vector.tensor_reduce(col[:, 0, :], prob[:], AX.X, ALU.add))
                    link(nc.vector.reciprocal(col[:, 0, :], col[:, 0, :]))
                    link(nc.vector.tensor_tensor(prob[:], prob[:], over_e(0), ALU.mult))
                    for k in range(picks):
                        link(nc.vector.tensor_reduce(gate[:, k, :], prob[:], AX.X, ALU.max))
                        link(nc.vector.tensor_tensor(work[:], prob[:], gate[:, k, :].unsqueeze(2).to_broadcast([P, T, X]),
                                                     ALU.is_equal))
                        link(nc.vector.tensor_tensor(work[:], work[:], rank8[:], ALU.mult))
                        link(nc.vector.tensor_reduce(col[:, 1, :], work[:], AX.X, ALU.max))
                        link(nc.vector.tensor_tensor(pick[:, k], rank8[:], over_e(1), ALU.is_equal))
                        if k + 1 < picks:
                            link(nc.vector.scalar_tensor_tensor(prob[:], pick[:, k], -2.0, prob[:], ALU.mult, ALU.add))
                    if picks == 2:
                        nc.vector.tensor_tensor(both[:], pick[:, 0], pick[:, 1], ALU.add).then_inc(s_pick, 1)
                        link(nc.vector.tensor_tensor(col[:, 2, :], gate[:, 0, :], gate[:, 1, :], ALU.add))
                        link(nc.vector.reciprocal(col[:, 2, :], col[:, 2, :]))
                        link(nc.vector.tensor_tensor(gate[:], gate[:], col[:, 2, :].unsqueeze(1).to_broadcast([P, 2, T]), ALU.mult))
                    else:
                        nc.vector.tensor_copy(both[:], pick[:, 0]).then_inc(s_pick, 1)
                    v.wait_ge(s_cum, 1)
                    v.wait_ge(s_iota, 2)
                    link(nc.vector.tensor_copy(tot[:].rearrange("p t e -> p (t e)"), psN[0:P, T * X:2 * T * X]))
                    for e in range(X):
                        last = nc.vector.tensor_tensor_scan(run[:, :, e], one_row[:], tot[:, :, e], 0.0, ALU.mult, ALU.add)
                    link(last)
                    link(nc.vector.tensor_tensor(full[:], run[:, T - 1, :].unsqueeze(2).to_broadcast([P, X, T]), step[:], ALU.is_gt))
                    link(nc.vector.tensor_reduce(nblk[:, 0, :], full[:], AX.X, ALU.add))
                    link(nc.vector.tensor_tensor_scan(nblk[:, 1, :], one_row[:, 0:X], nblk[:, 0, :], 0.0, ALU.mult, ALU.add))
                    link(nc.vector.tensor_tensor(nblk[:, 2, :], nblk[:, 1, :], nblk[:, 0, :], ALU.subtract))
                    link(nc.vector.tensor_tensor(run[:], run[:], tot[:], ALU.subtract))
                    link(nc.vector.tensor_tensor(run[:], run[:], psN[0:P, 0:T * X].rearrange("p (t e) -> p t e", e=X), ALU.add))
                    link(nc.vector.tensor_scalar(nblk[:, 0, :], nblk[:, 2, :], float(S), None, ALU.mult))
                    link(nc.vector.tensor_tensor(run[:], run[:], nblk[:, 0, :].unsqueeze(1).to_broadcast([P, T, X]), ALU.add))
                    for k in range(picks):
                        link(nc.vector.tensor_tensor(work[:], run[:], pick[:, k], ALU.mult))
                        link(nc.vector.tensor_reduce(slot_f[:, k, :], work[:], AX.X, ALU.add))
                        last = nc.vector.tensor_copy(slot_i[:, k, :], slot_f[:, k, :])
                    last.then_inc(s_slot, 1)
                    link(nc.vector.tensor_tensor(b_of[:], b_of[:], nblk[0:1, 1, :].unsqueeze(1)
                                                 .to_broadcast([1, n_blocks, X]), ALU.is_ge))
                    link(nc.vector.tensor_reduce(be_f[:], b_of[:], AX.X, ALU.add))
                    link(nc.vector.tensor_scalar(be_f[:], be_f[:], float(X - 1), None, ALU.min))
                    link(nc.vector.tensor_copy(block_e[:, 0:n_blocks], be_f[:]))

        def experts(name, n_blocks, xg, yg, W1, W2, b2, own_w1):
            s_w1c, s_x0 = sem(name + "_common_w1"), [sem(f"{name}_rows{n}") for n in range(2)]
            s_w1 = [sem(f"{name}_w1_{n}_loaded") for n in range(2)] if own_w1 else None
            s_w2 = [sem(f"{name}_w2_{n}_loaded") for n in range(2)]
            s_tr, s_xT, s_h, s_ge, s_y, s_ye, s_yfree, s_yst = (sem(name + n) for n in (
                "_turned", "_xT_ready", "_hidden", "_gelu", "_y_done", "_y_ready", "_y_free", "_y_stored"))
            turns = n_blocks // 2
            assert n_blocks == 2 * turns
            with ExitStack() as st:
                w1 = [sb(st, f"{name}w1_{n}", [128, KD, C]) for n in range(2 if own_w1 else 1)]
                w2 = [sb(st, f"{name}w2_{n}", [128, KC, D]) for n in range(2)]
                b2r = [sb(st, f"{name}b2_{n}", [S, D]) for n in range(2)]
                xr = [sb(st, f"{name}xr_{n}", [S, D]) for n in range(2)]
                xT = [sb(st, f"{name}xT_{n}", [128, KD, S]) for n in range(2)]
                hT = [sb(st, f"{name}hT_{n}", [128, KC, S]) for n in range(2)]
                yr = [sb(st, f"{name}yr_{n}", [S, D]) for n in range(2)]
                par = [sb(st, f"{name}par_{n}", [128, KC + 2 * KD]) for n in range(2)]
                psT = ps(st, name + "psT", [128, 2, 512])
                psH = [ps(st, f"{name}psH{n}", [128, C]) for n in range(2)]
                psY = ps(st, name + "psY", [128, 2, 512])
                exp_flat = exp_par[:].rearrange("p e c -> p (e c)")
                npar = KC + 2 * KD
                block = st.enter_context(nc.Block())

                @block.sync
                def _(sp):
                    if not own_w1:
                        sp.dma_start(w1[0][:], W1.rearrange("(k p) c -> p k c", p=128)).then_inc(s_w1c, 16)
                    def expert_of(at):
                        return sp.value_load(block_e[0:1, at], min_val=0, max_val=X - 1)

                    def load_rows_and_w1(b, s, at):
                        sp.wait_ge(s_tr, b + 1)
                        sp.dma_start(xr[s][:], xg[bass.ds(b * S, S), :]).then_inc(s_x0[s], 16)
                        if own_w1:
                            e = expert_of(at)
                            sp.wait_ge(s_h, b * 2 + 2)
                            sp.dma_start(w1[s][:], W1[bass.ds(e, 1)].rearrange("a (k p) c -> p (a k) c", p=128))\
                              .then_inc(s_w1[s], 16)

                    def load_w2(b, s, at):
                        e = expert_of(at)
                        sp.wait_ge(s_ye, b + 1)
                        sp.dma_start(w2[s][:], W2[bass.ds(e, 1)].rearrange("a (k p) c -> p (a k) c", p=128)).then_inc(s_w2[s], 16)
                        sp.dma_start(b2r[s][:], b2[bass.ds(e, 1), :].to_broadcast([S, D])).then_inc(s_w2[s], 16)

                    load_rows_and_w1(0, 0, slice(0, 1))
                    with sp.Fori(0, turns - 1) as t:
                        load_rows_and_w1(t * 2 + 1, 1, bass.ds(t * 2 + 1, 1))
                        load_w2(t * 2, 0, bass.ds(t * 2, 1))
                        load_rows_and_w1(t * 2 + 2, 0, bass.ds(t * 2 + 2, 1))
                        load_w2(t * 2 + 1, 1, bass.ds(t * 2 + 1, 1))
                    load_rows_and_w1(n_blocks - 1, 1, slice(n_blocks - 1, n_blocks))
                    for b in (n_blocks - 2, n_blocks - 1):
                        load_w2(b, b % 2, slice(b, b + 1))

                @block.gpsimd
                def _(pool):
                    pool.sem_inc(s_yfree, 2)
                    with pool.Fori(0, turns) as t:
                        for s in range(2):
                            pool.wait_ge(s_ye, t * 2 + s + 1 + 2)
                            pool.sem_inc(carrier, 1)
                            pool.dma_start(yg[bass.ds((t * 2 + s) * S, S), :], yr[s][:]).then_inc(s_yst, 16)
                            pool.wait_ge(s_yst, (t * 2 + s + 1) * 16)
                            pool.sem_inc(s_yfree, 1)

                @block.scalar
                def _(act):
                    act.sem_inc(s_ge, 2)
                    with act.Fori(0, turns) as t:
                        for s in range(2):
                            for m in range(KC):
                                if m % (KC // 2) == 0:
                                    act.wait_ge(s_h, (t * 2 + s) * 2 + 5 + m // (KC // 2))
                                last = nc.scalar.activation(hT[s][:, m, :], psH[s][:, m * 128:(m + 1) * 128], ACT.Gelu,
                                                            bias=par[s][:, m:m + 1] if own_w1 else b1_0[:, m:m + 1])
                            last.then_inc(s_ge, 1)

                @block.tensor
                def _(pe):
                    def turn(t, s):
                        pe.wait_ge(s_x0[s], (t + 1) * 16)
                        for k in range(KD):
                            last = nc.tensor.transpose(psT[:, s, k * 128:(k + 1) * 128], xr[s][:, k * 128:(k + 1) * 128], ident[:])
                        last.then_inc(s_tr, 1)

                    def hidden(t, s):
                        b = t * 2 + s
                        pe.wait_ge(s_xT, b + 1)
                        if own_w1:
                            pe.wait_ge(s_w1[s], (t + 1) * 16)
                        pe.wait_ge(s_ge, b + 1)
                        for m in range(KC):
                            for k in range(KD):
                                last = nc.tensor.matmul(psH[s][:, m * 128:(m + 1) * 128],
                                                        w1[s if own_w1 else 0][:, k, m * 128:(m + 1) * 128], xT[s][:, k, :],
                                                        start=(k == 0), stop=(k == KD - 1))
                            if m % (KC // 2) == KC // 2 - 1:
                                last.then_inc(s_h, 1)

                    def output(t, s):
                        b = t * 2 + s
                        pe.wait_ge(s_w2[s], (t + 1) * 32)
                        pe.wait_ge(s_ge, b + 3)
                        pe.wait_ge(s_ye, b + 1)
                        for m in range(KC):
                            last = nc.tensor.matmul(psY[:, s, 0:D], hT[s][:, m, :], w2[s][:, m, :],
                                                    start=(m == 0), stop=(m == KC - 1))
                        last.then_inc(s_y, 1)

                    pe.sem_inc(s_tr, 2)
                    pe.sem_inc(s_h, 4)
                    turn(0, 0)
                    turn(0, 1)
                    if not own_w1:
                        pe.wait_ge(s_w1c, 16)
                    hidden(0, 0)
                    with pe.Fori(0, turns - 1) as t:
                        hidden(t, 1)
                        turn(t + 1, 0)
                        output(t, 0)
                        hidden(t + 1, 0)
                        turn(t + 1, 1)
                        output(t, 1)
                    hidden(turns - 1, 1)
                    output(turns - 1, 0)
                    output(turns - 1, 1)

                @block.vector
                def _(v):
                    def fetch_rows(t, s, order):
                        b = t * 2 + s
                        if own_w1:
                            e = v.value_load(block_e[0:1, order], min_val=0, max_val=X - 1)
                            v.wait_ge(s_ge, b + 1)
                            v.sem_inc(carrier, 1)
                            dve_order.link(v, nc.vector.tensor_copy(par[s][:], exp_flat[:, bass.ds(e * npar, npar)]))
                        v.wait_ge(s_tr, b + 3)
                        if own_w1:
                            for k in range(KD):
                                last = nc.vector.tensor_scalar(xT[s][:, k, :], psT[:, s, k * 128:(k + 1) * 128],
                                                               par[s][:, KC + k:KC + k + 1],
                                                               par[s][:, KC + KD + k:KC + KD + k + 1], ALU.mult, ALU.add)
                        else:
                            last = nc.vector.tensor_copy(xT[s][:].rearrange("p k c -> p (k c)"), psT[:, s, 0:KD * 128])
                        last.then_inc(s_xT, 1)

                    def fetch_output(t, s):
                        b = t * 2 + s
                        v.wait_ge(s_y, b + 1)
                        v.wait_ge(s_yfree, b + 1)
                        nc.vector.tensor_tensor(yr[s][:], psY[:, s, 0:D], b2r[s][:], ALU.add).then_inc(s_ye, 1)

                    v.sem_inc(s_ye, 2)
                    for s in range(2):
                        fetch_rows(0, s, slice(s, s + 1))
                    with v.Fori(0, turns - 1) as t:
                        if own_w1:
                            dve_order.turn(t, 2)
                        for s in range(2):
                            fetch_rows(t + 1, s, bass.ds(t * 2 + s + 2, 1))
                            fetch_output(t, s)
                    if own_w1:
                        dve_order.leave(turns - 1)
                    for s in range(2):
                        fetch_output(turns - 1, s)

        route("r0", 1, NB0, xg0)
        experts("m0", NB0, xg0, yg0, L0_ffn_W1, L0_ffn_Wd, L0_ffn_bd, False)

        s_y0, s_f6, s_f6st = sem("y0_gathered"), sem("f6_ready"), sem("f6_stored")
        with ExitStack() as st:
            yt = sb(st, "yt6", [P, T, D])
            block = st.enter_context(nc.Block())

            @block.gpsimd
            def _(pool):
                for t in range(T):
                    nc.gpsimd.indirect_dma_start(out=yt[:, t, :], out_offset=None, in_=yg0,
                                                 in_offset=bass.IndirectOffsetOnAxis(ap=slot_i[:, 0, t:t + 1], axis=0))\
                      .then_inc(s_y0, 16)

            @block.vector
            def _(v):
                v.wait_ge(s_y0, 16 * T)
                with v.Fori(0, NG) as i:
                    dve_order.turn(i, 16)
                    one = lambda a, u: a[:, bass.ds(i * G + u, 1), :].rearrange("p a d -> p (a d)")
                    for u in range(G):
                        last = nc.vector.scalar_tensor_tensor(one(x_sb, u), one(yt, u), gate[:, 0, bass.ds(i * G + u, 1)],
                                                              one(x_sb, u), ALU.mult, ALU.add)
                    dve_order.link(v, last)
                    dve_order.link(v, normalise(v, lambda u: one(x_sb, u), lambda u: one(n_sb, u)))
                    nc.vector.tensor_tensor(yt[:, bass.ds(i * G, G), :], n_sb[:, bass.ds(i * G, G), :],
                                            rsq_deg[:, bass.ds(i * G, G)].unsqueeze(2).to_broadcast([P, G, D]), ALU.mult)\
                      .then_inc(s_f6, 1)
                dve_order.leave(NG)

            @block.sync
            def _(sp):
                with sp.Fori(0, NG) as i:
                    sp.wait_ge(s_f6, i + 1)
                    sp.dma_start(rows_of_tiles(f_rows)[:, bass.ds(i * G, G), :], yt[:, bass.ds(i * G, G), :]).then_inc(s_f6st, 16)
                sp.wait_ge(s_f6st, 16 * NG)

        s_st7, s_open7, s_free7, s_acc, s_accst, s_accfree, s_a0 = (sem(n) for n in (
            "indices7_staged", "gathers7_open", "rows7_free", "sums7_ready", "sums7_stored", "sums7_free", "sums7_zeroed"))
        s_got7 = [sem(f"rows7_{g}_gathered") for g in range(G)]
        acc_ctx = ExitStack()
        acc = sb(acc_ctx, "acc7", [P, G, G, D])
        with ExitStack() as st:
            src_s = sb(st, "src_s7", [P, G, G], I32)
            fr = sb(st, "fr", [P, G, G, D])
            block = st.enter_context(nc.Block())

            @block.scalar
            def _(act):
                with act.Fori(0, EITER) as i:
                    for g in range(G):
                        act.wait_ge(s_free7, i * G + g + 1)
                        act.sem_inc(carrier, 1)
                        nc.scalar.activation(src_s[:, g, :], src_i[:, bass.ds(i * G * G + g * G, G)], ACT.Copy).then_inc(s_st7, 1)

            @block.gpsimd
            def _(pool):
                with pool.Fori(0, EITER) as i:
                    for g in range(G):
                        pool.wait_ge(s_st7, i * G + g + 1)
                        pool.sem_inc(s_open7, 1)
                        for u in range(G):
                            nc.gpsimd.indirect_dma_start(out=fr[:, g, u, :], out_offset=None, in_=f_rows,
                                                         in_offset=bass.IndirectOffsetOnAxis(ap=src_s[:, g, u:u + 1], axis=0))\
                              .then_inc(s_got7[g], 16)

            @block.vector
            def _(v):
                dve_order.link(v, nc.vector.memset(acc[:, G - 1, G - 1, :], 0.0))
                v.sem_inc(s_free7, G)
                v.sem_inc(s_acc, 1)
                with v.Fori(0, EITER) as i:
                    dve_order.turn(i, G * (G - 1))
                    for g in range(G):
                        v.wait_ge(s_got7[g], (i + 1) * G * 16)
                        v.wait_ge(s_accfree, i * G + g + 1)
                        if g:
                            v.wait_ge(s_acc, i * G + g)
                        else:
                            v.wait_ge(s_acc, i * G + 1)
                        for u in range(G):
                            n = g * G + u - 1
                            ins = nc.vector.scalar_tensor_tensor(acc[:, g, u, :], acc[:, n // G % G, n % G, :],
                                                                 same[:, bass.ds(i * G * G + g * G + u, 1)], fr[:, g, u, :],
                                                                 ALU.mult, ALU.add)
                            if u < G - 1:
                                dve_order.link(v, ins)
                        ins.then_inc(s_acc, 1)
                        v.wait_ge(s_acc, i * G + g + 2)
                        v.sem_inc(s_free7, 1)
                dve_order.leave(EITER)

            @block.sync
            def _(sp):
                sp.sem_inc(s_accfree, G)
                to = run_rows.rearrange("(p j) d -> p j d", p=P)
                with sp.Fori(0, EITER) as i:
                    for g in range(G):
                        sp.wait_ge(s_acc, i * G + g + 2)
                        for a, b in HALVES:
                            sp.dma_start(to[a:b, bass.ds(i * G * G + g * G, G), :], acc[a:b, g]).then_inc(s_accst, 16)
                        sp.wait_ge(s_accst, (i * G + g + 1) * 32)
                        sp.sem_inc(s_accfree, 1)

        s_w8, s_b8, s_gr, s_bd, s_g8, s_tr8, s_t8, s_e8, s_ef, s_n8, s_tr8n, s_t8n, s_lg8, s_lg8e, s_cs = (sem(n) for n in (
            "w8_loaded", "bias8_loaded", "sums8_gathered", "joined8", "g8_ready", "sums8_turned", "sums8T_ready", "e8_done",
            "e8_fetched", "n8_ready", "n8_turned", "n8T_ready", "logits8_done", "logits8_kept", "carry_staged"))
        s_br = sem("router_bias_loaded")
        with ExitStack() as st:
            wg1 = sb(st, "wg1", [128, KD, D])
            wg2 = sb(st, "wg2", [128, KD, D])
            wr = sb(st, "wr", [128, KD, X])
            bn = sb(st, "bn", [P, D])
            gr = sb(st, "gr", [P, T, D])
            tile_s = sb(st, "tile_s", [P, G, D])
            tile_q = sb(st, "tile_q", [P, G, D])
            squares = sb(st, "squares", [P, G, D])
            tN = sb(st, "tN8", [128, G * KD, P])
            emb = sb(st, "emb", [P, G, D])
            sq = sb(st, "sq", [P, G])
            inv_norm = sb(st, "inv_norm", [P, G])
            carry_stage = sb(st, "carry_stage", [P, G, P])
            tS = sb(st, "tS8", [128, G * KD, P])
            tQ = sb(st, "tQ8", [128, G * KD, P])
            psT = ps(st, "psT8", [128, 3, 512])
            psO = ps(st, "psO8", [128, 3 * 512])
            psG = ps(st, "psG8", [128, 512])
            block = st.enter_context(nc.Block())

            @block.sync
            def _(sp):
                sp.dma_start(wg1[:], L1_gnn_W1.rearrange("(k p) d -> p k d", p=128)).then_inc(s_w8, 16)
                sp.dma_start(wg2[:], L1_gnn_W2.rearrange("(k p) d -> p k d", p=128)).then_inc(s_w8, 16)
                sp.dma_start(wr[:], L1_ffn_Wr.rearrange("(k p) d -> p k d", p=128)).then_inc(s_w8, 16)
                sp.dma_start(bn[:], L1_gnn_b.partition_broadcast(P)).then_inc(s_b8, 16)
                sp.dma_start(gate_b[:], L1_ffn_br.partition_broadcast(P)).then_inc(s_br, 16)
                sp.wait_ge(s_w8, 48)
                sp.wait_ge(s_b8, 16)
                sp.wait_ge(s_br, 16)

            @block.gpsimd
            def _(pool):
                for t in range(T):
                    nc.gpsimd.indirect_dma_start(out=gr[:, t, :], out_offset=None, in_=run_rows,
                                                 in_offset=bass.IndirectOffsetOnAxis(ap=end_i[:, t:t + 1], axis=0))\
                      .then_inc(s_gr, 16)

            @block.vector
            def _(v):
                link = lambda ins: dve_order.link(v, ins)
                one = lambda a, i, u: a[:, bass.ds(i * G + u, 1), :].rearrange("p a d -> p (a d)")

                def stage_carry(i):
                    tiles = bass.ds(i * G, G)
                    nc.vector.tensor_tensor(carry_stage[:], carry_on[:, tiles, :], carry_on[:, tiles, :], ALU.max).then_inc(s_cs, 1)

                def join(i):
                    tiles = bass.ds(i * G, G)
                    v.wait_ge(s_bd, i + 1)
                    for u in range(G):
                        last = nc.vector.scalar_tensor_tensor(one(gr, i, u), one(gr, i, u), has_in[:, bass.ds(i * G + u, 1)],
                                                              psO[0:P, u * D:(u + 1) * D], ALU.mult, ALU.add)
                    link(last)
                    link(nc.vector.tensor_tensor(gr[:, tiles, :], gr[:, tiles, :],
                                                 rsq_deg[:, tiles].unsqueeze(2).to_broadcast([P, G, D]), ALU.mult))
                    nc.vector.tensor_tensor(tile_s[:], n_sb[:, tiles, :], gr[:, tiles, :], ALU.add)
                    nc.vector.tensor_tensor(tile_q[:], n_sb[:, tiles, :], gr[:, tiles, :], ALU.mult).then_inc(s_g8, 1)

                def fetch_embedding(i):
                    v.wait_ge(s_e8, i + 1)
                    for u in range(G):
                        last = nc.vector.scalar_tensor_tensor(emb[:, u, :], psO[0:P, u * D:(u + 1) * D],
                                                              has_in[:, bass.ds(i * G + u, 1)], bn[:], ALU.mult, ALU.add)
                    link(last)
                    v.sem_inc(s_ef, 1)

                def finish(i):
                    tiles = bass.ds(i * G, G)
                    link(nc.vector.scalar_tensor_tensor(emb[:], emb[:], 0.01, emb[:], ALU.mult, ALU.max))
                    link(nc.vector.tensor_tensor(squares[:], emb[:], emb[:], ALU.mult))
                    link(nc.vector.tensor_reduce(sq[:], squares[:], AX.X, ALU.add))
                    link(nc.vector.tensor_scalar(sq[:], sq[:], 1e-24, None, ALU.max))
                    inverse_root(v, inv_norm[:], sq[:], root_t[:, 0:G])
                    link(nc.vector.tensor_tensor(emb[:], emb[:], inv_norm[:].unsqueeze(2).to_broadcast([P, G, D]), ALU.mult))
                    link(nc.vector.tensor_tensor(x_sb[:, tiles, :], x_sb[:, tiles, :], emb[:], ALU.add))
                    link(normalise(v, lambda u: one(x_sb, i, u), lambda u: tile_n[:, u, :]))
                    v.sem_inc(s_n8, 1)
                    link(normalise(v, lambda u: tile_n[:, u, :], lambda u: one(n_sb, i, u)))

                v.wait_ge(s_gr, 16 * T)
                v.wait_ge(s_b8, 16)
                v.sem_inc(s_ef, 1)
                stage_carry(0)
                join(0)
                with v.Fori(0, NG - 1) as i:
                    dve_order.turn(i, 50)
                    stage_carry(i + 1)
                    fetch_embedding(i)
                    join(i + 1)
                    v.wait_ge(s_tr8n, i + 1)
                    finish(i)
                dve_order.leave(NG - 1)
                fetch_embedding(NG - 1)
                v.wait_ge(s_tr8n, NG)
                finish(NG - 1)

            @block.scalar
            def _(act):
                def fetch_sums(i):
                    for n, to in enumerate((tS, tQ)):
                        act.wait_ge(s_tr8, i * 2 + n + 1)
                        fetch_turned(to, psT).then_inc(s_t8, 1)

                def keep_logits(i):
                    act.wait_ge(s_tr8n, i + 2)
                    fetch_turned(tN, psT).then_inc(s_t8n, 1)
                    act.wait_ge(s_lg8, i + 1)
                    act.sem_inc(carrier, 1)
                    nc.scalar.activation(logits[:, bass.ds(i * G, G), :].rearrange("p u e -> p (u e)"), psG[0:P, 0:G * X], ACT.Copy)\
                      .then_inc(s_lg8e, 1)

                fetch_sums(0)
                with act.Fori(0, NG - 1) as i:
                    fetch_sums(i + 1)
                    keep_logits(i)
                keep_logits(NG - 1)
                act.wait_ge(s_lg8e, NG)

            @block.tensor
            def _(pe):
                def products(i):
                    pe.wait_ge(s_cs, i + 1)
                    pe.wait_ge(s_ef, i + 1)
                    for u in range(G):
                        last = nc.tensor.matmul(psO[0:P, u * D:(u + 1) * D],
                                                carry_stage[:, u, :], acc[:, G - 1, G - 1, :], start=True, stop=True)
                    last.then_inc(s_bd, 1)
                    pe.wait_ge(s_g8, i + 1)
                    turn_tiles(pe, psT, tile_s).then_inc(s_tr8, 1)
                    pe.wait_ge(s_t8, i * 2 + 1)
                    turn_tiles(pe, psT, tile_q).then_inc(s_tr8, 1)
                    pe.wait_ge(s_t8, i * 2 + 2)
                    for u in range(G):
                        for n, (tt, w) in enumerate(((tS, wg1), (tQ, wg2))):
                            for k in range(KD):
                                last = nc.tensor.matmul(psO[0:P, u * D:(u + 1) * D], tt[:, u * KD + k, :], w[:, k, :],
                                                        start=(n == 0 and k == 0), stop=(n == 1 and k == KD - 1))
                    last.then_inc(s_e8, 1)

                def route_logits(i):
                    pe.wait_ge(s_n8, i + 1)
                    turn_tiles(pe, psT, tile_n).then_inc(s_tr8n, 1)
                    pe.wait_ge(s_t8n, i + 1)
                    for u in range(G):
                        for k in range(KD):
                            last = nc.tensor.matmul(psG[0:P, u * X:(u + 1) * X], tN[:, u * KD + k, :], wr[:, k, :],
                                                    start=(k == 0), stop=(k == KD - 1))
                    last.then_inc(s_lg8, 1)

                pe.sem_inc(s_tr8n, 1)
                pe.wait_ge(s_w8, 48)
                products(0)
                with pe.Fori(0, NG - 1) as i:
                    products(i + 1)
                    route_logits(i)
                route_logits(NG - 1)

        acc_ctx.close()
        route("r1", 2, NB1, xg1)
        experts("m1", NB1, xg1, yg1, L1_ffn_W1, L1_ffn_W2, L1_ffn_b2, True)

        s_y1, s_o11, s_out = [sem(f"y1_{n}_gathered") for n in range(2)], sem("o11_ready"), sem("out_stored")
        with ExitStack() as st:
            yt = sb(st, "yt11", [P, 2, T, D])
            block = st.enter_context(nc.Block())

            @block.gpsimd
            def _(pool):
                for k in range(2):
                    for t in range(T):
                        nc.gpsimd.indirect_dma_start(out=yt[:, k, t, :], out_offset=None, in_=yg1,
                                                     in_offset=bass.IndirectOffsetOnAxis(ap=slot_i[:, k, t:t + 1], axis=0))\
                          .then_inc(s_y1[k], 16)

            @block.vector
            def _(v):
                for k in range(2):
                    v.wait_ge(s_y1[k], 16 * T)
                    with v.Fori(0, NG) as i:
                        one = lambda a, u: a[:, bass.ds(i * G + u, 1), :].rearrange("p a d -> p (a d)")
                        for u in range(G):
                            last = nc.vector.scalar_tensor_tensor(
                                one(x_sb, u), yt[:, k, bass.ds(i * G + u, 1), :].rearrange("p a d -> p (a d)"),
                                gate[:, k, bass.ds(i * G + u, 1)], one(x_sb, u), ALU.mult, ALU.add)
                        last.then_inc(s_o11, 1)
                    v.wait_ge(s_o11, NG * (k + 1))

            @block.sync
            def _(sp):
                with sp.Fori(0, NG) as i:
                    sp.wait_ge(s_o11, NG + i + 1)
                    sp.dma_start(rows_of_tiles(out)[:, bass.ds(i * G, G), :], x_sb[:, bass.ds(i * G, G), :]).then_inc(s_out, 16)
                sp.wait_ge(s_out, 16 * NG)


_INS = ['x', 'src', 'dst', 'edge_attr_64', 'L0_gnn_Wq', 'L0_gnn_Wk', 'L0_gnn_Wv', 'L0_gnn_We', 'L0_gnn_Wo', 'L0_gnn_bo',
        'L0_ffn_W1', 'L0_ffn_b1', 'L0_ffn_Wg', 'L0_ffn_bg', 'L0_ffn_Wd', 'L0_ffn_bd', 'L1_gnn_W1', 'L1_gnn_W2', 'L1_gnn_b',
        'L1_ffn_Wr', 'L1_ffn_br', 'L1_ffn_ln_g', 'L1_ffn_ln_b', 'L1_ffn_W1', 'L1_ffn_b1', 'L1_ffn_W2', 'L1_ffn_b2']


def kernel(**inputs):
    import numpy as _np
    import concourse.bacc as _bacc
    from concourse import mybir as _mybir
    from concourse.bass_utils import run_bass_kernel_spmd as _run

    nc = _bacc.Bacc("TRN2", target_bir_lowering=False, num_devices=1)
    arrays, args = {}, []
    for name in _INS:
        a = _np.ascontiguousarray(inputs[name])
        arrays[f"in_{name}_dram"] = a
        args.append(nc.dram_tensor(f"in_{name}_dram", a.shape, _mybir.dt.from_np(a.dtype), kind="ExternalInput").ap())
    args.append(nc.dram_tensor("out_0_dram", (N_NODES, D), F32, kind="ExternalOutput").ap())
    build(nc, *args)
    r = _run(nc, [arrays], core_ids=[0])
    return r.results[0]["out_0_dram"]
```

```python
from contextlib import ExitStack

import concourse.bass as bass
from concourse import mybir

F32 = mybir.dt.float32
BF16 = mybir.dt.bfloat16
I32 = mybir.dt.int32
ALU = mybir.AluOpType
ACT = mybir.ActivationFunctionType
AX = mybir.AxisListType

N_NODES, D = 3125, 256
N_EDGES, ED = 53125, 64
H, DH = 8, 32
X, C = 8, 1024
P = 125
T = N_NODES // P
G = 5
NG = T // G
J = N_EDGES // P
EITER = J // (G * G)
NK = J // G
AHEAD = 3
R = 42
CB = -(-(R - 1 + P) // R)
CD = CB // 2
KB = -(-N_NODES // R) + CB - 1
KD, KC = D // 128, C // 128
S = 128
NB0 = (N_NODES + X * (S - 1)) // S
NB1 = (2 * N_NODES + X * (S - 1)) // S
BIG = 1.5e38
MAGIC = 1.5 * 2.0 ** 23
LN_EPS = 1e-5
HALVES = ((0, 112), (112, P))


def previous_use(u, n, per):
    return u - n if u >= n else max(v for v in range(per) if v % n == u % n) - per


class Order:

    def __init__(self, sem):
        self.sem, self.n, self.base = sem, 0, 0

    def link(self, eng, ins):
        ins.then_inc(self.sem, 1)
        self.n += 1
        eng.wait_ge(self.sem, self.base + self.n)

    def turn(self, i, per):
        self.base, self.start, self.per = i * per, self.n, per

    def leave(self, turns):
        assert self.n - self.start == self.per, (self.n - self.start, self.per)
        self.base, self.n = 0, self.start + turns * self.per


def build(nc, x, src, dst, edge_attr_64, L0_gnn_Wq, L0_gnn_Wk, L0_gnn_Wv, L0_gnn_We, L0_gnn_Wo, L0_gnn_bo,
          L0_ffn_W1, L0_ffn_b1, L0_ffn_Wg, L0_ffn_bg, L0_ffn_Wd, L0_ffn_bd, L1_gnn_W1, L1_gnn_W2, L1_gnn_b,
          L1_ffn_Wr, L1_ffn_br, L1_ffn_ln_g, L1_ffn_ln_b, L1_ffn_W1, L1_ffn_b1, L1_ffn_W2, L1_ffn_b2, out):
    top = ExitStack()

    def sb(ctx, name, shape, dt=F32):
        return ctx.enter_context(nc.sbuf_tensor(name, shape, dt))

    def ps(ctx, name, shape, dt=F32):
        return ctx.enter_context(nc.psum_tensor(name, shape, dt))

    def sem(name):
        return top.enter_context(nc.semaphore(name))

    def dram(name, shape, dt=F32):
        return nc.dram_tensor(name, shape, dt, kind="Internal").ap()

    def rows_of_tiles(a):
        return a.rearrange("(t p) d -> p t d", p=P)

    with top:
        q_rows = dram("q_rows", [N_NODES, D])
        k_rows = dram("k_rows", [KB * R, 3 * D], BF16)
        dst_rows = dram("dst_rows", [P, J])
        ranks = dram("ranks", [N_EDGES])
        locals_ = dram("locals_", [N_EDGES + G * P], BF16)
        bases = dram("bases", [1, J], I32)
        dot_rows = dram("dot_rows", [H, N_EDGES])
        expsum_rows = dram("expsum_rows", [N_EDGES, H])
        f_rows = dram("f_rows", [N_NODES, D])
        run_rows = dram("run_rows", [N_EDGES, D])
        tok0 = dram("tok0", [N_NODES, D])
        tok1 = dram("tok1", [N_NODES, D])
        y0 = dram("y0", [1 + N_NODES + 2 * S, D])
        y1 = dram("y1", [1 + 2 * N_NODES + 2 * S, D])

        n_sb = sb(top, "n_sb", [P, T, D])
        ident = sb(top, "ident", [128, 128])
        iota_row = sb(top, "iota_row", [P, P])
        before = sb(top, "before", [P, P])
        ones = sb(top, "ones", [128, 128])
        rank8 = sb(top, "rank8", [P, T, X])
        src_i = sb(top, "src_i", [P, J], I32)
        dst_i = sb(top, "dst_i", [P, J], I32)
        dst_f = sb(top, "dst_f", [P, J])
        same = sb(top, "same", [P, J])
        counts = sb(top, "counts", [P, 2, T])
        node_f = sb(top, "node_f", [P, T])
        rank_p = sb(top, "rank_p", [3 * R, CB])
        has_in = sb(top, "has_in", [P, T])
        rsq_deg = sb(top, "rsq_deg", [P, T])
        end_i = sb(top, "end_i", [P, T], I32)
        src_t = sb(top, "src_t", [P, NK + AHEAD, G], I32)
        base_i = sb(top, "base_i", [1, J], I32)
        logits = sb(top, "logits", [P, T, X])
        gate_b = sb(top, "gate_b", [P, X])
        gate = sb(top, "gate", [P, 2, T])
        from_i = sb(top, "from_i", [S, NB1 + 2], I32)
        to_i = sb(top, "to_i", [S, NB1], I32)
        block_e = sb(top, "block_e", [1, NB1], I32)
        stats = sb(top, "stats", [P, G, 6])
        mean_var = sb(top, "mean_var", [P, G, 2])
        variance = sb(top, "variance", [P, G])
        rstd = sb(top, "rstd", [P, G])
        root_t = sb(top, "root_t", [P, T])
        tile_n = sb(top, "tile_n", [P, G, D])
        exp_par = sb(top, "exp_par", [128, X, KC + 2 * KD])
        b1_0 = sb(top, "b1_0", [128, KC])

        dve_order = Order(sem("dve_order"))
        act_order = Order(sem("act_order"))
        pool_order = Order(sem("pool_order"))
        s_group = [sem(f"group{n}_gathered") for n in range(NG)]
        GATHER = 16 * G
        carrier = sem("carrier")

        def inverse_root(v, y, a, t):
            link = lambda ins: dve_order.link(v, ins)
            link(nc.vector.tensor_scalar(y.bitcast(I32), a.bitcast(I32), 1, None, ALU.logical_shift_right))
            link(nc.vector.tensor_scalar(y.bitcast(I32), y.bitcast(I32), -1.0, float(0x5F3759DF), ALU.mult, ALU.add))
            for _ in range(3):
                link(nc.vector.tensor_tensor(t, y, y, ALU.mult))
                link(nc.vector.scalar_tensor_tensor(t, t, -0.5, a, ALU.mult, ALU.mult))
                link(nc.vector.scalar_tensor_tensor(y, t, 1.5, y, ALU.add, ALU.mult))

        def normalise(v, src_tile, dst_tile):
            v.sem_inc(carrier, 1)
            for u in range(G):
                last = nc.vector.bn_stats(stats[:, u, :], src_tile(u))
            dve_order.link(v, last)
            v.sem_inc(carrier, 1)
            for u in range(G):
                last = nc.vector.bn_aggr(mean_var[:, u, :], stats[:, u, :])
            dve_order.link(v, last)
            dve_order.link(v, nc.vector.tensor_scalar(variance[:], mean_var[:, :, 1], LN_EPS, None, ALU.add))
            inverse_root(v, rstd[:], variance[:], root_t[:, 0:G])
            for u in range(G):
                last = nc.vector.tensor_scalar(dst_tile(u), src_tile(u), mean_var[:, u, 0:1], rstd[:, u:u + 1],
                                               ALU.subtract, ALU.mult)
            return last

        def turn_tiles(pe, psum, tiles):
            for n in range(G * KD):
                u, k = n // KD, n % KD
                last = nc.tensor.transpose(psum[:, n // 4, (n % 4) * P:(n % 4 + 1) * P],
                                           tiles[:, u, k * 128:(k + 1) * 128], ident[0:P, 0:P])
            return last

        def fetch_turned(tT, psum):
            for b in range(3):
                n = min(4, G * KD - 4 * b)
                last = nc.scalar.activation(tT[:, 4 * b:4 * b + n, :].rearrange("p n c -> p (n c)"),
                                            psum[:, b, 0:n * P], ACT.Copy)
            return last

        sems0 = []

        def sem0(name):
            sems0.append(nc.alloc_semaphore(name=name))
            return sems0[-1]

        s_dst, s_src, s_srcp, s_x0, s_xr, s_w0, s_par, s_zero = (sem0(n) for n in (
            "dst_loaded", "src_loaded", "src_by_partition", "x0_loaded", "x_rest_loaded", "qkv_w_loaded", "par_loaded", "zeros_made"))
        s_const, s_par_turned, s_par_kept = sem0("consts_made"), sem0("par_turned"), sem0("par_kept")
        s_n0, s_tr0, s_t0, s_qk0, s_v0 = (sem0(n) for n in ("n0_ready", "tr0_done", "t0_ready", "qk0_done", "v0_done"))
        s_qk0e, s_v0e, s_qst = sem0("qk0_fetched"), sem0("v0_fetched"), sem0("q_stored")
        s_run, s_runpre, s_rank, s_rankst, s_rankd, s_local, s_localst, s_base = (sem0(n) for n in (
            "runs_counted", "run_prefix_done", "ranks_made", "ranks_stored", "ranks_by_tile", "locals_made", "locals_stored",
            "bases_loaded"))
        s_srcf, s_srcT, s_srck, s_dstf, s_dstst, s_lasts, s_lastsB, s_part, s_end, s_shift, s_deg, s_degpre, s_pos = (sem0(n) for n in (
            "src_float", "src_turned", "src_kept", "dst_float", "dst_stored", "lasts_made", "lasts_spread", "parts_found", "ends_found",
            "ends_shifted", "degrees_known", "degree_prefix_done", "k_places"))
        s_rowu, s_kst = sem0("dst_rows_used"), sem("k_stored")
        s_khi, s_krem, s_kmid, s_klo, s_tail = (sem0(n) for n in ("k_hi", "k_rest", "k_mid", "k_lo", "tail_zeroed"))
        with ExitStack() as st:
            x0 = sb(st, "x0", [P, T, D])
            w_qkv = sb(st, "w_qkv", [128, KD, 3 * D])
            q_sb = sb(st, "q_sb", [P, T, D])
            k_f = sb(st, "k_f", [P, G, D])
            k_r = sb(st, "k_r", [P, G, D])
            k3 = sb(st, "k3", [P, T, 3, D], BF16)
            tT = sb(st, "tT0", [128, G * KD, P])
            zeros = sb(st, "zeros", [128, 3 * D // 2])
            par = sb(st, "par", [X * KC, 4, 128])
            prev_i = sb(st, "prev_i", [P, 1], I32)
            prev_f = sb(st, "prev_f", [P, 1])
            begins = sb(st, "begins", [P, J])
            rank_e = sb(st, "rank_e", [P, J])
            run_pre = sb(st, "run_pre", [P, 1])
            rank_g = sb(st, "rank_g", [NK, G * P])
            base_f = sb(st, "base_f", [NK, G])
            base_g = sb(st, "base_g", [NK, G], I32)
            base_p = sb(st, "base_p", [NK, G])
            local_g = sb(st, "local_g", [NK, G * P], BF16)
            src_g = sb(st, "src_g", [NK, G * P], I32)
            src_gf = sb(st, "src_gf", [NK, G * P])
            last_d = sb(st, "last_d", [P, P])
            lasts = sb(st, "lasts", [P, P])
            part_n = sb(st, "part_n", [P, T])
            part_i = sb(st, "part_i", [P, T], I32)
            rows = sb(st, "rows", [P, NG - 1, G, J])
            end_f = sb(st, "end_f", [P, T])
            end_p = sb(st, "end_p", [P, T])
            shift = sb(st, "shift", [P, P])
            wrap = sb(st, "wrap", [P, P])
            tot = sb(st, "tot0", [P, T])
            pre = sb(st, "pre0", [P, T])
            one_row = sb(st, "one_row0", [P, T])
            distinct = sb(st, "distinct", [P, 1])
            idle = sb(st, "idle", [P, T])
            pos_i = sb(st, "pos_i", [P, T], I32)
            psT = ps(st, "psT0", [128, 3, 512])
            psQ = ps(st, "psQ0", [128, 2, 512])
            psV = ps(st, "psV0", [128, 2, 512])
            psP = ps(st, "psP0", [128, 512])
            par_rows = (X * KC, X * KD, X * KD, KC)
            par_at = (0, X * KC, X * (KC + KD), X * (KC + 2 * KD))
            block = st.enter_context(nc.Block())
            by_tile = lambda a: a[:].rearrange("k (u q) -> k u q", q=P)

            @block.sync
            def _(sp):
                dst_p = dst.rearrange("(p j) -> p j", p=P)
                sp.dma_start(dst_i[:], dst_p).then_inc(s_dst, 16)
                sp.wait_ge(s_const, 1)
                sp.dma_start(prev_i[1:P, :], dst_p[0:P - 1, J - 1:J], allow_slow_non_contiguous=True).then_inc(s_dst, 16)

                def load_x(i, loaded):
                    for a, b in HALVES:
                        sp.dma_start(x0[a:b, i * G:(i + 1) * G, :], rows_of_tiles(x)[a:b, i * G:(i + 1) * G, :]).then_inc(loaded, 16)

                load_x(0, s_x0)
                for n, w in enumerate((L0_gnn_Wq, L0_gnn_Wk, L0_gnn_Wv)):
                    sp.dma_start(w_qkv[:, :, n * D:(n + 1) * D], w.rearrange("(k p) d -> p k d", p=128)).then_inc(s_w0, 16)
                sp.wait_ge(s_dstf, 1)
                sp.dma_start(dst_rows, dst_f[:]).then_inc(s_dstst, 16)
                sp.dma_start(src_g[:], src.rearrange("(k e) -> k e", k=NK)).then_inc(s_src, 16)
                for i in range(1, NG):
                    load_x(i, s_xr)
                sp.dma_start(src_i[:], src.rearrange("(p j) -> p j", p=P)).then_inc(s_srcp, 16)
                sp.wait_ge(s_rank, 1)
                sp.dma_start(ranks.rearrange("(p j) -> p j", p=P), rank_e[:]).then_inc(s_rankst, 16)
                sp.wait_ge(s_rankst, 16)
                sp.dma_start(rank_g[:], ranks.rearrange("(k e) -> k e", k=NK)).then_inc(s_rankd, 16)
                sp.wait_ge(s_local, 2)
                sp.dma_start(locals_[0:N_EDGES].rearrange("(k e) -> k e", k=NK), local_g[:]).then_inc(s_localst, 16)
                sp.dma_start(locals_[N_EDGES:N_EDGES + G * P].rearrange("(k e) -> k e", k=1), local_g[NK - 1:NK, :])\
                  .then_inc(s_localst, 16)
                sp.dma_start(bases.rearrange("a (k u) -> (a k) u", u=G), base_g[:]).then_inc(s_localst, 16)
                sp.wait_ge(s_localst, 48)
                sp.dma_start(base_i[:], bases).then_inc(s_base, 16)
                with sp.Fori(0, NG) as i:
                    sp.wait_ge(s_qk0e, (i + 1) * G + G)
                    for a, b in HALVES:
                        sp.dma_start(rows_of_tiles(q_rows)[a:b, bass.ds(i * G, G), :],
                                     q_sb[a:b, bass.ds(i * G, G), :]).then_inc(s_qst, 16)
                sp.wait_ge(s_qst, 32 * NG)
                sp.wait_ge(s_base, 16)
                sp.wait_ge(s_srcp, 16)

            @block.gpsimd
            def _(pool):
                nc.gpsimd.memset(prev_i[:], -1).then_inc(s_const, 1)
                nc.gpsimd.memset(ones[:], 1.0).then_inc(s_const, 1)
                pool_order.link(pool, nc.gpsimd.memset(ident[:], 0.0))
                nc.gpsimd.affine_select(out=ident[:], in_=ident[:], compare_op=ALU.not_equal, fill=1.0, base=0,
                                        pattern=[[-1, 128]], channel_multiplier=1).then_inc(s_const, 1)
                pool_order.link(pool, nc.gpsimd.memset(before[:], 1.0))
                nc.gpsimd.affine_select(out=before[:], in_=before[:], compare_op=ALU.is_gt, fill=0.0, base=0,
                                        pattern=[[1, P]], channel_multiplier=-1).then_inc(s_const, 1)
                nc.gpsimd.iota(iota_row[:], pattern=[[1, P]], base=0, channel_multiplier=0,
                               allow_small_or_imprecise_dtypes=True).then_inc(s_const, 1)
                nc.gpsimd.iota(node_f[:], pattern=[[P, T]], base=0, channel_multiplier=1,
                               allow_small_or_imprecise_dtypes=True).then_inc(s_const, 1)
                nc.gpsimd.iota(rank_p[:], pattern=[[R, CB]], base=0, channel_multiplier=1,
                               allow_small_or_imprecise_dtypes=True).then_inc(s_const, 1)
                for m, (step, base) in ((shift, (-1, 1)), (wrap, (-2 * P, 1 - P))):
                    pool_order.link(pool, nc.gpsimd.memset(m[:], 0.0))
                    nc.gpsimd.affine_select(out=m[:], in_=m[:], compare_op=ALU.not_equal, fill=1.0, base=base,
                                            pattern=[[step, P]], channel_multiplier=1).then_inc(s_const, 1)
                nc.gpsimd.memset(zeros[:], 0.0).then_inc(s_zero, 1)
                nc.gpsimd.iota(rank8[:], pattern=[[0, T], [-1, X]], base=X, channel_multiplier=0,
                               allow_small_or_imprecise_dtypes=True).then_inc(s_const, 1)
                pool.wait_ge(s_part, 1)
                pool.wait_ge(s_dstst, 16)
                for t in range(T):
                    if t == T - G:
                        pool.wait_ge(s_rowu, 1)
                    nc.gpsimd.indirect_dma_start(out=rows[:, t // G % (NG - 1), t % G, :], out_offset=None, in_=dst_rows,
                                                 in_offset=bass.IndirectOffsetOnAxis(ap=part_i[:, t:t + 1], axis=0))\
                      .then_inc(s_group[t // G], 16)
                pool.wait_ge(s_pos, 1)
                for t in range(T):
                    if t % G == 0:
                        pool.wait_ge(s_klo, t // G + 2)
                    nc.gpsimd.indirect_dma_start(out=k_rows, out_offset=bass.IndirectOffsetOnAxis(ap=pos_i[:, t:t + 1], axis=0),
                                                 in_=k3[:, t].rearrange("p c d -> p (c d)"), in_offset=None).then_inc(s_kst, 16)
                pool.wait_ge(s_kst, 16 * T)

            @block.scalar
            def _(act):
                for n, (a, r) in enumerate(((L1_ffn_b1, "e (c f) -> (e c) f"), (L1_ffn_ln_g, "e (c f) -> (e c) f"),
                                            (L1_ffn_ln_b, "e (c f) -> (e c) f"), (L0_ffn_b1, "(c f) -> c f"))):
                    act.dma_start(par[0:par_rows[n], n, :], a.rearrange(r, f=128)).then_inc(s_par, 16)
                act.wait_ge(s_zero, 1)
                for a in range(N_NODES, KB * R, 128):
                    n = min(128, KB * R - a)
                    act.dma_start(k_rows[a:a + n, :], zeros[0:n, :].bitcast(BF16)).then_inc(s_tail, 16)
                act.sem_inc(s_qk0e, G)
                act.sem_inc(s_v0e, G)

                def fetch_normed(i):
                    act.wait_ge(s_tr0, i + 1)
                    fetch_turned(tT, psT).then_inc(s_t0, 1)

                def fetch_products(i):
                    act.wait_ge(s_krem, i + 1)
                    for u in range(G):
                        act.wait_ge(s_qk0, i * G + u + 1)
                        act.sem_inc(carrier, 1)
                        nc.scalar.activation(q_sb[:, bass.ds(i * G + u, 1), :].rearrange("p a d -> p (a d)"),
                                             psQ[0:P, u % 2, 0:D], ACT.Copy, scale=DH ** -0.5)
                        nc.scalar.activation(k_f[:, u, :], psQ[0:P, u % 2, D:2 * D], ACT.Copy).then_inc(s_qk0e, 1)
                    act.wait_ge(s_qk0e, (i + 1) * G + G)
                    act.sem_inc(carrier, 1)
                    nc.scalar.activation(k3[:, bass.ds(i * G, G), 0, :], k_f[:], ACT.Copy).then_inc(s_khi, 1)
                    for u in range(G):
                        act.wait_ge(s_v0, i * G + u + 1)
                        act.sem_inc(carrier, 1)
                        nc.scalar.activation(n_sb[:, bass.ds(i * G + u, 1), :].rearrange("p a d -> p (a d)"),
                                             psV[0:P, u % 2, 0:D], ACT.Copy).then_inc(s_v0e, 1)

                def middle_part(i):
                    act.wait_ge(s_krem, i + 2)
                    act.sem_inc(carrier, 1)
                    nc.scalar.activation(k3[:, bass.ds(i * G, G), 1, :], k_r[:], ACT.Copy).then_inc(s_kmid, 1)

                fetch_normed(0)
                with act.Fori(0, NG - 1) as i:
                    fetch_products(i)
                    fetch_normed(i + 1)
                    middle_part(i)
                fetch_products(NG - 1)
                middle_part(NG - 1)
                act.wait_ge(s_tail, 16 * -(-(KB * R - N_NODES) // 128))

            @block.tensor
            def _(pe):
                pe.wait_ge(s_const, 10)
                pe.wait_ge(s_run, 1)
                nc.tensor.matmul(psV[0:P, 0, 0:1], before[:], rank_e[:, J - 1:J], start=True, stop=True).then_inc(s_runpre, 1)
                pe.wait_ge(s_par, 64)
                for n in range(4):
                    last = nc.tensor.transpose(psP[:, par_at[n]:par_at[n] + par_rows[n]], par[0:par_rows[n], n, :],
                                               ident[0:par_rows[n], 0:par_rows[n]])
                last.then_inc(s_par_turned, 1)
                pe.wait_ge(s_lasts, 1)
                pe.wait_ge(s_par_kept, 1)
                nc.tensor.matmul(psP[0:P, 0:P], ones[0:P, 0:P], last_d[:], start=True, stop=True).then_inc(s_lastsB, 1)
                pe.wait_ge(s_w0, 48)
                pe.wait_ge(s_rank, 1)

                def products(i):
                    pe.wait_ge(s_n0, i + 1)
                    turn_tiles(pe, psT, tile_n).then_inc(s_tr0, 1)
                    pe.wait_ge(s_t0, i + 1)
                    for u in range(G):
                        pe.wait_ge(s_qk0e, i * G + previous_use(u, 2, G) + 1 + G)
                        for k in range(KD):
                            last = nc.tensor.matmul(psQ[0:P, u % 2, :], tT[:, u * KD + k, :], w_qkv[:, k, 0:2 * D],
                                                    start=(k == 0), stop=(k == KD - 1))
                        last.then_inc(s_qk0, 1)
                    for u in range(G):
                        pe.wait_ge(s_v0e, i * G + previous_use(u, 2, G) + 1 + G)
                        for k in range(KD):
                            last = nc.tensor.matmul(psV[0:P, u % 2, 0:D], tT[:, u * KD + k, :], w_qkv[:, k, 2 * D:3 * D],
                                                    start=(k == 0), stop=(k == KD - 1))
                        last.then_inc(s_v0, 1)

                products(0)
                pe.wait_ge(s_srcf, 1)
                pe.wait_ge(s_part, 1)
                for u in range(G):
                    last = nc.tensor.transpose(psP[0:P, u * NK:(u + 1) * NK], src_gf[:, u * P:(u + 1) * P], ident[0:NK, 0:NK])
                last.then_inc(s_srcT, 1)
                products(1)
                pe.wait_ge(s_end, 1)
                pe.wait_ge(s_srck, 1)
                nc.tensor.matmul(psP[0:P, 0:T], shift[:], end_f[:], start=True, stop=True)
                nc.tensor.matmul(psP[0:P, T:2 * T - 1], wrap[:], end_f[:, 0:T - 1], start=True, stop=True).then_inc(s_shift, 1)
                products(2)
                pe.wait_ge(s_deg, 1)
                nc.tensor.matmul(psP[0:P, 0:T], before[:], has_in[:], start=True, stop=True)
                nc.tensor.matmul(psP[0:P, T:2 * T], ones[0:P, 0:P], has_in[:], start=True, stop=True).then_inc(s_degpre, 1)
                with pe.Fori(3, NG) as i:
                    products(i)

            @block.vector
            def _(v):
                link = lambda ins: dve_order.link(v, ins)

                def norm_group(i):
                    if i:
                        v.wait_ge(s_tr0, i)
                    normalise(v, lambda u: x0[:, i * G + u, :], lambda u: tile_n[:, u, :]).then_inc(s_n0, 1)

                def second_part(i):
                    v.wait_ge(s_khi, i + 1)
                    v.wait_ge(s_klo, i + 1)
                    nc.vector.tensor_tensor(k_r[:], k_f[:], k3[:, i * G:(i + 1) * G, 0, :], ALU.subtract).then_inc(s_krem, 1)

                def third_part(i):
                    v.wait_ge(s_kmid, i + 1)
                    v.wait_ge(s_krem, i + 2)
                    nc.vector.tensor_tensor(k3[:, i * G:(i + 1) * G, 2, :], k_r[:], k3[:, i * G:(i + 1) * G, 1, :], ALU.subtract)\
                      .then_inc(s_klo, 1)

                def ends():
                    for i in range(NG):
                        v.wait_ge(s_group[i], GATHER)
                        for u in range(G):
                            t = i * G + u
                            link(nc.vector.tensor_scalar(rows[:, i % (NG - 1), u, :], rows[:, i % (NG - 1), u, :], node_f[:, t:t + 1], 0.0, ALU.is_le, ALU.add,
                                                         accum_out=end_f[:, t:t + 1]))
                        if i == 0:
                            v.sem_inc(s_rowu, 1)
                    nc.vector.scalar_tensor_tensor(end_f[:], part_n[:], float(J), end_f[:], ALU.mult, ALU.add).then_inc(s_end, 1)

                def degrees():
                    v.wait_ge(s_shift, 1)
                    link(nc.vector.tensor_copy(end_p[:], psP[0:P, 0:T]))
                    link(nc.vector.tensor_tensor(end_p[:, 1:T], end_p[:, 1:T], psP[0:P, T:2 * T - 1], ALU.add))
                    nc.vector.tensor_tensor(has_in[:], end_f[:], end_p[:], ALU.is_gt).then_inc(s_deg, 1)
                    link(nc.vector.tensor_scalar(end_f[:], end_f[:], -1.0, 0.0, ALU.add, ALU.max))
                    nc.vector.tensor_copy(end_i[:], end_f[:])

                def places():
                    v.wait_ge(s_degpre, 1)
                    link(nc.vector.tensor_copy(tot[:], psP[0:P, T:2 * T]))
                    link(nc.vector.tensor_tensor_scan(pre[:], one_row[:], tot[:], 0.0, ALU.mult, ALU.add))
                    link(nc.vector.tensor_copy(distinct[:], pre[:, T - 1:T]))
                    link(nc.vector.tensor_tensor(pre[:], pre[:], tot[:], ALU.subtract))
                    link(nc.vector.tensor_tensor(pre[:], pre[:], psP[0:P, 0:T], ALU.add))
                    link(nc.vector.tensor_tensor(idle[:], node_f[:], pre[:], ALU.subtract))
                    link(nc.vector.tensor_scalar(idle[:], idle[:], distinct[:, 0:1], None, ALU.add))
                    link(nc.vector.tensor_tensor(pre[:], pre[:], idle[:], ALU.subtract))
                    link(nc.vector.tensor_tensor(pre[:], pre[:], has_in[:], ALU.mult))
                    link(nc.vector.tensor_tensor(idle[:], idle[:], pre[:], ALU.add))
                    nc.vector.tensor_copy(pos_i[:], idle[:]).then_inc(s_pos, 1)

                v.sem_inc(s_krem, 1)
                v.sem_inc(s_klo, 1)
                v.wait_ge(s_dst, 32)
                nc.vector.memset(same[:, 0:1], 0.0)
                nc.vector.memset(one_row[:], 1.0)
                nc.vector.tensor_copy(prev_f[:], prev_i[:])
                nc.vector.tensor_copy(dst_f[:], dst_i[:]).then_inc(s_dstf, 1)
                v.wait_ge(s_dstf, 1)
                link(nc.vector.tensor_tensor(same[:, 1:J], dst_f[:, 1:J], dst_f[:, 0:J - 1], ALU.is_equal))
                nc.vector.tensor_tensor(begins[:, 0:1], dst_f[:, 0:1], prev_f[:], ALU.not_equal)
                link(nc.vector.tensor_scalar(begins[:, 1:J], same[:, 1:J], -1.0, 1.0, ALU.mult, ALU.add))
                nc.vector.tensor_tensor_scan(rank_e[:], begins[:], begins[:], 0.0, ALU.add, ALU.max).then_inc(s_run, 1)
                v.wait_ge(s_const, 10)
                nc.vector.tensor_scalar(last_d[:], ident[0:P, 0:P], dst_f[:, J - 1:J], None, ALU.mult).then_inc(s_lasts, 1)
                v.wait_ge(s_runpre, 1)
                link(nc.vector.tensor_copy(run_pre[:], psV[0:P, 0, 0:1]))
                nc.vector.tensor_scalar(rank_e[:], rank_e[:], run_pre[:, 0:1], -1.0, ALU.add, ALU.add).then_inc(s_rank, 1)
                v.wait_ge(s_par_turned, 1)
                for n, (a, b) in enumerate(((0, KC), (KC, KC + KD), (KC + KD, KC + 2 * KD))):
                    nc.vector.tensor_copy(exp_par[:, :, a:b], psP[:, par_at[n]:par_at[n] + par_rows[n]]
                                          .rearrange("p (e c) -> p e c", e=X))
                nc.vector.tensor_copy(b1_0[:], psP[:, par_at[3]:par_at[3] + KC]).then_inc(s_par_kept, 1)
                v.wait_ge(s_x0, 32)
                norm_group(0)
                v.wait_ge(s_lastsB, 1)
                link(nc.vector.tensor_copy(lasts[:], psP[0:P, 0:P]))
                for t in range(T):
                    link(nc.vector.tensor_scalar(last_d[:], lasts[:], node_f[:, t:t + 1], 0.0, ALU.is_le, ALU.add,
                                                 accum_out=part_n[:, t:t + 1]))
                link(nc.vector.tensor_scalar(part_n[:], part_n[:], float(P - 1), None, ALU.min))
                nc.vector.tensor_copy(part_i[:], part_n[:]).then_inc(s_part, 1)
                v.wait_ge(s_src, 16)
                nc.vector.tensor_copy(src_gf[:], src_g[:]).then_inc(s_srcf, 1)
                v.wait_ge(s_rankd, 16)
                link(nc.vector.tensor_scalar(base_f[:], by_tile(rank_g)[:, :, 0], -(R - 1) / 2, 1.0 / R, ALU.add, ALU.mult))
                link(nc.vector.tensor_scalar(base_f[:], base_f[:], MAGIC, None, ALU.add))
                link(nc.vector.tensor_scalar(base_f[:], base_f[:], MAGIC, None, ALU.subtract))
                nc.vector.tensor_copy(base_g[:], base_f[:]).then_inc(s_local, 1)
                link(nc.vector.tensor_scalar(base_p[:], base_f[:], float(R), None, ALU.mult))
                nc.vector.tensor_tensor(by_tile(local_g), by_tile(rank_g), base_p[:].unsqueeze(2).to_broadcast([NK, G, P]),
                                        ALU.subtract).then_inc(s_local, 1)
                v.wait_ge(s_xr, 32 * (NG - 1))
                for i in range(NG):
                    if i + 1 < NG:
                        norm_group(i + 1)
                    second_part(i)
                    if i == 0:
                        v.wait_ge(s_srcT, 1)
                        nc.vector.memset(src_t[:, NK:], 0)
                        nc.vector.tensor_copy(src_t[:, 0:NK], psP[0:P, 0:J].rearrange("p (u k) -> p k u", u=G)).then_inc(s_srck, 1)
                    elif i == 1:
                        ends()
                    elif i == 2:
                        degrees()
                    elif i == 3:
                        places()
                    third_part(i)

        score = sb(top, "score", [P, H, J])
        s_webd, s_ea = sem("we_loaded"), [sem(f"ea{g}_loaded") for g in range(G)]
        s_staged, s_open = sem("indices_staged"), sem("gathers_open")
        s_got = [sem(f"rows{g}_gathered") for g in range(G)]
        s_loc = [sem(f"locals{g}_loaded") for g in range(G)]
        s_kp = [sem(f"k_parts{n}_loaded") for n in range(3)]
        s_free, s_ead, s_eae, s_es, s_esk = (sem(n) for n in ("rows_free", "ea_turned", "ea_fetched", "edge_score_done",
                                                       "edge_score_kept"))
        s_oh, s_ohu, s_cnt, s_webz, s_cntz = (sem(n) for n in ("onehots_made", "onehots_used", "counts_done", "we_zeroed",
                                                       "zero_lhs"))
        s_kt, s_kabs, s_kta, s_kx, s_kfree, s_dT, s_dk, s_dst1 = (sem(n) for n in (
            "k_onehots", "k_distances", "k_onehots_act", "k_expanded", "k_banks_free", "dots_turned", "dots_kept", "dots_stored"))
        with ExitStack() as st:
            we2 = sb(st, "we2", [2 * ED, 2 * H])
            src_s = sb(st, "src_s", [P, G, G], I32)
            qr = sb(st, "qr", [P, G, G, D])
            kp = sb(st, "kp", [3 * R, KB, D], BF16)
            loc = sb(st, "loc", [3 * R, G, G * P], BF16)
            k_at = sb(st, "k_at", [3 * R, CB])
            k_neg = sb(st, "k_neg", [3 * R, CB])
            part_of = sb(st, "part_of", [3 * R, 2])
            dist = sb(st, "dist", [3 * R, CB - CD, G * P], BF16)
            oh_k = sb(st, "oh_k", [3 * R, 3, CB, G * P], BF16)
            ea = sb(st, "ea", [P, G, G * ED])
            eaT = sb(st, "eaT", [128, G, 3 * P])
            dots = sb(st, "dots", [P, H, J])
            lo = sb(st, "lo", [P, J])
            hi = sb(st, "hi", [P, J])
            src_f = sb(st, "src_f", [P, J])
            oh_lo = sb(st, "oh_lo", [P, G, G, P], BF16)
            oh_hi = sb(st, "oh_hi", [P, G, G, T], BF16)
            zb = sb(st, "zb", [P, P], BF16)
            psE = ps(st, "psE1", [128, 2, 512])
            psS = ps(st, "psS1", [128, 2, 512])
            psC = ps(st, "psC1", [128, 512])
            psK = ps(st, "psK1", [128, 3, 512])
            block = st.enter_context(nc.Block())
            eav = edge_attr_64.rearrange("(p j) f -> p (j f)", p=P)
            K_GROUPS = (0, 2, 3)
            K_ENDS = [min(KB, g * G * P // R + CB) for g in K_GROUPS[1:]] + [KB]
            K_SLOT = (0, 1, 0, 1, 2)
            BANKS = ((0, 2), (2, 4), (4, G))
            CH = 112
            CHUNKS = [(a, min(a + CH, J)) for a in range(0, J, CH)]
            turned = qr[:].rearrange("p g u d -> p (g u d)")[:, 0:H * len(CHUNKS) * P]\
                          .rearrange("p (h c q) -> p h c q", h=H, c=len(CHUNKS))

            def load_k(eng, n):
                a, b = (K_ENDS[n - 1] if n else 0), K_ENDS[n]
                for c in range(3):
                    eng.dma_start(kp[c * R:(c + 1) * R, a:b, :],
                                  k_rows[a * R:b * R, c * D:(c + 1) * D].rearrange("(b r) d -> r b d", r=R)).then_inc(s_kp[n], 16)

            @block.sync
            def _(sp):
                sp.dma_start(loc[:, 0, :], locals_[0:G * P].partition_broadcast(3 * R)).then_inc(s_loc[0], 16)
                load_k(sp, 0)
                with sp.Fori(0, EITER) as i:
                    for g in range(G):
                        sp.wait_ge(s_ead, i * G + g + 1)
                        for a, b in HALVES:
                            sp.dma_start(ea[a:b, g, :], eav[a:b, bass.ds((i * G * G + g * G) * ED, G * ED)])\
                              .then_inc(s_ea[g], 16)
                        sp.wait_ge(s_kt, i * G + g + 2)
                        sp.wait_ge(s_kta, i * G + g + 2)
                        sp.dma_start(loc[:, (g + 1) % G, :], locals_[bass.ds((i * G + g + 1) * G * P, G * P)]
                                     .partition_broadcast(3 * R)).then_inc(s_loc[(g + 1) % G], 16)
                for part in range(2):
                    heads = slice(part * H // 2, (part + 1) * H // 2)
                    sp.wait_ge(s_dk, (part + 1) * H // 2)
                    for c, (a, b) in enumerate(CHUNKS):
                        sp.dma_start(dot_rows[heads, a * P:b * P].rearrange("h (t q) -> t h q", q=P),
                                     turned[0:b - a, heads, c, :]).then_inc(s_dst1, 16)
                sp.wait_ge(s_dst1, 2 * 16 * len(CHUNKS))

            @block.gpsimd
            def _(pool):
                with pool.Fori(0, EITER) as i:
                    for g in range(G):
                        pool.wait_ge(s_staged, i * G + g + 1)
                        pool.sem_inc(s_open, 1)
                        for u in range(G):
                            nc.gpsimd.indirect_dma_start(
                                out=qr[:, g, u, :], out_offset=None, in_=q_rows,
                                in_offset=bass.IndirectOffsetOnAxis(ap=src_s[:, g, u:u + 1], axis=0)).then_inc(s_got[g], 16)
                for s in sems0:
                    pool.sem_clear(s)

            @block.scalar
            def _(act):
                act.wait_ge(s_webz, 1)
                act.dma_start(we2[0:ED, 0:H], L0_gnn_We).then_inc(s_webd, 16)
                act.dma_start(we2[ED:2 * ED, H:2 * H], L0_gnn_We).then_inc(s_webd, 16)
                act.sem_inc(s_eae, G)
                act.sem_inc(s_esk, G)

                def stage(at, g):
                    nc.scalar.activation(src_s[:, g, :], src_t[:, at, :].rearrange("p a u -> p (a u)"), ACT.Copy)\
                      .then_inc(s_staged, 1)

                def k_onehots(slot, k_slot, turn):
                    act.wait_ge(s_loc[slot], 16 * (turn + 1))
                    act.wait_ge(s_kta, turn * G + slot + G)
                    act.sem_inc(carrier, 1)
                    for c in range(CD, CB):
                        last = nc.scalar.activation(dist[:, c - CD, :], loc[:, slot, :], ACT.Abs, bias=k_neg[:, c:c + 1])
                    last.then_inc(s_kabs, 1)
                    act.wait_ge(s_kabs, turn * G + slot + 1)
                    act.sem_inc(carrier, 1)
                    nc.scalar.activation(oh_k[:, k_slot, CD:CB, :], dist[:], ACT.Relu, bias=ones[0:3 * R, 0:1], scale=-1.0)\
                      .then_inc(s_kta, 1)

                act.wait_ge(s_free, G)
                for k in range(AHEAD):
                    stage(slice(k, k + 1), k)
                act.sem_inc(s_kta, G)
                act.wait_ge(s_kt, 1)
                k_onehots(0, K_SLOT[0], 0)
                for n in range(1, len(K_GROUPS)):
                    load_k(act, n)
                with act.Fori(0, EITER) as i:
                    for g in range(G):
                        act.wait_ge(s_free, i * G + g + AHEAD + 1)
                        act.sem_inc(carrier, 1)
                        stage(bass.ds(i * G + g + AHEAD, 1), (g + AHEAD) % G)
                        act.wait_ge(s_ead, i * G + g + 1 + G)
                        nc.scalar.activation(eaT[:, g, 0:2 * P], psE[:, g % 2, 0:2 * P], ACT.Copy)
                        nc.scalar.activation(eaT[0:ED, g, 2 * P:3 * P], psE[0:ED, g % 2, 2 * P:3 * P], ACT.Copy)\
                          .then_inc(s_eae, 1)
                        k_onehots((g + 1) % G, K_SLOT[(g + 1) % G], i + (g + 1) // G)
                        act.wait_ge(s_es, i * G + g + 1)
                        act.sem_inc(carrier, 1)
                        nc.scalar.activation(score[:, :, bass.ds(i * G * G + g * G, G)].rearrange("p h u -> p u h"),
                                             psS[0:P, g % 2, 0:G * H].rearrange("p (u h) -> p u h", h=H), ACT.Copy)\
                          .then_inc(s_esk, 1)
                for h in range(H):
                    act.wait_ge(s_dT, h + 1)
                    for c, (a, b) in enumerate(CHUNKS):
                        if b - a < CH:
                            nc.scalar.activation(turned[0:CH, h, 0:c, :].rearrange("t c q -> t (c q)"),
                                                 psK[0:CH, h % 3, 0:c * P], ACT.Copy)
                            last = nc.scalar.activation(turned[0:b - a, h, c, :], psK[0:b - a, h % 3, c * P:(c + 1) * P], ACT.Copy)
                    last.then_inc(s_dk, 1)

            @block.tensor
            def _(pe):
                pe.wait_ge(s_cntz, 1)
                pe.wait_ge(s_webd, 32)
                nc.tensor.matmul(psC[0:P, 0:T], zb[:], zb[:, 0:T], start=True, stop=False, skip_group_check=True)
                pe.sem_inc(s_ead, G)
                pe.sem_inc(s_ohu, G)
                with pe.Fori(0, EITER) as i:
                    for g in range(G):
                        _, first = nc.values_load_multi_w_load_instructions(
                            base_i[0:1, bass.ds(i * G * G + g * G, G)], engines=[mybir.EngineType.PE], min_val=0, max_val=KB - CB)
                        pe.wait_ge(s_ea[g], 32 * (i + 1))
                        pe.wait_ge(s_eae, i * G + previous_use(g, 2, G) + 1 + G)
                        for n in range(3):
                            w = min(128, G * ED - n * 128)
                            last = nc.tensor.transpose(psE[0:w, g % 2, n * P:(n + 1) * P], ea[:, g, n * 128:n * 128 + w],
                                                       ident[0:P, 0:P])
                        last.then_inc(s_ead, 1)
                        pe.wait_ge(s_kt, i * G + g + 1 + G)
                        pe.wait_ge(s_kta, i * G + g + 1 + G)
                        if g in K_GROUPS:
                            pe.wait_ge(s_kp[K_GROUPS.index(g)], 48)
                        for m, (a, b) in enumerate(BANKS):
                            pe.wait_ge(s_kfree, (i * G + g) * 3 + m + 1)
                            for u in range(a, b):
                                for c in range(CB):
                                    last = nc.tensor.matmul(psK[0:P, m, (u - a) * D:(u - a + 1) * D],
                                                            oh_k[:, K_SLOT[g], c, u * P:(u + 1) * P],
                                                            kp[:, bass.ds(first[u] + c, 1), :].rearrange("p a d -> p (a d)"),
                                                            start=(c == 0), stop=(c == CB - 1))
                            last.then_inc(s_kx, 1)
                        pe.wait_ge(s_eae, i * G + g + 1 + G)
                        pe.wait_ge(s_esk, i * G + previous_use(g, 2, G) + 1 + G)
                        for n in range(3):
                            w = min(128, G * ED - n * 128)
                            last = nc.tensor.matmul(psS[0:P, g % 2, n * 2 * H:n * 2 * H + w // ED * H],
                                                    eaT[0:w, g, n * P:(n + 1) * P], we2[0:w, 0:w // ED * H],
                                                    start=True, stop=True)
                        last.then_inc(s_es, 1)
                        pe.wait_ge(s_oh, i * G + g + 1)
                        for u in range(G):
                            last = nc.tensor.matmul(psC[0:P, 0:T], oh_lo[:, g, u, :], oh_hi[:, g, u, :], start=False, stop=False,
                                                    skip_group_check=True)
                        last.then_inc(s_ohu, 1)
                nc.tensor.matmul(psC[0:P, 0:T], zb[:], zb[:, 0:T], start=False, stop=True,
                                 skip_group_check=True).then_inc(s_cnt, 1)
                pe.wait_ge(s_free, G + NK)
                for h in range(H):
                    if h >= 3:
                        pe.wait_ge(s_dk, h - 2)
                    for c, (a, b) in enumerate(CHUNKS):
                        last = nc.tensor.transpose(psK[0:b - a, h % 3, c * P:(c + 1) * P], dots[:, h, a:b], ident[0:P, 0:P])
                    last.then_inc(s_dT, 1)

            @block.vector
            def _(v):
                def k_onehots(slot, k_slot, turn):
                    v.wait_ge(s_loc[slot], 16 * (turn + 1))
                    for c in range(CD):
                        last = nc.vector.tensor_scalar(oh_k[:, k_slot, c, :], loc[:, slot, :], k_at[:, c:c + 1], None, ALU.is_equal)
                    last.then_inc(s_kt, 1)

                nc.vector.memset(we2[:], 0.0).then_inc(s_webz, 1)
                nc.vector.memset(zb[:], 0.0).then_inc(s_cntz, 1)
                for n in range(2):
                    last = nc.vector.tensor_scalar(part_of[:, n:n + 1], rank_p[:, 0:1], float((n + 1) * R), -float(R), ALU.is_ge, ALU.mult)
                dve_order.link(v, last)
                for n in range(2):
                    dve_order.link(v, nc.vector.tensor_scalar(k_at[:], rank_p[:] if n == 0 else k_at[:], part_of[:, n:n + 1], None, ALU.add))
                dve_order.link(v, nc.vector.tensor_copy(src_f[:], src_i[:]))
                dve_order.link(v, nc.vector.tensor_scalar(lo[:], src_f[:], -float(P // 2), 1.0 / P, ALU.add, ALU.mult))
                dve_order.link(v, nc.vector.tensor_scalar(hi[:], lo[:], MAGIC, None, ALU.add))
                dve_order.link(v, nc.vector.tensor_scalar(hi[:], hi[:], MAGIC, None, ALU.subtract))
                dve_order.link(v, nc.vector.scalar_tensor_tensor(lo[:], hi[:], -float(P), src_f[:], ALU.mult, ALU.add))
                dve_order.link(v, nc.vector.tensor_scalar(k_neg[:], k_at[:], -1.0, None, ALU.mult))
                v.sem_inc(s_free, G)
                v.sem_inc(s_kt, G)
                v.sem_inc(s_kfree, 3)
                k_onehots(0, K_SLOT[0], 0)
                with v.Fori(0, EITER) as i:
                    for g in range(G):
                        at = bass.ds(i * G * G + g * G, G)
                        k_onehots((g + 1) % G, K_SLOT[(g + 1) % G], i + (g + 1) // G)
                        v.wait_ge(s_ohu, i * G + g + 1)
                        nc.vector.tensor_tensor(oh_lo[:, g], iota_row[:].unsqueeze(1).to_broadcast([P, G, P]),
                                                lo[:, at].unsqueeze(2).to_broadcast([P, G, P]), ALU.is_equal)
                        nc.vector.tensor_tensor(oh_hi[:, g], iota_row[:, 0:T].unsqueeze(1).to_broadcast([P, G, T]),
                                                hi[:, at].unsqueeze(2).to_broadcast([P, G, T]), ALU.is_equal).then_inc(s_oh, 1)
                        v.wait_ge(s_got[g], G * 16 * (i + 1))
                        for m, (a, b) in enumerate(BANKS):
                            v.wait_ge(s_kx, (i * G + g) * 3 + m + 1)
                            nc.vector.tensor_tensor(qr[:, g, a:b].rearrange("p u d -> p (u d)"),
                                                    qr[:, g, a:b].rearrange("p u d -> p (u d)"),
                                                    psK[0:P, m, 0:(b - a) * D], ALU.mult).then_inc(s_kfree, 1)
                        v.wait_ge(s_kfree, (i * G + g) * 3 + 6)
                        v.sem_inc(carrier, 1)
                        nc.vector.tensor_reduce(dots[:, :, at].rearrange("p h u -> p u h"),
                                                qr[:, g].rearrange("p u (h d) -> p u h d", h=H), AX.X, ALU.add).then_inc(s_free, 1)
                v.wait_ge(s_cnt, 1)
                dve_order.link(v, nc.vector.tensor_copy(counts[:, 0, :], psC[0:P, 0:T]))

        for s in sems0:
            nc.release_semaphore(s)

        x_sb = sb(top, "x_sb", [P, T, D])
        carry_on = sb(top, "carry_on", [P, T, P])
        over = sb(top, "over", [P, T, H])
        attn = sb(top, "attn", [P, T, H])
        s_next, s_rows, s_cont = sem("next_loaded"), sem("heads_tails"), sem("carry_on_made")
        s_rowsT, s_lr, s_lrT = (sem(n) for n in ("rows_turned", "reach_made", "reach_turned"))
        s_dot, s_xback, s_targets, s_m, s_ex, s_sums, s_sumst, s_over = (sem(n) for n in (
            "dots_loaded", "x_back", "targets_ready", "shifted", "exp_done", "sums_ready", "sums_stored", "over_done"))
        with ExitStack() as st:
            fmax = sb(st, "fmax", [P, H, J])
            rmax = sb(st, "rmax", [P, H, J])
            sums = sb(st, "sums", [P, J, H])
            next_i = sb(st, "next_i", [P, 1], I32)
            next_f = sb(st, "next_f", [P, 1])
            key = sb(st, "key", [P, 2])
            apart = sb(st, "apart", [P, J + 1])
            first = sb(st, "first", [P, 2, J])
            cols = sb(st, "cols", [P, 4, H])
            row = sb(st, "row", [H, 4, P])
            gap = sb(st, "gap", [H, 3, P])
            ext = sb(st, "ext", [H, 4, P])
            reach = sb(st, "reach", [P, 2, H])
            pre = sb(st, "pre", [P, T])
            dot = sb(st, "dot", [P, H, J])
            bo = sb(st, "bo", [P, D])
            psR = ps(st, "psR2", [128, 512])
            psL = ps(st, "psL2", [128, 512])
            psO = ps(st, "psO2", [128, 512])
            block = st.enter_context(nc.Block())
            TAIL, HEAD, FIRST, LAST = range(4)

            @block.sync
            def _(sp):
                for a, b in HALVES:
                    sp.dma_start(dot[a:b], dot_rows.rearrange("h (p j) -> p h j", p=P)[a:b]).then_inc(s_dot, 16)
                sp.wait_ge(s_next, 1)
                sp.dma_start(next_i[0:P - 1, :], dst.rearrange("(p j) -> p j", p=P)[1:P, 0:1],
                             allow_slow_non_contiguous=True).then_inc(s_next, 16)
                sp.wait_ge(s_dot, 32)
                for a, b in HALVES:
                    sp.dma_start(x_sb[a:b], rows_of_tiles(x)[a:b]).then_inc(s_xback, 16)
                sp.dma_start(bo[:], L0_gnn_bo.partition_broadcast(P)).then_inc(s_xback, 16)
                sp.wait_ge(s_sums, 1)
                for a, b in HALVES:
                    sp.dma_start(expsum_rows.rearrange("(p j) h -> p (j h)", p=P)[a:b, :],
                                 sums[a:b].rearrange("p j h -> p (j h)")).then_inc(s_sumst, 16)
                sp.wait_ge(s_sumst, 32)

            @block.gpsimd
            def _(pool):
                nc.gpsimd.iota(carry_on[:], pattern=[[P, T], [1, P]], base=0, channel_multiplier=0,
                               allow_small_or_imprecise_dtypes=True).then_inc(s_targets, 1)

            @block.scalar
            def _(act):
                for h in range(H):
                    act.wait_ge(s_m, h + 1)
                    nc.scalar.activation(fmax[:, h, :], rmax[:, h, :], ACT.Exp).then_inc(s_ex, 1)

            @block.tensor
            def _(pe):
                pe.wait_ge(s_rows, 1)
                for n in range(4):
                    last = nc.tensor.transpose(psR[0:H, n * P:(n + 1) * P], cols[:, n, :], ident[0:P, 0:P])
                last.then_inc(s_rowsT, 1)
                pe.wait_ge(s_lr, 1)
                for n in range(2):
                    last = nc.tensor.transpose(psL[0:P, n * H:(n + 1) * H], ext[:, 2 + n, :], ident[0:H, 0:H])
                last.then_inc(s_lrT, 1)
                pe.wait_ge(s_sums, 1)
                pe.wait_ge(s_cont, 1)
                for t in range(T):
                    last = nc.tensor.matmul(psO[0:P, t * H:(t + 1) * H], carry_on[:, t, :], sums[:, J - 1, :],
                                            start=True, stop=True)
                last.then_inc(s_over, 1)

            @block.vector
            def _(v):
                link = lambda ins: dve_order.link(v, ins)
                nc.vector.memset(next_i[:], -1).then_inc(s_next, 1)
                link(nc.vector.tensor_scalar(pre[:], counts[:, 0, :], 1.0, None, ALU.max))
                inverse_root(v, rsq_deg[:], pre[:], root_t[:])
                nc.vector.memset(apart[:, J:J + 1], -BIG)
                nc.vector.tensor_scalar(apart[:, 0:J], same[:], -1.0, BIG, ALU.add, ALU.mult)
                for n, c in ((0, 0), (1, J - 1)):
                    last = nc.vector.tensor_scalar(first[:, n, :], dst_f[:], dst_f[:, c:c + 1], None, ALU.is_equal)
                link(last)
                link(nc.vector.tensor_scalar(first[:], first[:], -1.0, BIG, ALU.add, ALU.mult))
                v.wait_ge(s_dot, 32)
                link(nc.vector.tensor_tensor(score[:], score[:], dot[:], ALU.add))
                for h in range(H):
                    last = nc.vector.tensor_tensor_scan(fmax[:, h, :], apart[:, 0:J], score[:, h, :], -BIG, ALU.add, ALU.max)
                link(last)
                for h in range(H):
                    last = nc.vector.tensor_tensor_scan(rmax[:, h, ::-1], apart[:, 1:J + 1][:, ::-1], fmax[:, h, ::-1], -BIG,
                                                        ALU.add, ALU.max)
                link(last)
                nc.vector.tensor_copy(cols[:, TAIL, :], rmax[:, :, J - 1])
                nc.vector.tensor_copy(cols[:, HEAD, :], rmax[:, :, 0])
                nc.vector.tensor_copy(cols[:, FIRST, :], dst_f[:, 0:1].to_broadcast([P, H]))
                nc.vector.tensor_copy(cols[:, LAST, :], dst_f[:, J - 1:J].to_broadcast([P, H])).then_inc(s_rows, 1)
                v.wait_ge(s_rowsT, 1)
                nc.vector.memset(gap[:], 0.0)
                link(nc.vector.tensor_copy(row[:].rearrange("h n p -> h (n p)"), psR[0:H, 0:4 * P]))
                nc.vector.tensor_tensor(gap[:, 0, 1:P], row[:, LAST, 1:P], row[:, LAST, 0:P - 1], ALU.is_equal)
                nc.vector.tensor_tensor(gap[:, 1, 0:P - 1], row[:, FIRST, 0:P - 1], row[:, FIRST, 1:P], ALU.is_equal)
                link(nc.vector.tensor_tensor(gap[:, 2, 1:P], row[:, FIRST, 1:P], row[:, LAST, 0:P - 1], ALU.is_equal))
                link(nc.vector.tensor_scalar(gap[:], gap[:], -1.0, BIG, ALU.add, ALU.mult))
                nc.vector.memset(ext[:, 2:4, :], -BIG)
                nc.vector.tensor_tensor_scan(ext[:, 0, :], gap[:, 0, :], row[:, TAIL, :], -BIG, ALU.add, ALU.max)
                link(nc.vector.tensor_tensor_scan(ext[:, 1, ::-1], gap[:, 1, ::-1], row[:, HEAD, ::-1], -BIG, ALU.add, ALU.max))
                nc.vector.tensor_tensor(ext[:, 2, 1:P], ext[:, 0, 0:P - 1], gap[:, 2, 1:P], ALU.add)
                nc.vector.tensor_tensor(ext[:, 3, 0:P - 1], ext[:, 1, 1:P], gap[:, 2, 1:P], ALU.add).then_inc(s_lr, 1)
                v.wait_ge(s_lrT, 1)
                link(nc.vector.tensor_copy(reach[:].rearrange("p n h -> p (n h)"), psL[0:P, 0:2 * H]))
                for n in range(2):
                    for h in range(H):
                        last = nc.vector.scalar_tensor_tensor(rmax[:, h, :], first[:, n, :], reach[:, n, h:h + 1], rmax[:, h, :],
                                                              ALU.add, ALU.max)
                    link(last)
                for h in range(H):
                    nc.vector.tensor_tensor(rmax[:, h, :], score[:, h, :], rmax[:, h, :], ALU.subtract).then_inc(s_m, 1)
                v.wait_ge(s_next, 17)
                link(nc.vector.tensor_copy(next_f[:], next_i[:]))
                link(nc.vector.tensor_tensor(key[:, 0:1], dst_f[:, J - 1:J], next_f[:], ALU.is_equal))
                link(nc.vector.tensor_scalar(key[:, 1:2], dst_f[:, J - 1:J], 1.0, None, ALU.add))
                link(nc.vector.tensor_tensor(key[:, 1:2], key[:, 1:2], key[:, 0:1], ALU.mult))
                link(nc.vector.tensor_scalar(key[:, 1:2], key[:, 1:2], -1.0, None, ALU.add))
                v.wait_ge(s_targets, 1)
                nc.vector.tensor_scalar(carry_on[:], carry_on[:], key[:, 1:2], None, ALU.is_equal).then_inc(s_cont, 1)
                for h in range(H):
                    v.wait_ge(s_ex, h + 1)
                    last = nc.vector.tensor_tensor_scan(sums[:, :, h], same[:], fmax[:, h, :], 0.0, ALU.mult, ALU.add)
                last.then_inc(s_sums, 1)
                v.wait_ge(s_xback, 48)
                link(nc.vector.tensor_tensor(x_sb[:], x_sb[:], bo[:].unsqueeze(1).to_broadcast([P, T, D]), ALU.add))
                v.wait_ge(s_over, 1)
                link(nc.vector.tensor_copy(over[:].rearrange("p t h -> p (t h)"), psO[0:P, 0:T * H]))

        s_w3, s_agg, s_trA, s_tA, s_trB, s_tB, s_o3, s_n3, s_kept3, s_h3, s_ge3, s_lg3, s_lg3e = (sem(n) for n in (
            "w3_loaded", "agg_ready", "agg_turned", "aggT_ready", "n3_turned", "n3T_ready", "o3_done", "n3_ready", "n3_kept",
            "h3_done", "gelu3_done", "logits3_done", "logits3_kept"))
        s_lgT, s_res = sem("logits_turned"), sem("residual_ready")
        s_tok = [sem(f"tokens{n}_stored") for n in range(2)]
        HALF = (313, 312)
        with ExitStack() as st:
            wo = sb(st, "wo", [128, KD, D])
            w1 = sb(st, "w1_3", [128, KD, C])
            wg = sb(st, "wg", [128, KC, X])
            tile_a = sb(st, "tile_a", [P, G, D])
            tT = sb(st, "tT3", [128, G * KD, P])
            nT = sb(st, "nT3", [128, KD, G * P])
            hT = sb(st, "hT3", [128, KC, G * P])
            logitsT = sb(st, "logitsT", [X, N_NODES])
            den = sb(st, "den", [P, T, H])
            den2 = sb(st, "den2", [P, G, H])
            psT = ps(st, "psT3", [128, 3, 512])
            psO = ps(st, "psO3", [128, 3 * 512])
            psH = ps(st, "psH3", [128, 2, 512])
            block = st.enter_context(nc.Block())

            @block.sync
            def _(sp):
                sp.dma_start(wo[:], L0_gnn_Wo.rearrange("(k p) d -> p k d", p=128)).then_inc(s_w3, 16)
                sp.dma_start(w1[:], L0_ffn_W1.rearrange("(k p) d -> p k d", p=128)).then_inc(s_w3, 16)
                sp.dma_start(wg[:], L0_ffn_Wg.rearrange("(k p) d -> p k d", p=128)).then_inc(s_w3, 16)
                sp.dma_start(gate_b[:], L0_ffn_bg.partition_broadcast(P)).then_inc(s_w3, 16)
                with sp.Fori(0, NG) as i:
                    sp.wait_ge(s_kept3, i + 1)
                    for a, b in HALVES:
                        sp.dma_start(rows_of_tiles(tok0)[a:b, bass.ds(i * G, G), :], n_sb[a:b, bass.ds(i * G, G), :])\
                          .then_inc(s_tok[0], 16)
                sp.wait_ge(s_w3, 64)

            @block.gpsimd
            def _(pool):
                for t in range(T):
                    nc.gpsimd.indirect_dma_start(out=den[:, t, :], out_offset=None, in_=expsum_rows,
                                                 in_offset=bass.IndirectOffsetOnAxis(ap=end_i[:, t:t + 1], axis=0))\
                      .then_inc(s_group[t // G], 16)

            @block.vector
            def _(v):
                def weights(i):
                    tiles = slice(i * G, (i + 1) * G)
                    link = lambda ins: dve_order.link(v, ins)
                    v.wait_ge(s_group[i], 2 * GATHER)
                    link(nc.vector.tensor_tensor(den[:, tiles], den[:, tiles], has_in[:, tiles].unsqueeze(2)
                                                 .to_broadcast([P, G, H]), ALU.mult))
                    link(nc.vector.tensor_tensor(den[:, tiles], den[:, tiles], over[:, tiles], ALU.add))
                    link(nc.vector.tensor_scalar(den2[:], den[:, tiles], 1e-30, None, ALU.max))
                    link(nc.vector.reciprocal(den2[:], den2[:]))
                    link(nc.vector.tensor_tensor(attn[:, tiles], den[:, tiles], den2[:], ALU.mult))

                def weigh(i):
                    tiles = bass.ds(i * G, G)
                    nc.vector.tensor_tensor(tile_a[:].rearrange("p u (h d) -> p (u h) d", h=H),
                                            n_sb[:, tiles, :].rearrange("p u (h d) -> p (u h) d", h=H),
                                            attn[:, tiles, :].rearrange("p u h -> p (u h)").unsqueeze(2)
                                            .to_broadcast([P, G * H, DH]), ALU.mult).then_inc(s_agg, 1)

                def update(i):
                    tiles = bass.ds(i * G, G)
                    v.wait_ge(s_o3, i + 1)
                    dve_order.link(v, nc.vector.tensor_tensor(x_sb[:, tiles, :], x_sb[:, tiles, :],
                                                              psO[0:P, :].rearrange("p (u d) -> p u d", d=D)[:, 0:G, :], ALU.add))
                    v.sem_inc(s_res, 1)
                    v.wait_ge(s_trB, i + 1)
                    dve_order.link(v, normalise(v, lambda u: x_sb[:, bass.ds(i * G + u, 1), :].rearrange("p a d -> p (a d)"),
                                                lambda u: tile_n[:, u, :]))
                    v.sem_inc(s_n3, 1)
                    nc.vector.tensor_tensor(n_sb[:, tiles, :], tile_n[:], tile_n[:], ALU.max).then_inc(s_kept3, 1)

                v.sem_inc(s_n3, 1)
                v.sem_inc(s_res, 1)
                weights(0)
                weigh(0)
                weights(1)
                v.wait_ge(s_trA, 1)
                weigh(1)
                update_links = 16
                update(0)
                for i in range(2, NG):
                    weights(i)
                with v.Fori(1, NG - 1) as i:
                    dve_order.turn(i - 1, update_links)
                    update(i)
                    weigh(i + 1)
                dve_order.leave(NG - 2)
                update(NG - 1)
                v.wait_ge(s_kept3, NG)

            @block.scalar
            def _(act):
                def fetch_aggregate(i):
                    act.wait_ge(s_trA, i + 1)
                    fetch_turned(tT, psT).then_inc(s_tA, 1)

                def gelus(i):
                    act.wait_ge(s_trB, i + 2)
                    for u in range(G):
                        for k in range(KD):
                            n = u * KD + k
                            last = nc.scalar.activation(nT[:, k, u * P:(u + 1) * P],
                                                        psT[:, n // 4, (n % 4) * P:(n % 4 + 1) * P], ACT.Copy)
                    last.then_inc(s_tB, 1)
                    for n in range(2 * KC):
                        m, f = n // 2, n % 2
                        act.wait_ge(s_h3, i * 2 * KC + n + 1)
                        nc.scalar.activation(hT[:, m, f * HALF[0]:f * HALF[0] + HALF[f]], psH[:, n % 2, 0:HALF[f]], ACT.Gelu,
                                             bias=b1_0[:, m:m + 1]).then_inc(s_ge3, 1)

                def keep_logits(i):
                    for f in range(2):
                        act.wait_ge(s_lg3, i * 2 + f + 1)
                        act.sem_inc(carrier, 1)
                        nc.scalar.activation(logitsT[:, bass.ds(i * G * P + f * HALF[0], HALF[f])], psH[0:X, f, 0:HALF[f]], ACT.Copy)\
                          .then_inc(s_lg3e, 1)

                act.sem_inc(s_lg3e, 2)
                fetch_aggregate(0)
                with act.Fori(0, NG - 1) as i:
                    fetch_aggregate(i + 1)
                    gelus(i)
                    keep_logits(i)
                gelus(NG - 1)
                keep_logits(NG - 1)
                act.wait_ge(s_lgT, 1)
                nc.scalar.activation(logits[:].rearrange("p t e -> p (t e)"), psO[0:P, 0:T * X], ACT.Copy)

            @block.tensor
            def _(pe):
                def project(i):
                    pe.wait_ge(s_agg, i + 1)
                    turn_tiles(pe, psT, tile_a).then_inc(s_trA, 1)
                    pe.wait_ge(s_tA, i + 1)
                    pe.wait_ge(s_res, i + 1)
                    for u in range(G):
                        for k in range(KD):
                            last = nc.tensor.matmul(psO[0:P, u * D:(u + 1) * D], tT[:, u * KD + k, :], wo[:, k, :],
                                                    start=(k == 0), stop=(k == KD - 1))
                    last.then_inc(s_o3, 1)

                def gate_logits(i):
                    pe.wait_ge(s_n3, i + 2)
                    turn_tiles(pe, psT, tile_n).then_inc(s_trB, 1)
                    pe.wait_ge(s_tB, i + 1)
                    for n in range(2 * KC):
                        m, f = n // 2, n % 2
                        if n >= 2:
                            pe.wait_ge(s_ge3, i * 2 * KC + n - 1)
                        else:
                            pe.wait_ge(s_lg3e, i * 2 + n + 1)
                        for k in range(KD):
                            last = nc.tensor.matmul(psH[:, n % 2, 0:HALF[f]], w1[:, k, m * 128:(m + 1) * 128],
                                                    nT[:, k, f * HALF[0]:f * HALF[0] + HALF[f]],
                                                    start=(k == 0), stop=(k == KD - 1))
                        last.then_inc(s_h3, 1)
                    pe.wait_ge(s_ge3, (i + 1) * 2 * KC)
                    for f in range(2):
                        for m in range(KC):
                            last = nc.tensor.matmul(psH[0:X, f, 0:HALF[f]], wg[:, m, :],
                                                    hT[:, m, f * HALF[0]:f * HALF[0] + HALF[f]],
                                                    start=(m == 0), stop=(m == KC - 1))
                        last.then_inc(s_lg3, 1)

                pe.sem_inc(s_trB, 1)
                pe.wait_ge(s_w3, 64)
                project(0)
                with pe.Fori(0, NG - 1) as i:
                    project(i + 1)
                    gate_logits(i)
                gate_logits(NG - 1)
                pe.wait_ge(s_lg3e, 2 * NG + 2)
                pe.wait_ge(s_n3, NG + 1)
                for t in range(T):
                    last = nc.tensor.transpose(psO[0:P, t * X:(t + 1) * X], logitsT[:, t * P:(t + 1) * P], ident[0:X, 0:X])
                last.then_inc(s_lgT, 1)

        def route(name, picks, n_blocks):
            s_pick, s_cum, s_onehot, s_map, s_iota = (sem(name + n) for n in (
                "_picked", "_counted", "_one_hots", "_mapped", "_iota"))
            with ExitStack() as st:
                e3 = sb(st, name + "e3", [P, T, X])
                prob = sb(st, name + "prob", [P, T, X])
                work = sb(st, name + "work", [P, T, X])
                pick = sb(st, name + "pick", [P, 2, T, X])
                both = sb(st, name + "both", [P, T, X])
                col = sb(st, name + "col", [P, 4, T])
                tot = sb(st, name + "tot", [P, T, X])
                run = sb(st, name + "run", [P, T, X])
                one_row = sb(st, name + "ones", [P, T])
                step = sb(st, name + "step", [P, X, T])
                full = sb(st, name + "full", [P, X, T])
                nblk = sb(st, name + "nblk", [P, 3, X])
                slot_f = sb(st, name + "slot_f", [P, picks, T])
                slot_i = sb(st, name + "slot_i", [P, picks, T], I32)
                blk_i = sb(st, name + "blk_i", [P, picks, T], I32)
                blk_f = sb(st, name + "blk_f", [P, picks, T])
                at_f = sb(st, name + "at_f", [P, picks, T])
                p_num = sb(st, name + "p_num", [P, 1])
                t_num = sb(st, name + "t_num", [P, picks, T])
                row_s = sb(st, name + "row_s", [P, S])
                row_b = sb(st, name + "row_b", [P, n_blocks])
                in_slot = sb(st, name + "in_slot", [P, picks, T, S], BF16)
                in_block = sb(st, name + "in_block", [P, T, n_blocks])
                named = sb(st, name + "named", [P, picks, T, 2, n_blocks], BF16)
                spare = sb(st, name + "spare", [S, n_blocks])
                goal = sb(st, name + "goal", [S, n_blocks])
                mark = sb(st, name + "mark", [S, n_blocks])
                goal_f = sb(st, name + "goal_f", [S, n_blocks])
                psM = ps(st, name + "psM", [128, 512])
                b_of = sb(st, name + "b_of", [1, n_blocks, X])
                be_f = sb(st, name + "be_f", [1, n_blocks])
                psN = ps(st, name + "psN", [128, 512])
                block = st.enter_context(nc.Block())

                @block.gpsimd
                def _(pool):
                    nc.gpsimd.iota(step[:], pattern=[[0, X], [S, T]], base=0, channel_multiplier=0,
                                   allow_small_or_imprecise_dtypes=True).then_inc(s_iota, 1)
                    nc.gpsimd.iota(b_of[:], pattern=[[1, n_blocks], [0, X]], base=0, channel_multiplier=0,
                                   allow_small_or_imprecise_dtypes=True).then_inc(s_iota, 1)
                    for row, n in ((row_s, S), (row_b, n_blocks)):
                        nc.gpsimd.iota(row[:], pattern=[[1, n]], base=0, channel_multiplier=0,
                                       allow_small_or_imprecise_dtypes=True).then_inc(s_iota, 1)
                    nc.gpsimd.iota(t_num[:], pattern=[[T, picks], [1, T]], base=0, channel_multiplier=0,
                                   allow_small_or_imprecise_dtypes=True).then_inc(s_iota, 1)
                    nc.gpsimd.iota(spare[:], pattern=[[0, n_blocks // 2], [S, 2]], base=1 + picks * N_NODES, channel_multiplier=1,
                                   allow_small_or_imprecise_dtypes=True).then_inc(s_iota, 1)

                @block.scalar
                def _(act):
                    act.wait_ge(s_pick, 1)
                    nc.scalar.activation(prob[:], work[:], ACT.Exp).then_inc(s_pick, 1)

                @block.tensor
                def _(pe):
                    pe.wait_ge(s_pick, 3)
                    nc.tensor.matmul(psN[0:P, 0:T * X], before[:], both[:].rearrange("p t e -> p (t e)"), start=True, stop=True)
                    nc.tensor.matmul(psN[0:P, T * X:2 * T * X], ones[0:P, 0:P], both[:].rearrange("p t e -> p (t e)"),
                                     start=True, stop=True).then_inc(s_cum, 1)
                    for k in range(picks):
                        pe.wait_ge(s_onehot, k + 1)
                        for t in range(T):
                            last = nc.tensor.matmul(psM[0:S, 0:2 * n_blocks], in_slot[:, k, t, :],
                                                    named[:, k, t].rearrange("p a b -> p (a b)"),
                                                    start=(k == 0 and t == 0), stop=(k == picks - 1 and t == T - 1))
                    last.then_inc(s_map, 1)

                @block.vector
                def _(v):
                    link = lambda ins: dve_order.link(v, ins)
                    over_e = lambda c: col[:, c, :].unsqueeze(2).to_broadcast([P, T, X])
                    link(nc.vector.memset(one_row[:], 1.0))
                    link(nc.vector.memset(from_i[:], 0))
                    link(nc.vector.tensor_scalar(p_num[:], node_f[:, 0:1], 1.0, None, ALU.add))
                    link(nc.vector.tensor_tensor(logits[:], logits[:], gate_b[:].unsqueeze(1).to_broadcast([P, T, X]), ALU.add))
                    link(nc.vector.tensor_reduce(col[:, 0, :], logits[:], AX.X, ALU.max))
                    nc.vector.tensor_tensor(work[:], logits[:], over_e(0), ALU.subtract).then_inc(s_pick, 1)
                    v.wait_ge(s_pick, 2)
                    link(nc.vector.tensor_reduce(col[:, 0, :], prob[:], AX.X, ALU.add))
                    link(nc.vector.reciprocal(col[:, 0, :], col[:, 0, :]))
                    link(nc.vector.tensor_tensor(prob[:], prob[:], over_e(0), ALU.mult))
                    for k in range(picks):
                        link(nc.vector.tensor_reduce(gate[:, k, :], prob[:], AX.X, ALU.max))
                        link(nc.vector.tensor_tensor(work[:], prob[:], gate[:, k, :].unsqueeze(2).to_broadcast([P, T, X]),
                                                     ALU.is_equal))
                        link(nc.vector.tensor_tensor(work[:], work[:], rank8[:], ALU.mult))
                        link(nc.vector.tensor_reduce(col[:, 1, :], work[:], AX.X, ALU.max))
                        link(nc.vector.tensor_tensor(pick[:, k], rank8[:], over_e(1), ALU.is_equal))
                        if k + 1 < picks:
                            link(nc.vector.scalar_tensor_tensor(prob[:], pick[:, k], -2.0, prob[:], ALU.mult, ALU.add))
                    if picks == 2:
                        nc.vector.tensor_tensor(both[:], pick[:, 0], pick[:, 1], ALU.add).then_inc(s_pick, 1)
                        link(nc.vector.tensor_tensor(col[:, 2, :], gate[:, 0, :], gate[:, 1, :], ALU.add))
                        link(nc.vector.reciprocal(col[:, 2, :], col[:, 2, :]))
                        link(nc.vector.tensor_tensor(gate[:], gate[:], col[:, 2, :].unsqueeze(1).to_broadcast([P, 2, T]), ALU.mult))
                    else:
                        nc.vector.tensor_copy(both[:], pick[:, 0]).then_inc(s_pick, 1)
                    v.wait_ge(s_cum, 1)
                    v.wait_ge(s_iota, 6)
                    link(nc.vector.tensor_copy(tot[:].rearrange("p t e -> p (t e)"), psN[0:P, T * X:2 * T * X]))
                    for e in range(X):
                        last = nc.vector.tensor_tensor_scan(run[:, :, e], one_row[:], tot[:, :, e], 0.0, ALU.mult, ALU.add)
                    link(last)
                    link(nc.vector.tensor_tensor(full[:], run[:, T - 1, :].unsqueeze(2).to_broadcast([P, X, T]), step[:], ALU.is_gt))
                    link(nc.vector.tensor_reduce(nblk[:, 0, :], full[:], AX.X, ALU.add))
                    link(nc.vector.tensor_tensor_scan(nblk[:, 1, :], one_row[:, 0:X], nblk[:, 0, :], 0.0, ALU.mult, ALU.add))
                    link(nc.vector.tensor_tensor(nblk[:, 2, :], nblk[:, 1, :], nblk[:, 0, :], ALU.subtract))
                    link(nc.vector.tensor_tensor(run[:], run[:], tot[:], ALU.subtract))
                    link(nc.vector.tensor_tensor(run[:], run[:], psN[0:P, 0:T * X].rearrange("p (t e) -> p t e", e=X), ALU.add))
                    link(nc.vector.tensor_scalar(nblk[:, 0, :], nblk[:, 2, :], float(S), None, ALU.mult))
                    link(nc.vector.tensor_tensor(run[:], run[:], nblk[:, 0, :].unsqueeze(1).to_broadcast([P, T, X]), ALU.add))
                    for k in range(picks):
                        link(nc.vector.tensor_tensor(work[:], run[:], pick[:, k], ALU.mult))
                        link(nc.vector.tensor_reduce(slot_f[:, k, :], work[:], AX.X, ALU.add))
                    link(nc.vector.tensor_copy(slot_i[:], slot_f[:]))
                    link(nc.vector.tensor_scalar(blk_i[:], slot_i[:], S.bit_length() - 1, None, ALU.logical_shift_right))
                    link(nc.vector.tensor_copy(blk_f[:], blk_i[:]))
                    link(nc.vector.scalar_tensor_tensor(at_f[:], blk_f[:], -float(S), slot_f[:], ALU.mult, ALU.add))
                    over_n = lambda a, k, n: a[:, k, :].unsqueeze(2).to_broadcast([P, T, n])
                    over_t = lambda a, n: a[:].unsqueeze(1).to_broadcast([P, T, n])
                    for k in range(picks):
                        link(nc.vector.tensor_tensor(in_block[:], over_n(blk_f, k, n_blocks), over_t(row_b, n_blocks), ALU.is_equal))
                        nc.vector.tensor_scalar(named[:, k, :, 0, :], in_block[:], p_num[:, 0:1], None, ALU.mult)
                        link(nc.vector.tensor_tensor(named[:, k, :, 1, :], in_block[:], over_n(t_num, k, n_blocks), ALU.mult))
                        link(nc.vector.tensor_tensor(in_slot[:, k], over_n(at_f, k, S), over_t(row_s, S), ALU.is_equal))
                        v.sem_inc(s_onehot, 1)
                    link(nc.vector.tensor_tensor(b_of[:], b_of[:], nblk[0:1, 1, :].unsqueeze(1)
                                                 .to_broadcast([1, n_blocks, X]), ALU.is_ge))
                    link(nc.vector.tensor_reduce(be_f[:], b_of[:], AX.X, ALU.add))
                    link(nc.vector.tensor_scalar(be_f[:], be_f[:], float(X - 1), None, ALU.min))
                    link(nc.vector.tensor_copy(block_e[:, 0:n_blocks], be_f[:]))
                    v.wait_ge(s_map, 1)
                    link(nc.vector.tensor_copy(goal[:], psM[0:S, 0:n_blocks]))
                    link(nc.vector.scalar_tensor_tensor(goal[:], psM[0:S, n_blocks:2 * n_blocks], float(P), goal[:], ALU.mult, ALU.add))
                    link(nc.vector.tensor_scalar(mark[:], goal[:], 0.0, None, ALU.is_equal))
                    link(nc.vector.tensor_tensor(goal_f[:], mark[:], spare[:], ALU.mult))
                    link(nc.vector.tensor_tensor(goal_f[:], goal_f[:], goal[:], ALU.add))
                    link(nc.vector.tensor_copy(to_i[:, 0:n_blocks], goal_f[:]))
                    link(nc.vector.tensor_scalar(goal[:], goal[:], -1.0, 0.0, ALU.add, ALU.max))
                    if picks == 2:
                        link(nc.vector.tensor_scalar(mark[:], goal[:], float(N_NODES), None, ALU.is_ge))
                        link(nc.vector.scalar_tensor_tensor(goal[:], mark[:], -float(N_NODES), goal[:], ALU.mult, ALU.add))
                    link(nc.vector.tensor_copy(from_i[:, 0:n_blocks], goal[:]))

        def experts(name, n_blocks, tok, s_tok, y, W1, W2, b2, own_w1):
            s_w1c, s_x0 = sem(name + "_common_w1"), [sem(f"{name}_rows{n}") for n in range(2)]
            s_w1 = [sem(f"{name}_w1_{n}_loaded") for n in range(2)] if own_w1 else None
            s_w2 = [sem(f"{name}_w2_{n}_loaded") for n in range(2)]
            s_tr, s_xT, s_h, s_ge, s_y, s_ye = (sem(name + n) for n in (
                "_turned", "_xT_ready", "_hidden", "_gelu", "_y_done", "_y_ready"))
            s_yst = [sem(f"{name}_y{n}_stored") for n in range(2)]
            turns = n_blocks // 2
            assert n_blocks == 2 * turns
            with ExitStack() as st:
                w1 = [sb(st, f"{name}w1_{n}", [128, KD, C]) for n in range(2 if own_w1 else 1)]
                w2 = [sb(st, f"{name}w2_{n}", [128, KC, D]) for n in range(2)]
                b2r = [sb(st, f"{name}b2_{n}", [S, D]) for n in range(2)]
                xr = [sb(st, f"{name}xr_{n}", [S, D]) for n in range(2)]
                from_s = [sb(st, f"{name}from_{n}", [S, 1], I32) for n in range(2)]
                to_s = [sb(st, f"{name}to_{n}", [S, 1], I32) for n in range(2)]
                xT = [sb(st, f"{name}xT_{n}", [128, KD, S]) for n in range(2)]
                hT = [sb(st, f"{name}hT_{n}", [128, KC, S]) for n in range(2)]
                yr = [sb(st, f"{name}yr_{n}", [S, D]) for n in range(2)]
                par = [sb(st, f"{name}par_{n}", [128, KC + 2 * KD]) for n in range(2)]
                psT = ps(st, name + "psT", [128, 2, 512])
                psH = [ps(st, f"{name}psH{n}", [128, C]) for n in range(2)]
                psY = ps(st, name + "psY", [128, 2, 512])
                exp_flat = exp_par[:].rearrange("p e c -> p (e c)")
                npar = KC + 2 * KD
                s_from = sem(name + "_tokens_named")
                block = st.enter_context(nc.Block())

                @block.sync
                def _(sp):
                    if not own_w1:
                        sp.dma_start(w1[0][:], W1.rearrange("(k p) c -> p k c", p=128)).then_inc(s_w1c, 16)
                    def expert_of(at):
                        return sp.value_load(block_e[0:1, at], min_val=0, max_val=X - 1)

                    def load_w1(b, s, at):
                        if own_w1:
                            e = expert_of(at)
                            sp.wait_ge(s_h, b * 2 + 2)
                            sp.dma_start(w1[s][:], W1[bass.ds(e, 1)].rearrange("a (k p) c -> p (a k) c", p=128))\
                              .then_inc(s_w1[s], 16)

                    def load_w2(b, s, at):
                        e = expert_of(at)
                        sp.wait_ge(s_ye, b + 1)
                        sp.dma_start(w2[s][:], W2[bass.ds(e, 1)].rearrange("a (k p) c -> p (a k) c", p=128)).then_inc(s_w2[s], 16)
                        sp.dma_start(b2r[s][:], b2[bass.ds(e, 1), :].to_broadcast([S, D])).then_inc(s_w2[s], 16)

                    load_w1(0, 0, slice(0, 1))
                    with sp.Fori(0, turns - 1) as t:
                        load_w1(t * 2 + 1, 1, bass.ds(t * 2 + 1, 1))
                        load_w2(t * 2, 0, bass.ds(t * 2, 1))
                        load_w1(t * 2 + 2, 0, bass.ds(t * 2 + 2, 1))
                        load_w2(t * 2 + 1, 1, bass.ds(t * 2 + 1, 1))
                    load_w1(n_blocks - 1, 1, slice(n_blocks - 1, n_blocks))
                    for b in (n_blocks - 2, n_blocks - 1):
                        load_w2(b, b % 2, slice(b, b + 1))

                @block.gpsimd
                def _(pool):
                    def load_rows(t, s):
                        b = t * 2 + s
                        pool.wait_ge(s_from, b + 1)
                        pool.wait_ge(s_tr, b + 1)
                        pool.sem_inc(carrier, 1)
                        nc.gpsimd.indirect_dma_start(out=xr[s][:], out_offset=None, in_=tok,
                                                     in_offset=bass.IndirectOffsetOnAxis(ap=from_s[s][:, 0:1], axis=0))\
                          .then_inc(s_x0[s], 16)

                    def store_rows(t, s):
                        b = t * 2 + s
                        pool.wait_ge(s_ye, b + 3)
                        pool.sem_inc(carrier, 1)
                        nc.gpsimd.indirect_dma_start(out=y, out_offset=bass.IndirectOffsetOnAxis(ap=to_s[s][:, 0:1], axis=0),
                                                     in_=yr[s][:], in_offset=None).then_inc(s_yst[s], 16)

                    pool.wait_ge(s_tok, 32 * NG)
                    for b in range(3):
                        load_rows(b // 2, b % 2)
                    with pool.Fori(0, turns - 2) as t:
                        load_rows(t + 1, 1)
                        store_rows(t, 0)
                        load_rows(t + 2, 0)
                        store_rows(t, 1)
                    load_rows(turns - 1, 1)
                    for b in range(n_blocks - 4, n_blocks):
                        store_rows(b // 2, b % 2)
                    for s in range(2):
                        pool.wait_ge(s_yst[s], 16 * turns)

                @block.scalar
                def _(act):
                    act.sem_inc(s_ge, 2)
                    with act.Fori(0, turns) as t:
                        for s in range(2):
                            for m in range(KC):
                                if m % (KC // 2) == 0:
                                    act.wait_ge(s_h, (t * 2 + s) * 2 + 5 + m // (KC // 2))
                                last = nc.scalar.activation(hT[s][:, m, :], psH[s][:, m * 128:(m + 1) * 128], ACT.Gelu,
                                                            bias=par[s][:, m:m + 1] if own_w1 else b1_0[:, m:m + 1])
                            last.then_inc(s_ge, 1)

                @block.tensor
                def _(pe):
                    def turn(t, s):
                        pe.wait_ge(s_x0[s], (t + 1) * 16)
                        for k in range(KD):
                            last = nc.tensor.transpose(psT[:, s, k * 128:(k + 1) * 128], xr[s][:, k * 128:(k + 1) * 128], ident[:])
                        last.then_inc(s_tr, 1)

                    def hidden(t, s):
                        b = t * 2 + s
                        pe.wait_ge(s_xT, b + 1)
                        if own_w1:
                            pe.wait_ge(s_w1[s], (t + 1) * 16)
                        pe.wait_ge(s_ge, b + 1)
                        for m in range(KC):
                            for k in range(KD):
                                last = nc.tensor.matmul(psH[s][:, m * 128:(m + 1) * 128],
                                                        w1[s if own_w1 else 0][:, k, m * 128:(m + 1) * 128], xT[s][:, k, :],
                                                        start=(k == 0), stop=(k == KD - 1))
                            if m % (KC // 2) == KC // 2 - 1:
                                last.then_inc(s_h, 1)

                    def output(t, s):
                        b = t * 2 + s
                        pe.wait_ge(s_w2[s], (t + 1) * 32)
                        pe.wait_ge(s_ge, b + 3)
                        pe.wait_ge(s_ye, b + 1)
                        for m in range(KC):
                            last = nc.tensor.matmul(psY[:, s, 0:D], hT[s][:, m, :], w2[s][:, m, :],
                                                    start=(m == 0), stop=(m == KC - 1))
                        last.then_inc(s_y, 1)

                    pe.sem_inc(s_tr, 2)
                    pe.sem_inc(s_h, 4)
                    turn(0, 0)
                    turn(0, 1)
                    if not own_w1:
                        pe.wait_ge(s_w1c, 16)
                    hidden(0, 0)
                    with pe.Fori(0, turns - 1) as t:
                        hidden(t, 1)
                        turn(t + 1, 0)
                        output(t, 0)
                        hidden(t + 1, 0)
                        turn(t + 1, 1)
                        output(t, 1)
                    hidden(turns - 1, 1)
                    output(turns - 1, 0)
                    output(turns - 1, 1)

                @block.vector
                def _(v):
                    def fetch_rows(t, s, order):
                        b = t * 2 + s
                        if own_w1:
                            e = v.value_load(block_e[0:1, order], min_val=0, max_val=X - 1)
                            v.wait_ge(s_ge, b + 1)
                            v.sem_inc(carrier, 1)
                            dve_order.link(v, nc.vector.tensor_copy(par[s][:], exp_flat[:, bass.ds(e * npar, npar)]))
                        v.wait_ge(s_tr, b + 3)
                        if own_w1:
                            for k in range(KD):
                                last = nc.vector.tensor_scalar(xT[s][:, k, :], psT[:, s, k * 128:(k + 1) * 128],
                                                               par[s][:, KC + k:KC + k + 1],
                                                               par[s][:, KC + KD + k:KC + KD + k + 1], ALU.mult, ALU.add)
                        else:
                            last = nc.vector.tensor_copy(xT[s][:].rearrange("p k c -> p (k c)"), psT[:, s, 0:KD * 128])
                        last.then_inc(s_xT, 1)

                    def fetch_output(t, s, order, slot_used=True):
                        b = t * 2 + s
                        if slot_used:
                            v.wait_ge(s_yst[s], t * 16)
                        v.sem_inc(carrier, 1)
                        dve_order.link(v, nc.vector.tensor_copy(to_s[s][:], to_i[:, order]))
                        v.wait_ge(s_y, b + 1)
                        nc.vector.tensor_tensor(yr[s][:], psY[:, s, 0:D], b2r[s][:], ALU.add).then_inc(s_ye, 1)

                    def name_tokens(s, order):
                        nc.vector.tensor_copy(from_s[s][:], from_i[:, order]).then_inc(s_from, 1)

                    v.sem_inc(s_ye, 2)
                    for s in range(2):
                        name_tokens(s, slice(s, s + 1))
                    for s in range(2):
                        fetch_rows(0, s, slice(s, s + 1))
                        name_tokens(s, slice(s + 2, s + 3))
                    for s in range(2):
                        fetch_rows(1, s, slice(s + 2, s + 3))
                        name_tokens(s, slice(s + 4, s + 5))
                        fetch_output(0, s, slice(s, s + 1), slot_used=False)
                    with v.Fori(1, turns - 1) as t:
                        dve_order.turn(t - 1, 4 if own_w1 else 2)
                        for s in range(2):
                            fetch_rows(t + 1, s, bass.ds(t * 2 + s + 2, 1))
                            name_tokens(s, bass.ds(t * 2 + s + 4, 1))
                            fetch_output(t, s, bass.ds(t * 2 + s, 1))
                    dve_order.leave(turns - 2)
                    for s in range(2):
                        fetch_output(turns - 1, s, slice(n_blocks - 2 + s, n_blocks - 1 + s))

        route("r0", 1, NB0)
        experts("m0", NB0, tok0, s_tok[0], y0, L0_ffn_W1, L0_ffn_Wd, L0_ffn_bd, False)

        s_yt = [sem(f"outputs{n}_loaded") for n in range(NG)]
        s_n6, s_f6, s_f6st = sem("n6_ready"), sem("f6_ready"), sem("f6_stored")
        with ExitStack() as st:
            yt = sb(st, "yt6", [P, T, D])
            stats6 = sb(st, "stats6", [P, T, 6])
            mv6 = sb(st, "mv6", [P, T, 2])
            sq6 = sb(st, "sq6", [P, T])
            inv_dev6 = sb(st, "inv_dev6", [P, T])
            block = st.enter_context(nc.Block())

            @block.vector
            def _(v):
                link = lambda ins: dve_order.link(v, ins)
                for i in range(NG):
                    v.wait_ge(s_yt[i], 32)
                    for t in range(i * G, (i + 1) * G):
                        last = nc.vector.scalar_tensor_tensor(x_sb[:, t, :], yt[:, t, :], gate[:, 0, t:t + 1], x_sb[:, t, :],
                                                              ALU.mult, ALU.add)
                    link(last)
                    for t in range(i * G, (i + 1) * G):
                        last = nc.vector.bn_stats(stats6[:, t, :], x_sb[:, t, :])
                    link(last)
                    for t in range(i * G, (i + 1) * G):
                        last = nc.vector.bn_aggr(mv6[:, t, :], stats6[:, t, :])
                    link(last)
                link(nc.vector.tensor_scalar(sq6[:], mv6[:, :, 1], LN_EPS, None, ALU.add))
                inverse_root(v, inv_dev6[:], sq6[:], root_t[:])
                for i in range(NG):
                    for t in range(i * G, (i + 1) * G):
                        last = nc.vector.tensor_scalar(n_sb[:, t, :], x_sb[:, t, :], mv6[:, t, 0:1], inv_dev6[:, t:t + 1],
                                                       ALU.subtract, ALU.mult)
                    last.then_inc(s_n6, 1)
                v.wait_ge(s_n6, NG)

            @block.scalar
            def _(act):
                for i in range(NG):
                    act.wait_ge(s_n6, i + 1)
                    for t in range(i * G, (i + 1) * G):
                        last = nc.scalar.activation(yt[:, t, :], n_sb[:, t, :], ACT.Copy, scale=rsq_deg[:, t:t + 1])
                    last.then_inc(s_f6, 1)

            @block.sync
            def _(sp):
                for i in range(NG):
                    tiles = slice(i * G, (i + 1) * G)
                    for a, b in HALVES:
                        sp.dma_start(yt[a:b, tiles, :], rows_of_tiles(y0[1:1 + N_NODES])[a:b, tiles, :]).then_inc(s_yt[i], 16)
                with sp.Fori(0, NG) as i:
                    sp.wait_ge(s_f6, i + 1)
                    for a, b in HALVES:
                        sp.dma_start(rows_of_tiles(f_rows)[a:b, bass.ds(i * G, G), :], yt[a:b, bass.ds(i * G, G), :])\
                          .then_inc(s_f6st, 16)
                sp.wait_ge(s_f6st, 32 * NG)

        s_st7, s_free7, s_acc, s_accst, s_accfree = (sem(n) for n in (
            "indices7_staged", "rows7_free", "sums7_ready", "sums7_stored", "sums7_free"))
        s_got7 = [sem(f"rows7_{g}_gathered") for g in range(G)]
        acc_ctx = ExitStack()
        acc = sb(acc_ctx, "acc7", [P, G, G, D])
        with ExitStack() as st:
            src_s = sb(st, "src_s7", [P, G, G], I32)
            fr = sb(st, "fr", [P, G, G, D])
            block = st.enter_context(nc.Block())

            @block.scalar
            def _(act):
                with act.Fori(0, EITER) as i:
                    for g in range(G):
                        act.wait_ge(s_free7, i * G + g + 1)
                        act.sem_inc(carrier, 1)
                        nc.scalar.activation(src_s[:, g, :], src_i[:, bass.ds(i * G * G + g * G, G)], ACT.Copy).then_inc(s_st7, 1)

            @block.gpsimd
            def _(pool):
                with pool.Fori(0, EITER) as i:
                    for g in range(G):
                        pool.wait_ge(s_st7, i * G + g + 1)
                        pool.sem_inc(carrier, 1)
                        for u in range(G):
                            nc.gpsimd.indirect_dma_start(out=fr[:, g, u, :], out_offset=None, in_=f_rows,
                                                         in_offset=bass.IndirectOffsetOnAxis(ap=src_s[:, g, u:u + 1], axis=0))\
                              .then_inc(s_got7[g], 16)

            @block.vector
            def _(v):
                dve_order.link(v, nc.vector.memset(acc[:, G - 1, G - 1, :], 0.0))
                v.sem_inc(s_free7, G)
                v.sem_inc(s_acc, 1)
                with v.Fori(0, EITER) as i:
                    dve_order.turn(i, G * (G - 1))
                    for g in range(G):
                        v.wait_ge(s_got7[g], (i + 1) * G * 16)
                        v.wait_ge(s_accfree, i * G + g + 1)
                        if g:
                            v.wait_ge(s_acc, i * G + g)
                        else:
                            v.wait_ge(s_acc, i * G + 1)
                        for u in range(G):
                            n = g * G + u - 1
                            ins = nc.vector.scalar_tensor_tensor(acc[:, g, u, :], acc[:, n // G % G, n % G, :],
                                                                 same[:, bass.ds(i * G * G + g * G + u, 1)], fr[:, g, u, :],
                                                                 ALU.mult, ALU.add)
                            if u < G - 1:
                                dve_order.link(v, ins)
                        ins.then_inc(s_acc, 1)
                        v.wait_ge(s_acc, i * G + g + 2)
                        v.sem_inc(s_free7, 1)
                dve_order.leave(EITER)

            @block.sync
            def _(sp):
                sp.sem_inc(s_accfree, G)
                to = run_rows.rearrange("(p j) d -> p j d", p=P)
                with sp.Fori(0, EITER) as i:
                    for g in range(G):
                        sp.wait_ge(s_acc, i * G + g + 2)
                        for a, b in HALVES:
                            sp.dma_start(to[a:b, bass.ds(i * G * G + g * G, G), :], acc[a:b, g]).then_inc(s_accst, 16)
                        sp.wait_ge(s_accst, (i * G + g + 1) * 32)
                        sp.sem_inc(s_accfree, 1)

        s_w8, s_b8, s_bd, s_g8, s_tr8, s_t8, s_e8, s_ef, s_n8, s_tr8n, s_t8n, s_lg8, s_lg8e = (sem(n) for n in (
            "w8_loaded", "bias8_loaded", "joined8", "g8_ready", "sums8_turned", "sums8T_ready", "e8_done",
            "e8_fetched", "n8_ready", "n8_turned", "n8T_ready", "logits8_done", "logits8_kept"))
        s_br, s_own, s_inv = sem("router_bias_loaded"), sem("own_norm_done"), sem("own_deviations_ready")
        with ExitStack() as st:
            wg1 = sb(st, "wg1", [128, KD, D])
            wg2 = sb(st, "wg2", [128, KD, D])
            wr = sb(st, "wr", [128, KD, X])
            bn = sb(st, "bn", [P, D])
            gr = sb(st, "gr", [P, T, D])
            tile_s = sb(st, "tile_s", [P, G, D])
            tile_q = sb(st, "tile_q", [P, G, D])
            tN = sb(st, "tN8", [128, G * KD, P])
            stats8 = sb(st, "stats8", [P, T, 6])
            emb_mv = sb(st, "emb_mv", [P, T, 2])
            x_mv = sb(st, "x_mv", [P, T, 2])
            sq = sb(st, "sq", [P, T])
            inv_len = sb(st, "inv_len", [P, T])
            inv_dev = sb(st, "inv_dev", [P, T])
            inv_own = sb(st, "inv_own", [P, T])
            tS = sb(st, "tS8", [128, G * KD, P])
            tQ = sb(st, "tQ8", [128, G * KD, P])
            psT = ps(st, "psT8", [128, 3, 512])
            psO = ps(st, "psO8", [128, 3 * 512])
            psG = ps(st, "psG8", [128, 512])
            block = st.enter_context(nc.Block())

            @block.sync
            def _(sp):
                sp.dma_start(wg1[:], L1_gnn_W1.rearrange("(k p) d -> p k d", p=128)).then_inc(s_w8, 16)
                sp.dma_start(wg2[:], L1_gnn_W2.rearrange("(k p) d -> p k d", p=128)).then_inc(s_w8, 16)
                sp.dma_start(wr[:], L1_ffn_Wr.rearrange("(k p) d -> p k d", p=128)).then_inc(s_w8, 16)
                sp.dma_start(bn[:], L1_gnn_b.partition_broadcast(P)).then_inc(s_b8, 16)
                sp.dma_start(gate_b[:], L1_ffn_br.partition_broadcast(P)).then_inc(s_br, 16)
                sp.wait_ge(s_w8, 48)
                sp.wait_ge(s_b8, 16)
                sp.wait_ge(s_br, 16)
                for i in range(NG):
                    if i <= NG // 2:
                        sp.wait_ge(s_own, i + 1)
                    else:
                        sp.wait_ge(s_inv, i - NG // 2 + 1)
                    for a, b in HALVES:
                        sp.dma_start(rows_of_tiles(tok1)[a:b, i * G:(i + 1) * G, :], n_sb[a:b, i * G:(i + 1) * G, :])\
                          .then_inc(s_tok[1], 16)

            @block.gpsimd
            def _(pool):
                for t in range(T):
                    nc.gpsimd.indirect_dma_start(out=gr[:, t, :], out_offset=None, in_=run_rows,
                                                 in_offset=bass.IndirectOffsetOnAxis(ap=end_i[:, t:t + 1], axis=0))\
                      .then_inc(s_group[t // G], 16)

            @block.vector
            def _(v):
                link = lambda ins: dve_order.link(v, ins)

                def join(i):
                    tiles = slice(i * G, (i + 1) * G)
                    v.wait_ge(s_group[i], 3 * GATHER)
                    v.wait_ge(s_bd, i + 1)
                    for u in range(G):
                        t = i * G + u
                        last = nc.vector.scalar_tensor_tensor(gr[:, t, :], gr[:, t, :], has_in[:, t:t + 1],
                                                              psO[0:P, u * D:(u + 1) * D], ALU.mult, ALU.add)
                    link(last)
                    v.sem_inc(s_ef, 1)
                    link(nc.vector.tensor_tensor(gr[:, tiles, :], gr[:, tiles, :],
                                                 rsq_deg[:, tiles].unsqueeze(2).to_broadcast([P, G, D]), ALU.mult))

                def factors(i):
                    tiles = slice(i * G, (i + 1) * G)
                    v.wait_ge(s_tr8, i * 2 + 2)
                    nc.vector.tensor_tensor(tile_s[:], n_sb[:, tiles, :], gr[:, tiles, :], ALU.add)
                    nc.vector.tensor_tensor(tile_q[:], n_sb[:, tiles, :], gr[:, tiles, :], ALU.mult).then_inc(s_g8, 1)

                def moments(rows, of, i):
                    for t in range(i * G, (i + 1) * G):
                        last = nc.vector.bn_stats(stats8[:, t, :], rows[:, t, :])
                    link(last)
                    for t in range(i * G, (i + 1) * G):
                        last = nc.vector.bn_aggr(of[:, t, :], stats8[:, t, :])
                    link(last)

                def embedding(i):
                    tiles = slice(i * G, (i + 1) * G)
                    v.wait_ge(s_e8, i + 1)
                    for u in range(G):
                        last = nc.vector.scalar_tensor_tensor(gr[:, i * G + u, :], psO[0:P, u * D:(u + 1) * D],
                                                              has_in[:, i * G + u:i * G + u + 1], bn[:], ALU.mult, ALU.add)
                    link(last)
                    v.sem_inc(s_ef, 1)
                    link(nc.vector.scalar_tensor_tensor(gr[:, tiles], gr[:, tiles], 0.01, gr[:, tiles], ALU.mult, ALU.max))
                    moments(gr, emb_mv, i)

                def lengths(tiles):
                    mean, var = emb_mv[:, tiles, 0], emb_mv[:, tiles, 1]
                    link(nc.vector.tensor_tensor(sq[:, tiles], mean, mean, ALU.mult))
                    link(nc.vector.tensor_tensor(sq[:, tiles], sq[:, tiles], var, ALU.add))
                    link(nc.vector.tensor_scalar(sq[:, tiles], sq[:, tiles], float(D), 1e-24, ALU.mult, ALU.max))
                    inverse_root(v, inv_len[:, tiles], sq[:, tiles], root_t[:, tiles])

                def residual(i):
                    for t in range(i * G, (i + 1) * G):
                        last = nc.vector.scalar_tensor_tensor(x_sb[:, t, :], gr[:, t, :], inv_len[:, t:t + 1], x_sb[:, t, :],
                                                              ALU.mult, ALU.add)
                    link(last)
                    moments(x_sb, x_mv, i)

                def deviations(tiles):
                    link(nc.vector.tensor_scalar(sq[:, tiles], x_mv[:, tiles, 1], LN_EPS, None, ALU.add))
                    inverse_root(v, inv_dev[:, tiles], sq[:, tiles], root_t[:, tiles])

                def own_deviations(tiles):
                    link(nc.vector.tensor_tensor(sq[:, tiles], inv_dev[:, tiles], inv_dev[:, tiles], ALU.mult))
                    link(nc.vector.tensor_tensor(sq[:, tiles], sq[:, tiles], x_mv[:, tiles, 1], ALU.mult))
                    link(nc.vector.tensor_scalar(sq[:, tiles], sq[:, tiles], LN_EPS, None, ALU.add))
                    inverse_root(v, inv_own[:, tiles], sq[:, tiles], root_t[:, tiles])

                def router_rows(i):
                    for t in range(i * G, (i + 1) * G):
                        last = nc.vector.tensor_scalar(gr[:, t, :], x_sb[:, t, :], x_mv[:, t, 0:1], inv_dev[:, t:t + 1],
                                                       ALU.subtract, ALU.mult)
                    last.then_inc(s_n8, 1)

                v.sem_inc(s_ef, 1)
                for i in range(NG):
                    join(i)
                    if i == 0:
                        factors(0)
                v.wait_ge(s_b8, 16)
                factors(1)
                early = NG // 2 + 1
                for i in range(early):
                    embedding(i)
                    if i + 2 < NG:
                        factors(i + 2)
                part = slice(0, early * G)
                lengths(part)
                residual(0)
                embedding(early)
                for i in range(1, early):
                    residual(i)
                deviations(part)
                for i in range(early):
                    router_rows(i)
                own_deviations(part)
                v.sem_inc(s_inv, 1)
                for i in range(early + 1, NG):
                    embedding(i)
                part = slice(early * G, T)
                lengths(part)
                for i in range(early, NG):
                    residual(i)
                deviations(part)
                for i in range(early, NG):
                    router_rows(i)
                own_deviations(part)
                for i in range(early, NG):
                    for t in range(i * G, (i + 1) * G):
                        last = nc.vector.tensor_scalar(n_sb[:, t, :], gr[:, t, :], inv_own[:, t:t + 1], None, ALU.mult)
                    last.then_inc(s_inv, 1)

            @block.scalar
            def _(act):
                def fetch_factors(i):
                    for n, to in enumerate((tS, tQ)):
                        act.wait_ge(s_tr8, i * 2 + n + 3)
                        fetch_turned(to, psT).then_inc(s_t8, 1)

                def own_norm(i):
                    act.wait_ge(s_n8, i + 1)
                    act.wait_ge(s_inv, 1)
                    for t in range(i * G, (i + 1) * G):
                        last = nc.scalar.activation(n_sb[:, t, :], gr[:, t, :], ACT.Copy, scale=inv_own[:, t:t + 1])
                    last.then_inc(s_own, 1)

                def keep_logits(i):
                    act.wait_ge(s_tr8n, i + 1)
                    fetch_turned(tN, psT).then_inc(s_t8n, 1)
                    act.wait_ge(s_lg8, i + 1)
                    nc.scalar.activation(logits[:, i * G:(i + 1) * G, :].rearrange("p u e -> p (u e)"), psG[0:P, 0:G * X], ACT.Copy)\
                      .then_inc(s_lg8e, 1)

                with act.Fori(0, NG) as i:
                    fetch_factors(i)
                for i in range(NG):
                    keep_logits(i)
                    if i <= NG // 2:
                        own_norm(i)
                act.wait_ge(s_own, NG // 2 + 1)
                act.wait_ge(s_lg8e, NG)

            @block.tensor
            def _(pe):
                def turn_factors(i):
                    pe.wait_ge(s_g8, i + 1)
                    turn_tiles(pe, psT, tile_s).then_inc(s_tr8, 1)
                    pe.wait_ge(s_t8, i * 2 + 1)
                    turn_tiles(pe, psT, tile_q).then_inc(s_tr8, 1)
                    pe.wait_ge(s_t8, i * 2 + 2)

                def products(i):
                    pe.wait_ge(s_ef, NG + i + 1)
                    for u in range(G):
                        for n, (tt, w) in enumerate(((tS, wg1), (tQ, wg2))):
                            for k in range(KD):
                                last = nc.tensor.matmul(psO[0:P, u * D:(u + 1) * D], tt[:, u * KD + k, :], w[:, k, :],
                                                        start=(n == 0 and k == 0), stop=(n == 1 and k == KD - 1))
                    last.then_inc(s_e8, 1)

                def route_logits(i):
                    pe.wait_ge(s_n8, i + 1)
                    turn_tiles(pe, psT, gr[:, i * G:(i + 1) * G, :]).then_inc(s_tr8n, 1)
                    pe.wait_ge(s_t8n, i + 1)
                    for u in range(G):
                        for k in range(KD):
                            last = nc.tensor.matmul(psG[0:P, u * X:(u + 1) * X], tN[:, u * KD + k, :], wr[:, k, :],
                                                    start=(k == 0), stop=(k == KD - 1))
                    last.then_inc(s_lg8, 1)

                pe.sem_inc(s_tr8, 2)
                for i in range(NG):
                    pe.wait_ge(s_ef, i + 1)
                    for u in range(G):
                        last = nc.tensor.matmul(psO[0:P, u * D:(u + 1) * D],
                                                carry_on[:, i * G + u, :], acc[:, G - 1, G - 1, :], start=True, stop=True)
                    last.then_inc(s_bd, 1)
                pe.wait_ge(s_w8, 48)
                turn_factors(0)
                products(0)
                turn_factors(1)
                with pe.Fori(1, NG - 1) as i:
                    products(i)
                    turn_factors(i + 1)
                products(NG - 1)
                for i in range(NG):
                    route_logits(i)

        acc_ctx.close()
        route("r1", 2, NB1)
        experts("m1", NB1, tok1, s_tok[1], y1, L1_ffn_W1, L1_ffn_W2, L1_ffn_b2, True)

        s_o11, s_out = sem("o11_ready"), sem("out_stored")
        with ExitStack() as st:
            yt = sb(st, "yt11", [P, 2, T, D])
            block = st.enter_context(nc.Block())

            @block.vector
            def _(v):
                for i in range(NG):
                    v.wait_ge(s_yt[i], 32 + 64)
                    for k in range(2):
                        for t in range(i * G, (i + 1) * G):
                            last = nc.vector.scalar_tensor_tensor(x_sb[:, t, :], yt[:, k, t, :], gate[:, k, t:t + 1], x_sb[:, t, :],
                                                                  ALU.mult, ALU.add)
                        if k == 0:
                            dve_order.link(v, last)
                    last.then_inc(s_o11, 1)

            @block.sync
            def _(sp):
                for i in range(NG):
                    tiles = slice(i * G, (i + 1) * G)
                    for k in range(2):
                        for a, b in HALVES:
                            sp.dma_start(yt[a:b, k, tiles, :], rows_of_tiles(y1[1 + k * N_NODES:1 + (k + 1) * N_NODES])[a:b, tiles, :])\
                              .then_inc(s_yt[i], 16)
                with sp.Fori(0, NG) as i:
                    sp.wait_ge(s_o11, i + 1)
                    for a, b in HALVES:
                        sp.dma_start(rows_of_tiles(out)[a:b, bass.ds(i * G, G), :], x_sb[a:b, bass.ds(i * G, G), :]).then_inc(s_out, 16)
                sp.wait_ge(s_out, 32 * NG)


_INS = ['x', 'src', 'dst', 'edge_attr_64', 'L0_gnn_Wq', 'L0_gnn_Wk', 'L0_gnn_Wv', 'L0_gnn_We', 'L0_gnn_Wo', 'L0_gnn_bo',
        'L0_ffn_W1', 'L0_ffn_b1', 'L0_ffn_Wg', 'L0_ffn_bg', 'L0_ffn_Wd', 'L0_ffn_bd', 'L1_gnn_W1', 'L1_gnn_W2', 'L1_gnn_b',
        'L1_ffn_Wr', 'L1_ffn_br', 'L1_ffn_ln_g', 'L1_ffn_ln_b', 'L1_ffn_W1', 'L1_ffn_b1', 'L1_ffn_W2', 'L1_ffn_b2']


def kernel(**inputs):
    import numpy as _np
    import concourse.bacc as _bacc
    from concourse import mybir as _mybir
    from concourse.bass_utils import run_bass_kernel_spmd as _run

    nc = _bacc.Bacc("TRN2", target_bir_lowering=False, num_devices=1)
    arrays, args = {}, []
    for name in _INS:
        a = _np.ascontiguousarray(inputs[name])
        arrays[f"in_{name}_dram"] = a
        args.append(nc.dram_tensor(f"in_{name}_dram", a.shape, _mybir.dt.from_np(a.dtype), kind="ExternalInput").ap())
    args.append(nc.dram_tensor("out_0_dram", (N_NODES, D), F32, kind="ExternalOutput").ap())
    build(nc, *args)
    r = _run(nc, [arrays], core_ids=[0])
    return r.results[0]["out_0_dram"]
```
